# Optimizing a Trainium2 kernel written in Bass

```python
import numpy as np
import jax
import jax.numpy as jnp

def _softmax(x, axis=-1):
    return jax.nn.softmax(x, axis=axis)

def _gelu(x):
    return jax.nn.gelu(x, approximate=True)

def _silu(x):
    return jax.nn.silu(x)

def _sigmoid(x):
    return jax.nn.sigmoid(x)

def _layernorm(x, axis=-1, eps=1e-05):
    m = jnp.mean(x, axis=axis, keepdims=True)
    v = jnp.var(x, axis=axis, keepdims=True)
    return (x - m) / jnp.sqrt(v + eps)

def _scatter_add(tgt, idx, src, axis=0):
    return tgt.at[idx].add(src)

def _segment_sum(src, seg, n):
    return jax.ops.segment_sum(src, seg, n)
kernel_name = 'mk_lm_tower_d2_tok_ids256_r4_230e69'

def setup_inputs(seed: int=0):
    np.random.seed(seed)
    _w = jnp.asarray

    def _rec_inputs():
        import jax
        import jax.numpy as jnp
        _rk = jax.random.key(seed)
        x = jax.random.randint(jax.random.fold_in(_rk, 1), (2, 1024), 0, 50257, jnp.int32)
        return x
    x = _rec_inputs()

    def _L0_tok_setup():
        import jax, jax.numpy as jnp
        import numpy as np
        VOCAB = 50257
        DIM = 64

        def _positional_table(seq_len, dim, dtype=jnp.float32):
            pos = jnp.arange(seq_len, dtype=dtype)[:, None]
            d = jnp.arange(dim)
            exponent = (d - d % 2).astype(dtype) / dim
            inv_freq = jnp.power(jnp.asarray(10000.0, dtype), -exponent)
            angle = pos * inv_freq
            return jnp.where(d % 2 == 0, jnp.sin(angle), jnp.cos(angle))
        key = jax.random.key(seed)
        k1, k2 = jax.random.split(key)
        x = jax.random.randint(k1, (32, 1024), 0, VOCAB)
        W = jax.random.normal(k2, (VOCAB, DIM), dtype=jnp.float32)
        return {'x': x, 'W': W}
    _L0_tok_all = _L0_tok_setup()
    _L0_tok_in = {k: v for k, v in _L0_tok_all.items() if k in ('W',)}
    del _L0_tok_all

    def _L0_attn_setup():
        import jax, jax.numpy as jnp
        import numpy as np
        NUM_HEADS = 8
        key = jax.random.key(seed)
        ks = jax.random.split(key, 5)
        B, N, C = (8, 4096, 64)
        x = jax.random.normal(ks[0], (B, N, C), dtype=jnp.float32)
        Wq = jax.random.normal(ks[1], (C, C), dtype=jnp.float32) * 0.02
        Wkv = jax.random.normal(ks[2], (2 * C, C), dtype=jnp.float32) * 0.02
        Wproj = jax.random.normal(ks[3], (C, C), dtype=jnp.float32) * 0.02
        bproj = jnp.zeros((C,), dtype=jnp.float32)
        return {'x': x, 'Wq': Wq, 'Wkv': Wkv, 'Wproj': Wproj, 'bproj': bproj}
    _L0_attn_all = _L0_attn_setup()
    _L0_attn_in = {k: v for k, v in _L0_attn_all.items() if k in ('Wq', 'Wkv', 'Wproj', 'bproj')}
    del _L0_attn_all

    def _L0_ffn_setup():
        import jax, jax.numpy as jnp
        import numpy as np
        B, T, C = (64, 96, 64)
        NH, NKV = (4, 2)
        HD = C // NH
        NREP = NH // NKV
        NE, TOPK = (8, 2)
        HID = int(8 / 3 * C)
        EPS_RMS = 1e-06

        def _rope_tables(t_len):
            inv_freq = 1.0 / 10000.0 ** (np.arange(0, HD, 2, dtype=np.float32) / HD)
            t = np.arange(t_len, dtype=np.float32)
            freqs = np.outer(t, inv_freq)
            emb = np.concatenate([freqs, freqs], axis=-1)
            return (jnp.asarray(np.cos(emb)), jnp.asarray(np.sin(emb)))

        def _rotate_half(x):
            h = x.shape[-1] // 2
            return jnp.concatenate([-x[..., h:], x[..., :h]], axis=-1)

        def _rmsnorm(v, w):
            return v * jax.lax.rsqrt(jnp.mean(v * v, axis=-1, keepdims=True) + EPS_RMS) * w
        key = jax.random.key(seed)
        ks = jax.random.split(key, 10)
        s = lambda k, shape: jax.random.normal(k, shape, jnp.float32) * 0.02
        return {'x': jax.random.normal(ks[0], (B, T, C), jnp.float32), 'ln1_w': jnp.ones((C,), jnp.float32), 'ln2_w': jnp.ones((C,), jnp.float32), 'wq': s(ks[1], (NH * HD, C)), 'wk': s(ks[2], (NKV * HD, C)), 'wv': s(ks[3], (NKV * HD, C)), 'wo': s(ks[4], (C, C)), 'router_w': s(ks[5], (NE, C)), 'w1': s(ks[6], (NE, HID, C)), 'w2': s(ks[7], (NE, C, HID)), 'w3': s(ks[8], (NE, HID, C))}
    _L0_ffn_all = _L0_ffn_setup()
    _L0_ffn_in = {k: v for k, v in _L0_ffn_all.items() if k in ('ln1_w', 'ln2_w', 'wq', 'wk', 'wv', 'wo', 'router_w', 'w1', 'w2', 'w3')}
    del _L0_ffn_all

    def _L1_attn_setup():
        import jax, jax.numpy as jnp
        import numpy as np
        B, N, E, H = (4, 1024, 64, 8)
        EXP = 3
        D1 = EXP * E // H * H
        HD = D1 // H
        RPE = int(min(E / 8, 32))
        LAYERS = 3
        EPS = 1e-08

        def _srms(x, d):
            rms = jnp.linalg.norm(x, axis=-1, keepdims=True) * d ** (-0.5)
            return x / (rms + EPS)

        def _rpe(idx, pos_w, pos_b, rpe_lw, rpe_lb, out_w, out_b):
            h = idx @ pos_w.T + pos_b
            for i in range(LAYERS):
                h = jax.nn.relu(_srms(h, RPE)) @ rpe_lw[i].T + rpe_lb[i]
            return jax.nn.relu(_srms(h, RPE)) @ out_w.T + out_b
        key = jax.random.key(seed)
        ks = jax.random.split(key, 9)
        s = lambda k, shape, fan: jax.random.normal(k, shape, jnp.float32) * fan ** (-0.5)
        return {'x': jax.random.normal(ks[0], (B, N, E), jnp.float32), 'u_w': s(ks[1], (D1, E), E), 'u_b': jnp.zeros((D1,), jnp.float32), 'v_w': s(ks[2], (D1, E), E), 'v_b': jnp.zeros((D1,), jnp.float32), 'o_w': s(ks[3], (E, D1), D1), 'o_b': jnp.zeros((E,), jnp.float32), 't_w': s(ks[4], (E, E), E), 't_b': jnp.zeros((E,), jnp.float32), 'pos_w': s(ks[5], (RPE, 1), 1), 'pos_b': jnp.zeros((RPE,), jnp.float32), 'rpe_lw': s(ks[6], (LAYERS, RPE, RPE), RPE), 'rpe_lb': jnp.zeros((LAYERS, RPE), jnp.float32), 'out_w': s(ks[7], (H * HD, RPE), RPE), 'out_b': jnp.zeros((H * HD,), jnp.float32)}
    _L1_attn_all = _L1_attn_setup()
    _L1_attn_in = {k: v for k, v in _L1_attn_all.items() if k in ('u_w', 'u_b', 'v_w', 'v_b', 'o_w', 'o_b', 't_w', 't_b', 'pos_w', 'pos_b', 'rpe_lw', 'rpe_lb', 'out_w', 'out_b')}
    del _L1_attn_all

    def _L1_ffn_setup():
        import jax, jax.numpy as jnp
        import numpy as np
        IN_CH = 64
        OUT_CH = 64
        key = jax.random.key(seed)
        kx, kw, kb = jax.random.split(key, 3)
        x = jax.random.normal(kx, (8, 1024, IN_CH), dtype=jnp.float32)
        bound = 1.0 / np.sqrt(IN_CH)
        weight = jax.random.uniform(kw, (OUT_CH, IN_CH), dtype=jnp.float32, minval=-bound, maxval=bound)
        bias = jax.random.uniform(kb, (OUT_CH,), dtype=jnp.float32, minval=-bound, maxval=bound)
        return {'x': x, 'weight': weight, 'bias': bias}
    _L1_ffn_all = _L1_ffn_setup()
    _L1_ffn_in = {k: v for k, v in _L1_ffn_all.items() if k in ('weight', 'bias')}
    del _L1_ffn_all
    return {'x': x, 'L0_tok_W': _L0_tok_in['W'], 'L0_attn_Wq': _L0_attn_in['Wq'], 'L0_attn_Wkv': _L0_attn_in['Wkv'], 'L0_attn_Wproj': _L0_attn_in['Wproj'], 'L0_attn_bproj': _L0_attn_in['bproj'], 'L0_ffn_ln1_w': _L0_ffn_in['ln1_w'], 'L0_ffn_ln2_w': _L0_ffn_in['ln2_w'], 'L0_ffn_wq': _L0_ffn_in['wq'], 'L0_ffn_wk': _L0_ffn_in['wk'], 'L0_ffn_wv': _L0_ffn_in['wv'], 'L0_ffn_wo': _L0_ffn_in['wo'], 'L0_ffn_router_w': _L0_ffn_in['router_w'], 'L0_ffn_w1': _L0_ffn_in['w1'], 'L0_ffn_w2': _L0_ffn_in['w2'], 'L0_ffn_w3': _L0_ffn_in['w3'], 'L1_attn_u_w': _L1_attn_in['u_w'], 'L1_attn_u_b': _L1_attn_in['u_b'], 'L1_attn_v_w': _L1_attn_in['v_w'], 'L1_attn_v_b': _L1_attn_in['v_b'], 'L1_attn_o_w': _L1_attn_in['o_w'], 'L1_attn_o_b': _L1_attn_in['o_b'], 'L1_attn_t_w': _L1_attn_in['t_w'], 'L1_attn_t_b': _L1_attn_in['t_b'], 'L1_attn_pos_w': _L1_attn_in['pos_w'], 'L1_attn_pos_b': _L1_attn_in['pos_b'], 'L1_attn_rpe_lw': _L1_attn_in['rpe_lw'], 'L1_attn_rpe_lb': _L1_attn_in['rpe_lb'], 'L1_attn_out_w': _L1_attn_in['out_w'], 'L1_attn_out_b': _L1_attn_in['out_b'], 'L1_ffn_weight': _L1_ffn_in['weight'], 'L1_ffn_bias': _L1_ffn_in['bias']}

def reference(x, L0_tok_W, L0_attn_Wq, L0_attn_Wkv, L0_attn_Wproj, L0_attn_bproj, L0_ffn_ln1_w, L0_ffn_ln2_w, L0_ffn_wq, L0_ffn_wk, L0_ffn_wv, L0_ffn_wo, L0_ffn_router_w, L0_ffn_w1, L0_ffn_w2, L0_ffn_w3, L1_attn_u_w, L1_attn_u_b, L1_attn_v_w, L1_attn_v_b, L1_attn_o_w, L1_attn_o_b, L1_attn_t_w, L1_attn_t_b, L1_attn_pos_w, L1_attn_pos_b, L1_attn_rpe_lw, L1_attn_rpe_lb, L1_attn_out_w, L1_attn_out_b, L1_ffn_weight, L1_ffn_bias):
    import jax
    import jax.numpy as jnp

    def _L0_tok_ref(x, W):
        import jax, jax.numpy as jnp
        import numpy as np
        VOCAB = 50257
        DIM = 64

        def _positional_table(seq_len, dim, dtype=jnp.float32):
            pos = jnp.arange(seq_len, dtype=dtype)[:, None]
            d = jnp.arange(dim)
            exponent = (d - d % 2).astype(dtype) / dim
            inv_freq = jnp.power(jnp.asarray(10000.0, dtype), -exponent)
            angle = pos * inv_freq
            return jnp.where(d % 2 == 0, jnp.sin(angle), jnp.cos(angle))
        seq_len = x.shape[1]
        pe = _positional_table(seq_len, W.shape[1], W.dtype)
        return W[x] + pe[None, :, :]

    def _L0_attn_ref(x, Wq, Wkv, Wproj, bproj):
        import jax, jax.numpy as jnp
        import numpy as np
        NUM_HEADS = 8
        B, N, C = x.shape
        h = NUM_HEADS
        d = C // h
        q = jnp.einsum('bnc,oc->bno', x, Wq).reshape(B, N, h, d).transpose(0, 2, 1, 3)
        kv = jnp.einsum('bnc,oc->bno', x, Wkv).reshape(B, N, 2, h, d)
        k = kv[:, :, 0].transpose(0, 2, 1, 3)
        v = kv[:, :, 1].transpose(0, 2, 1, 3)
        q = jax.nn.elu(q) + 1.0
        k = jax.nn.elu(k) + 1.0
        k_sum = k.sum(axis=2)
        D_inv = 1.0 / jnp.maximum(jnp.einsum('bhnd,bhd->bhn', q, k_sum), 1e-06)
        context = jnp.einsum('bhnd,bhne->bhde', k, v)
        attn = jnp.einsum('bhnd,bhde->bhne', q, context) * D_inv[..., None]
        out = attn.transpose(0, 2, 1, 3).reshape(B, N, C)
        out = jnp.einsum('bnc,oc->bno', out, Wproj) + bproj
        return out

    def _L0_ffn_ref(x, ln1_w, ln2_w, wq, wk, wv, wo, router_w, w1, w2, w3):
        import jax, jax.numpy as jnp
        import numpy as np
        B, T, C = (64, 96, 64)
        NH, NKV = (4, 2)
        HD = C // NH
        NREP = NH // NKV
        NE, TOPK = (8, 2)
        HID = int(8 / 3 * C)
        EPS_RMS = 1e-06

        def _rope_tables(t_len):
            inv_freq = 1.0 / 10000.0 ** (np.arange(0, HD, 2, dtype=np.float32) / HD)
            t = np.arange(t_len, dtype=np.float32)
            freqs = np.outer(t, inv_freq)
            emb = np.concatenate([freqs, freqs], axis=-1)
            return (jnp.asarray(np.cos(emb)), jnp.asarray(np.sin(emb)))

        def _rotate_half(x):
            h = x.shape[-1] // 2
            return jnp.concatenate([-x[..., h:], x[..., :h]], axis=-1)

        def _rmsnorm(v, w):
            return v * jax.lax.rsqrt(jnp.mean(v * v, axis=-1, keepdims=True) + EPS_RMS) * w
        Bx, Tx, Cx = x.shape
        h = _rmsnorm(x, ln1_w)
        q = (h @ wq.T).reshape(Bx, Tx, NH, HD).transpose(0, 2, 1, 3)
        k = (h @ wk.T).reshape(Bx, Tx, NKV, HD).transpose(0, 2, 1, 3)
        v = (h @ wv.T).reshape(Bx, Tx, NKV, HD).transpose(0, 2, 1, 3)
        cos, sin = _rope_tables(Tx)
        cos, sin = (cos[None, None], sin[None, None])
        q = q * cos + _rotate_half(q) * sin
        k = k * cos + _rotate_half(k) * sin
        k = jnp.repeat(k, NREP, axis=1)
        v = jnp.repeat(v, NREP, axis=1)
        scores = jnp.einsum('bhtd,bhsd->bhts', q, k) / jnp.sqrt(jnp.float32(HD))
        causal = jnp.tril(jnp.ones((Tx, Tx), dtype=bool))
        scores = jnp.where(causal[None, None], scores, jnp.float32(-1e+30))
        att = jax.nn.softmax(scores, axis=-1)
        y = jnp.einsum('bhts,bhsd->bhtd', att, v).transpose(0, 2, 1, 3).reshape(Bx, Tx, Cx)
        x = x + y @ wo.T
        flat = _rmsnorm(x, ln2_w).reshape(-1, Cx)
        probs = jax.nn.softmax(flat @ router_w.T, axis=-1)
        tp, ti = jax.lax.top_k(probs, TOPK)
        tp = tp / (jnp.sum(tp, axis=-1, keepdims=True) + 1e-09)
        weights = jnp.sum(tp[..., None] * jax.nn.one_hot(ti, NE, dtype=flat.dtype), axis=1)
        out = jnp.zeros_like(flat)
        for e in range(NE):
            hh = jax.nn.silu(flat @ w1[e].T) * (flat @ w3[e].T)
            out = out + weights[:, e:e + 1] * (hh @ w2[e].T)
        return x + out.reshape(Bx, Tx, Cx)

    def _L1_attn_ref(x, u_w, u_b, v_w, v_b, o_w, o_b, t_w, t_b, pos_w, pos_b, rpe_lw, rpe_lb, out_w, out_b):
        import jax, jax.numpy as jnp
        import numpy as np
        B, N, E, H = (4, 1024, 64, 8)
        EXP = 3
        D1 = EXP * E // H * H
        HD = D1 // H
        RPE = int(min(E / 8, 32))
        LAYERS = 3
        EPS = 1e-08

        def _srms(x, d):
            rms = jnp.linalg.norm(x, axis=-1, keepdims=True) * d ** (-0.5)
            return x / (rms + EPS)

        def _rpe(idx, pos_w, pos_b, rpe_lw, rpe_lb, out_w, out_b):
            h = idx @ pos_w.T + pos_b
            for i in range(LAYERS):
                h = jax.nn.relu(_srms(h, RPE)) @ rpe_lw[i].T + rpe_lb[i]
            return jax.nn.relu(_srms(h, RPE)) @ out_w.T + out_b
        b, n, _ = x.shape
        u = jax.nn.silu(x @ u_w.T + u_b)
        v = jax.nn.silu(x @ v_w.T + v_b)
        v = v.reshape(b, n, H, HD).transpose(0, 2, 1, 3)
        pos_idx = jnp.arange(1, n, dtype=jnp.float32)
        idx = jnp.concatenate([jnp.zeros((1,), jnp.float32), pos_idx, jnp.zeros((1,), jnp.float32), -pos_idx[::-1]])[:, None]
        a = _rpe(idx, pos_w, pos_b, rpe_lw, rpe_lb, out_w, out_b)
        a = a.reshape(2 * n, H, HD).transpose(1, 0, 2)
        yf = jnp.fft.rfft(v, 2 * n, axis=-2)
        af = jnp.fft.rfft(a, 2 * n, axis=-2)[None]
        out = jnp.fft.irfft(af * yf, 2 * n, axis=-2)[:, :, :n, :]
        out = out.transpose(0, 2, 1, 3).reshape(b, n, D1)
        out = u * out @ o_w.T + o_b
        x_r = jax.nn.silu(_srms((x - out) @ t_w.T + t_b, D1))
        return x + x_r

    def _L1_ffn_ref(x, weight, bias):
        import jax, jax.numpy as jnp
        import numpy as np
        IN_CH = 64
        OUT_CH = 64
        return jnp.einsum('bsi,oi->bso', x, weight) + bias
    h = _L0_tok_ref(x, L0_tok_W)
    h = h + _L0_attn_ref(_layernorm(h, axis=-1), L0_attn_Wq, L0_attn_Wkv, L0_attn_Wproj, L0_attn_bproj)
    h = h + _L0_ffn_ref(_layernorm(h, axis=-1), L0_ffn_ln1_w, L0_ffn_ln2_w, L0_ffn_wq, L0_ffn_wk, L0_ffn_wv, L0_ffn_wo, L0_ffn_router_w, L0_ffn_w1, L0_ffn_w2, L0_ffn_w3)
    h = h + _L1_attn_ref(_layernorm(h, axis=-1), L1_attn_u_w, L1_attn_u_b, L1_attn_v_w, L1_attn_v_b, L1_attn_o_w, L1_attn_o_b, L1_attn_t_w, L1_attn_t_b, L1_attn_pos_w, L1_attn_pos_b, L1_attn_rpe_lw, L1_attn_rpe_lb, L1_attn_out_w, L1_attn_out_b)
    h = h + _L1_ffn_ref(_layernorm(h, axis=-1), L1_ffn_weight, L1_ffn_bias)
    return h

_drawn_inputs = setup_inputs


def setup_inputs(seed=0):
    import zlib

    import numpy as np

    out = dict(_drawn_inputs(seed))
    spreads = {'L0_attn_bproj': (0.0, 0.1),
     'L0_ffn_ln1_w': (1.0, 0.6),
     'L0_ffn_ln2_w': (1.0, 0.6),
     'L1_attn_u_b': (0.0, 0.376),
     'L1_attn_v_b': (0.0, 0.1),
     'L1_attn_o_b': (0.0, 2.0),
     'L1_attn_t_b': (0.0, 2.0),
     'L1_attn_pos_b': (0.0, 2.0),
     'L1_attn_rpe_lb': (0.0, 0.589),
     'L1_attn_out_b': (0.0, 0.441)}
    factors = {'L0_attn_Wq': 8.0,
     'L0_attn_Wkv': 8.0,
     'L0_attn_Wproj': 7.379,
     'L0_ffn_wq': 8.0,
     'L0_ffn_wk': 8.0,
     'L0_ffn_wv': 8.0,
     'L0_ffn_wo': 8.0,
     'L0_ffn_router_w': 8.0,
     'L0_ffn_w1': 8.0,
     'L0_ffn_w2': 8.0,
     'L0_ffn_w3': 8.0,
     'L1_ffn_bias': 4.926}
    for name, (base, spread) in spreads.items():
        noise = np.random.default_rng([zlib.crc32(name.encode()), seed]).standard_normal(out[name].shape)
        drawn = base * np.exp(spread * noise) if base else spread * noise
        out[name] = jnp.asarray(drawn.astype(out[name].dtype))
    for name, factor in factors.items():
        out[name] = (out[name] * factor).astype(out[name].dtype)
    return out
```

```python
from contextlib import ExitStack

import numpy as np
import concourse.bass as bass
from concourse import mybir

F32 = mybir.dt.float32
F32R = mybir.dt.float32r
BF16 = mybir.dt.bfloat16
I32 = mybir.dt.int32
ALU = mybir.AluOpType
ACT = mybir.ActivationFunctionType
AXX = mybir.AxisListType.X

P = 128
B, N, C = 2, 1024, 64
NT = N // P
H1 = 8
NH, NKV, HD = 4, 2, 16
NE, HID = 8, 170
NPAIR = NE // 2
REM = HID - P
D1 = 192
R = 8
LAYERS = 3
NU = N // 2 // P
NK = N // P
NEG = -1.0e30
TERMS_Q = [0, 0, 0, 1, 1, 2]
TERMS_K = [0, 1, 2, 0, 1, 0]
MROW = 16 * len(TERMS_Q)
KROWS = MROW + 3
TOPK_OFF = float(NE)
ROW_CHUNKS = [(hh, i, c) for hh in range(NH) for i in range(NT) for c in range(i // 4 + 1)]
EARLY = 12
WIDE = len(ROW_CHUNKS) + EARLY


def row_bank(n):
    return n % 6 if n < WIDE else n % 2


def row_free(n):
    return n - 5 if n < WIDE + 2 else n - 1


def col_heads(j):
    return [(hh,) for hh in range(NH)] if j < 4 else [(0, 1), (2, 3)]


COL_STEPS = [(j, heads) for j in range(NT) for heads in col_heads(j)]


def col_steps(b, j):
    return b * len(COL_STEPS) + sum(len(col_heads(i)) for i in range(j + 1))

WCOLS = {}
_at = 0
for _n, _w in (("q1", P), ("kv1", 2 * P), ("proj1", P), ("q2", P), ("q2r", P), ("k2", 64), ("k2r", 64), ("v2", 64),
               ("wo2", P), ("v3", 2 * D1), ("u3", 2 * D1), ("o3", 3 * P), ("t3", P), ("w4", P),
               ("bproj", P), ("ub", 2 * D1), ("vb", 2 * D1), ("ob", P), ("tb", P), ("b4", P), ("ln2", P),
               ("ln1", 1), ("mask_c", P), ("mask_k", 16), ("eidx", P)):
    WCOLS[_n] = (_at, _at + _w)
    _at += _w
WTOT = _at
RCOLS = {}
_at = 0
for _n, _w in (("lag", P), ("ones", P), ("l0", P), ("l1", P), ("l2", P), ("pw", 1), ("pb", 1), ("b0", 1), ("b1", 1),
               ("b2", 1), ("outw", D1), ("alt", NT * 2)):
    RCOLS[_n] = (_at, _at + _w)
    _at += _w
RTOT = _at
ECOLS = {}
_at = 0
for _n, _w in (("w1", 12 * P), ("w3", 12 * P), ("rt", 8), ("w2m", NE * 64), ("w2r", NPAIR * P), ("ii", 64)):
    ECOLS[_n] = (_at, _at + _w)
    _at += _w
ETOT = _at
REUSE = 8192
NSPLIT = ECOLS["rt"][1]


def spread(v, dim, n):
    v = v.unsqueeze(dim)
    shape = list(v.shape)
    shape[dim] = n
    return v.broadcast_to(shape)


def build(nc, idx, emb, pe, wpack, rpack, epack, ident, bfc, rope, tm, tu, tk, scr_q, scr_k, out):
    with ExitStack() as ctx:
        def sb(name, shape, dt=F32):
            return ctx.enter_context(nc.sbuf_tensor(name, shape, dt))

        def sem(name):
            return ctx.enter_context(nc.semaphore(name))

        ps = ctx.enter_context(nc.psum_tensor("ps", [P, 8, 512], F32))

        idx_s = sb("idx_s", [P, NT * B], I32)
        w = sb("w", [P, WTOT])
        rp = sb("rp", [P, RTOT])
        ew = sb("ew", [P, ETOT - NSPLIT])
        reuse = sb("reuse", [P, REUSE])
        idt = sb("idt", [P, P])
        bfc_s = sb("bfc_s", [P, 3 * P + B * NPAIR * P], BF16)
        arena = sb("arena", [P, 2 * NT * N])
        h = sb("h", [P, NT, B, C])
        xc = sb("xc", [P, NT, B, C])
        sq = sb("sq", [P, NT, B, C])
        x1 = sb("x1", [P, NT, B, C])
        xT = sb("xT", [P, N])
        st = sb("st", [P, 12, NT * B])
        rw = sb("rw", [P, 8, NT * B * NE])

        def W(name, lo=0, hi=None):
            a, b = WCOLS[name]
            return w[:, a + lo:(b if hi is None else a + hi)]

        def RP(name):
            a, b = RCOLS[name]
            return rp[:, a:b]

        def E(name, lo=0, hi=None):
            a, b = ECOLS[name]
            return ew[:, a - NSPLIT + lo:(b if hi is None else a + hi) - NSPLIT]

        def EP(piece, name, lo, hi):
            a = ECOLS[name][0]
            return piece[:, a + lo:a + hi]

        mask_ts, mask_st, ident_b = bfc_s[:, 0:P], bfc_s[:, P:2 * P], bfc_s[:, 2 * P:3 * P]

        def selw(b, pr):
            a = 3 * P + (b * NPAIR + pr) * P
            return bfc_s[:, a:a + P]

        tm_s = arena[:, :].rearrange("p (s m k) -> p s m k", s=2, m=NT)

        def plan(region, *parts):
            at, views = 0, []
            for shape, dt in parts:
                cols = int(np.prod(shape)) // (2 if dt == BF16 else 1)
                v = region[:, at:at + cols]
                at += cols
                v = v if dt == F32 else v.bitcast(dt)
                names = ["a", "b", "c", "d"][:len(shape)]
                if len(shape) > 1:
                    v = v.rearrange("p (%s) -> p %s" % (" ".join(names), " ".join(names)),
                                    **dict(zip(names[1:], shape[1:])))
                views.append(v)
            assert at <= region.shape[1], (at, region.shape)
            return views

        qst, kst, yT, pt = plan(arena, ([B * NH, N], BF16), ([B * NKV, N], BF16), ([B, N], F32), ([2, NH, N], F32))
        _, _, _, pieces_q, pieces_k, e_raw = plan(arena, ([B * NH, N], BF16), ([B * NKV, N], BF16), ([B, N], F32),
                                                  ([3, N], BF16), ([3, N], BF16), ([NSPLIT], F32))
        tk_s, tu_s = plan(arena, ([2, NK, 512], F32), ([2, NU, N], F32))
        gt, rope_s, rh, geo = plan(reuse, ([2, N], F32), ([2, N], F32), ([4, P], F32), ([2, NT, 32], F32))
        fhl, sil, gh, wb, zp_ = plan(reuse, ([NT, B, P], F32), ([2, 512], F32), ([2, 3, 512], F32),
                                     ([2, 512], F32), ([2, 512], F32))
        fhl = fhl.rearrange("p j b (q c) -> p j b q c", q=2)
        zacc = (xc[:].rearrange("p j b c -> p (j b c)"), sq[:].rearrange("p j b c -> p (j b c)"))
        us, oss = plan(reuse, ([NT, 384], F32), ([NK, 384], F32))

        gt2 = sb("gt2", [P, P])
        af = sb("af", [P, 2, NK, D1])
        afn = sb("afn", [P, D1])
        cbd = sb("cbd", [P, 144])
        tmp = sb("tmp", [P, N])
        va2 = sb("va2", [P, NT, B, NKV, 32])
        mrow = sb("mrow", [32, 3, P], BF16)
        mtmp = sb("mtmp", [32, P])
        wst = sb("wst", [P, N], BF16)
        with ExitStack() as experts:
            e_hi, e_lo, xs = (experts.enter_context(nc.sbuf_tensor(n, sh, F32R)) for n, sh in (
                ("e_hi", [P, NSPLIT]), ("e_lo", [P, NSPLIT]), ("xs", [P, B, N])))
        share = sb("share", [P, 2 * NSPLIT + B * N])
        pe_s, va1, kf1, qf1, qr, kr_ = plan(share, ([NT, C], F32), ([NT, 132], F32), ([NT, B, C], F32), ([N], F32),
                                            ([N], F32), ([N], F32))
        kr = kr_[0:64]
        vs, veo, y3 = plan(share, ([NT, 384], F32), ([2, NU, 384], F32), ([2, 384], F32))
        orr, yT3 = plan(share, ([NK, 384], F32), ([NT, 3, P], F32))
        ld_idx, ld_pe, ld_rp, ld_id, ld_w, ld_bf, ld_rope, ld_m, ld_e, ld_u, ld_k = (
            sem(n) for n in ("ld_idx", "ld_pe", "ld_rp", "ld_id", "ld_w", "ld_bf", "ld_rope", "ld_m", "ld_e", "ld_u", "ld_k"))
        gathered = sem("gathered")
        dve_chain, act_chain, pool_chain = sem("dve_chain"), sem("act_chain"), sem("pool_chain")

        names = {}

        def S(name):
            if name not in names:
                names[name] = sem(name)
            return names[name]

        def mm(o, l, r, start=True, stop=True, **kw):
            return nc.tensor.matmul(o, l, r, start=start, stop=stop, **kw)

        block = ctx.enter_context(nc.Block())

        @block.sync
        def _(sp):
            sp.dma_start(idx_s[:], idx).then_inc(ld_idx, 16)
            sp.dma_start(rp[:], rpack).then_inc(ld_rp, 16)
            sp.dma_start(idt[:], ident).then_inc(ld_id, 16)
            sp.dma_start(pe_s[:], pe).then_inc(ld_pe, 16)
            sp.dma_start(w[:], wpack).then_inc(ld_w, 16)
            sp.dma_start(rope_s[:], rope).then_inc(ld_rope, 16)
            sp.dma_start(bfc_s[:], bfc).then_inc(ld_bf, 16)
            sp.wait_ge(gathered, 16 * NT * B)
            for s in range(2):
                sp.dma_start(tm_s[:, s], tm[s]).then_inc(ld_m, 16)
            sp.dma_start(ew[:], epack[:, NSPLIT:ETOT]).then_inc(ld_e, 16)
            sp.wait_ge(S("gt_done"), 3)
            sp.dma_start(e_raw, epack[:, 0:NSPLIT]).then_inc(ld_e, 16)
            sp.wait_ge(S("k_pieces"), 2)
            sp.dma_start(scr_q.rearrange("s p t -> p s t"), pieces_q).then_inc(S("scr_written"), 16)
            sp.dma_start(scr_k.rearrange("s p t -> p s t"), pieces_k[0:64]).then_inc(S("scr_written"), 16)
            sp.wait_ge(S("scr_written"), 32)
            for n, pc in enumerate(TERMS_Q):
                sp.dma_start(qst[16 * n:16 * n + 16], scr_q[pc].rearrange("(g d) t -> d g t", d=HD)).then_inc(S("stacks"), 16)
            for n, pc in enumerate(TERMS_K):
                sp.dma_start(kst[16 * n:16 * n + 16], scr_k[pc].rearrange("(g d) t -> d g t", d=HD)).then_inc(S("stacks"), 16)
            for b in range(B):
                sp.wait_ge(S("max_pieces"), b + 1)
                for pc in range(3):
                    sp.dma_start(qst[MROW + pc:MROW + pc + 1, b * NH:(b + 1) * NH, :],
                                 mrow[:, pc, :]).then_inc(S("max_rows"), 16)
            sp.wait_ge(S("yTT"), B)
            for s in range(2):
                sp.dma_start(tu_s[:, s], tu[s]).then_inc(ld_u, 16)
            for s in range(2):
                sp.dma_start(tk_s[:, s].rearrange("p k u -> p (k u)"), tk[s]).then_inc(ld_k, 16)
            sp.wait_ge(S("final"), 1)
            sp.dma_start(out, sq[:].rearrange("p j b c -> p (j b c)")).then_inc(S("stored"), 16)
            sp.wait_ge(S("stored"), 16)

        @block.gpsimd
        def _(pool):
            def step(ins):
                chain[0] += 1
                ins.then_inc(pool_chain, 1)
                pool.wait_ge(pool_chain, chain[0])

            chain = [0]
            pool.wait_ge(ld_idx, 16)
            for j in range(NT):
                for b in range(B):
                    n = j * B + b
                    nc.gpsimd.indirect_dma_start(
                        xc[:, j, b, :], None, emb,
                        bass.IndirectOffsetOnAxis(ap=idx_s[:, n:n + 1], axis=0)).then_inc(gathered, 16)
            nc.gpsimd.memset(geo[:], 0.0).then_inc(S("geo_zero"), 1)
            pool.wait_ge(S("geo_zero"), 1)
            nc.gpsimd.memset(geo[:, 0, :, R:R + 1], 2.0).then_inc(S("geo_ones"), 1)
            nc.gpsimd.memset(va1[:, :, P:P + 1], 1.0).then_inc(S("va1_ones"), 1)
            nc.gpsimd.memset(va2[:], 0.0).then_inc(S("va2_zero"), 1)
            pool.wait_ge(S("va2_zero"), 1)
            nc.gpsimd.memset(va2[:, :, :, :, HD:HD + 1], 1.0).then_inc(S("va2_ones"), 1)
            nc.gpsimd.memset(wst[:], 0.0).then_inc(S("wst_zero"), 1)
            pool.wait_ge(S("wst_zero"), 1)
            pool.wait_ge(S("gt_done"), 3)
            nc.gpsimd.memset(kst[MROW:KROWS], 1.0).then_inc(S("k_ones"), 1)
            for t in range(4):
                b, hf = t // 2, t % 2
                for pr in range(NPAIR):
                    n = t * NPAIR + pr
                    pool.wait_ge(S("zpair"), n + 1)
                    z = zacc[b][:, hf * 512:(hf + 1) * 512]
                    if pr == 0:
                        nc.gpsimd.tensor_copy(z, zp_[:, n % 2, :]).then_inc(S("zsum"), 1)
                    else:
                        pool.wait_ge(S("zsum"), n)
                        nc.gpsimd.tensor_tensor(z, z, zp_[:, n % 2, :], ALU.add).then_inc(S("zsum"), 1)

        @block.tensor
        def _(pe):
            def transposes(src, banks, ready, value, done):
                pe.wait_ge(ready, value)
                for j in range(NT):
                    ins = nc.tensor.transpose(ps[:, banks + j // 4, (j % 4) * P:(j % 4 + 1) * P],
                                              src[:, j].rearrange("p b c -> p (b c)"), idt[:])
                    if j % 4 == 3:
                        ins.then_inc(done, 1)

            pe.wait_ge(ld_rp, 16)
            pe.wait_ge(ld_id, 16)
            for i in range(LAYERS + 1):
                pe.wait_ge(S("r_sq"), i + 1)
                mm(ps[:, 0, 0:P], RP("ones"), rh[:, 1]).then_inc(S("r_ss"), 1)
                pe.wait_ge(S("r_act"), i + 1)
                if i < LAYERS:
                    mm(ps[:, 1, 0:P], RP("l%d" % i), rh[:, 3]).then_inc(S("r_lin"), 1)
            nc.tensor.transpose(ps[:, 1, 0:P], rh[:, 3], idt[:]).then_inc(S("r_T"), 1)
            transposes(sq, 2, S("n1"), 1, S("T1"))
            pe.wait_ge(ld_w, 16)
            pe.wait_ge(S("xT1"), 2)
            for c in range(2):
                mm(ps[:, 4 + c], W("q1"), xT[:, c * 512:(c + 1) * 512]).then_inc(S("q1"), 1)
            pe.wait_ge(S("geo_done"), 1)
            KVB = (0, 1, 2, 3)
            for j in range(NT):
                mm(ps[:, KVB[j // 2], (j % 2) * 256:(j % 2 + 1) * 256], xT[:, j * P:(j + 1) * P], W("kv1")).then_inc(S("kv1"), 1)
            pe.wait_ge(S("kf1"), 1)
            pe.wait_ge(S("va1"), 1)
            pe.wait_ge(S("va1_ones"), 1)
            for j in range(NT):
                ins = mm(ps[:, 6, 0:P + 1], kf1[:, j].rearrange("p b c -> p (b c)"), va1[:, j, 0:P + 1],
                         start=(j == 0), stop=(j == NT - 1))
            ins.then_inc(S("ctx1"), 1)
            pe.wait_ge(S("cbd"), 2)
            pe.wait_ge(S("qf1"), 1)
            for j in range(NT):
                ins = mm(ps[:, j // 2, (j % 2) * 256:(j % 2) * 256 + 144], qf1[:, j * P:(j + 1) * P], cbd[:])
            ins.then_inc(S("nd1"), 1)
            transposes(sq, 4, S("attn1"), 1, S("T1b"))
            pe.wait_ge(S("xT1b"), 2)
            for j in range(NT):
                ins = mm(ps[:, j // 4, (j % 4) * P:(j % 4 + 1) * P], xT[:, j * P:(j + 1) * P], W("proj1"))
            ins.then_inc(S("o1"), 1)
            pe.wait_ge(ld_m, 32)
            pe.wait_ge(S("geo_done"), 1)
            pe.wait_ge(S("xT1b"), 2)
            for s in range(2):
                for c in range(2):
                    for half in range(2):
                        for q in range(4):
                            m = half * 4 + q
                            ins = mm(ps[32 * q:32 * q + 32, 4 + 2 * s + c], geo[:, s, m, :], tm_s[:, s, m, c * 512:(c + 1) * 512],
                                     start=(half == 0), stop=(half == 1), tile_position=(0, 32 * q))
                ins.then_inc(S("gf"), 1)
            for half in range(2):
                for q in range(4):
                    m = half * 4 + q
                    a = RCOLS["alt"][0] + 2 * m
                    ins = mm(ps[32 * q:32 * q + 32, 2, 0:2], geo[:, 0, m, :], rp[:, a:a + 2],
                             start=(half == 0), stop=(half == 1), tile_position=(0, 32 * q))
            ins.then_inc(S("gf"), 1)
            pe.wait_ge(S("gt_done"), 3)
            transposes(sq, 2, S("n2"), 1, S("T2"))
            pe.wait_ge(S("xT2"), 2)
            for name, bank, rows in (("q2", 4, P), ("q2r", 6, P), ("k2", 0, 64), ("k2r", 2, 64)):
                for c in range(2):
                    ins = mm(ps[0:rows, bank + c], W(name), xT[:, c * 512:(c + 1) * 512])
                ins.then_inc(S("qk2"), 1)
            pe.wait_ge(S("qrot"), 1)
            for j in range(NT):
                ins = mm(ps[:, 4, j * 64:(j + 1) * 64], xT[:, j * P:(j + 1) * P], W("v2"))
            ins.then_inc(S("v2"), 1)
            pe.wait_ge(S("krot"), 1)
            for s in range(2):
                for kt in range(NK):
                    n = s * NK + kt
                    if n % 2 == 0 and n >= 8:
                        pe.wait_ge(S("af_done"), n // 2 - 3)
                    bank = (0, 1, 2, 3)[n // 2 % 4]
                    ins = mm(ps[:, bank, (n % 2) * D1:(n % 2 + 1) * D1], gt[:, s, kt * P:(kt + 1) * P], RP("outw"))
                    if n % 2 == 1:
                        ins.then_inc(S("afp"), 1)
            mm(ps[:, 7, 0:D1], gt2[:], RP("outw")).then_inc(S("afp"), 1)
            pe.wait_ge(S("stacks"), 12 * 16)
            pe.wait_ge(S("k_ones"), 1)
            pe.wait_ge(S("af_done"), NK + 1)
            pe.wait_ge(ld_bf, 16)

            def score_rows(b, n):
                hh, i, c = ROW_CHUNKS[n]
                n += b * len(ROW_CHUNKS)
                if n >= 6:
                    pe.wait_ge(S("max_read"), row_free(n))
                bank = row_bank(n)
                wd = min(512, (i + 1) * P - c * 512)
                last = c == i // 4
                ins = mm(ps[:, bank, 0:wd], qst[0:MROW, b * NH + hh, i * P:(i + 1) * P],
                         kst[0:MROW, b * NKV + hh // 2, c * 512:c * 512 + wd], start=True, stop=not last)
                if last:
                    ins = mm(ps[:, bank, wd - P:wd], ident_b, mask_ts, start=False, stop=True)
                ins.then_inc(S("rows"), 1)

            def score_cols(b, step_n):
                j, heads = COL_STEPS[step_n]
                n = b * len(COL_STEPS) + step_n
                if n < 2:
                    pe.wait_ge(S("max_read"), WIDE - 2 + 2 * n)
                else:
                    pe.wait_ge(S("exp_done"), n - 1)
                bank = 2 + 2 * (n % 2)
                for x in range(2):
                    c, hh = (x, heads[0]) if len(heads) == 1 else (1, heads[x])
                    lo = max(j * P, c * 512)
                    diag = lo == j * P
                    ins = mm(ps[:, bank + x, lo - c * 512:512], kst[0:KROWS, b * NKV + hh // 2, j * P:(j + 1) * P],
                             qst[0:KROWS, b * NH + hh, lo:(c + 1) * 512], start=True, stop=not diag)
                    if diag:
                        ins = mm(ps[:, bank + x, lo - c * 512:lo - c * 512 + P], ident_b, mask_st, start=False, stop=True)
                ins.then_inc(S("cols"), 1)

            def weighted(b, j, c):
                if c < j // 4:
                    return
                pe.wait_ge(S("exp_done"), col_steps(b, j))
                if b == 1 and j == 0:
                    pe.wait_ge(S("yT0"), 2)
                lo = max(j * P, c * 512)
                for hh in range(NH):
                    ins = mm(ps[32 * hh:32 * hh + 32, 6 + c, lo - c * 512:512], va2[:, j, b, hh // 2, :],
                             pt[:, j % 2, hh, lo:(c + 1) * 512], start=(j == 0), stop=(j == 4 * c + 3),
                             tile_position=(0, 32 * hh))
                if c == 1:
                    ins.then_inc(S("pv"), 1)

            def y_transposes(b, bank):
                pe.wait_ge(S("yT%d" % b), 2)
                for j in range(NT):
                    ins = nc.tensor.transpose(ps[:, bank + j // 4, (j % 4) * P:(j % 4 + 1) * P], yT[:, b, j * P:(j + 1) * P], idt[:])
                ins.then_inc(S("yTT"), 1)

            for n in range(len(ROW_CHUNKS)):
                score_rows(0, n)
            for n in range(EARLY // 2):
                score_rows(1, n)
            pe.wait_ge(S("max_all"), 1)
            nc.tensor.transpose(ps[0:32, 6, 0:P], rw[:, 0, 0:32], idt[:]).then_inc(S("maxT"), 1)
            for n in range(EARLY // 2, EARLY):
                score_rows(1, n)
            todo = list(range(EARLY, len(ROW_CHUNKS)))
            pe.wait_ge(S("max_rows"), 48)
            pe.wait_ge(S("va2"), 1)
            for b in range(B):
                for n, (j, heads) in enumerate(COL_STEPS):
                    score_cols(b, n)
                    for _ in range(min(2, len(todo))):
                        score_rows(1, todo.pop(0))
                    if j >= 1 and heads[-1] == 1:
                        weighted(b, j - 1, 0)
                    if j >= 1 and heads[-1] == 3:
                        weighted(b, j - 1, 1)
                    if b == 1 and j == 1 and heads[-1] == 3:
                        pe.wait_ge(S("max_pieces"), 2)
                        y_transposes(0, 0)
                weighted(b, NT - 1, 1)
                if b == 0:
                    pe.wait_ge(S("max_all"), 2)
                    nc.tensor.transpose(ps[0:32, 0, 0:P], rw[:, 1, 0:32], idt[:]).then_inc(S("maxT"), 1)
                    pe.wait_ge(S("max_rows"), 96)
            y_transposes(1, 2)
            transposes(sq, 4, S("yn"), 2, S("T2b"))
            pe.wait_ge(S("xT2b"), 2)
            for j in range(NT):
                ins = mm(ps[:, j // 4, (j % 4) * P:(j % 4 + 1) * P], xT[:, j * P:(j + 1) * P], W("wo2"))
            ins.then_inc(S("o2"), 1)
            pe.wait_ge(S("fhl"), 2)
            for b in range(B):
                for j in range(NT):
                    ins = nc.tensor.transpose(ps[:, 2 + 2 * b + j // 4, (j % 4) * P:(j % 4 + 1) * P],
                                              fhl[:, j, b].rearrange("p q c -> p (q c)"), idt[:])
                    if j % 4 == 3:
                        ins.then_inc(S("Te"), 1)
            pe.wait_ge(S("e_split"), 2)
            for b in range(B):
                pe.wait_ge(S("xs%d" % b), 2)
                for j in range(NT):
                    o = ps[:, 6, (j * B + b) * 8:(j * B + b + 1) * 8]
                    mm(o, xs[:, b, j * P:(j + 1) * P], EP(e_hi, "rt", 0, 8), start=True, stop=False)
                    ins = mm(o, xs[:, b, j * P:(j + 1) * P], EP(e_lo, "rt", 0, 8), start=False, stop=True)
            ins.then_inc(S("logits"), 1)
            u_at = [0]
            z_at = [0]

            def up(t, pr, n3):
                b, hf = t // 2, t % 2
                n = u_at[0]
                u_at[0] += 1
                if n >= 3:
                    pe.wait_ge(S("gated"), n - 2)
                rhs = xs[:, b, hf * 512:(hf + 1) * 512]
                tile = 3 * pr + n3
                for m, name in enumerate(("w1", "w3")):
                    o = ps[:, 2 * (n % 3) + m]
                    mm(o, EP(e_hi, name, tile * P, (tile + 1) * P), rhs, start=True, stop=False)
                    ins = mm(o, EP(e_lo, name, tile * P, (tile + 1) * P), rhs, start=False, stop=True)
                ins.then_inc(S("up"), 1)

            def down(t, pr):
                n = t * NPAIR + pr
                b, hf = t // 2, t % 2
                if n == 0:
                    pe.wait_ge(S("wst"), 3)
                if n >= 1:
                    pe.wait_ge(S("zpair"), n)
                mm(ps[:, 7], selw(b, pr), wst[:, hf * 512:(hf + 1) * 512]).then_inc(S("wbp"), 1)
                pe.wait_ge(S("gated"), 3 * (n + 1))
                o = ps[:, 6]
                for k in range(2):
                    e = 2 * pr + k
                    mm(o[64 * k:64 * k + 64], E("w2m", e * 64, (e + 1) * 64), gh[:, n % 2, k, :], start=True, stop=False,
                       tile_position=(0, 64 * k), skip_group_check=True)
                mm(o, E("w2r", pr * P, (pr + 1) * P), gh[:, n % 2, 2, :], start=False, stop=True,
                   skip_group_check=True).then_inc(S("down"), 1)

            order = [(t, pr) for t in range(4) for pr in range(NPAIR)]
            pe.wait_ge(S("wT_src"), 1)
            for j in range(NT):
                ins = nc.tensor.transpose(ps[0:16, 6 + j // 4, (j % 4) * P:(j % 4 + 1) * P], rw[:, 7, j * 16:(j + 1) * 16], idt[:])
            ins.then_inc(S("wT"), 1)
            for n, (t, pr) in enumerate(order):
                for n3 in range(3):
                    up(t, pr, n3)
                if n >= 1:
                    down(*order[n - 1])
            down(*order[-1])
            pe.wait_ge(S("zsum"), 4 * NPAIR)
            pe.wait_ge(S("gated"), 48)
            for j in range(NT):
                for b in range(B):
                    ins = mm(ps[:, j // 4, (j % 4) * P + b * 64:(j % 4) * P + b * 64 + 64], zacc[b][:, j * P:(j + 1) * P], E("ii"))
            ins.then_inc(S("moe"), 1)
            transposes(x1, 2, S("n3"), 1, S("T3"))
            pe.wait_ge(S("xT3"), 2)

            def half_tokens(tile):
                at = (tile + NU) % NT * P
                return xT[:, at:at + P]

            for n in range(2 * NT):
                name, tile = ("v3", "u3")[n // NT], n % NT
                if n >= 4:
                    pe.wait_ge(S("uv_read"), n - 3)
                mm(ps[:, 4 + n % 4, 0:384], half_tokens(tile), W(name)).then_inc(S("uv"), 1)
            pe.wait_ge(ld_u, 32)
            pe.wait_ge(S("veo"), 2)
            pe.wait_ge(S("T3_read"), 1)
            for kt in range(NK):
                if kt >= 2:
                    pe.wait_ge(S("spec_read"), kt - 1)
                for s in range(2):
                    for u in range(NU):
                        ins = mm(ps[:, 2 * (kt % 2) + s, 0:384], tu_s[:, s, u, kt * P:(kt + 1) * P], veo[:, s, u, :],
                                 start=(u == 0), stop=(u == NU - 1))
                ins.then_inc(S("spec"), 1)
            pe.wait_ge(ld_k, 32)
            pe.wait_ge(S("uv_read"), 2 * NT)
            pe.wait_ge(S("prod"), NK)

            def back_transposes(u):
                for k in range(2):
                    n = 2 * u + k
                    pe.wait_ge(S("y3"), n + 1)
                    if n >= 2:
                        pe.wait_ge(S("yT3"), n - 1)
                    for c in range(3):
                        ins = nc.tensor.transpose(ps[:, n % 2, c * P:(c + 1) * P],
                                                  y3[:, n % 2, c * P:(c + 1) * P], idt[:])
                    ins.then_inc(S("yTp"), 1)

            for u in range(NU):
                if u >= 2:
                    pe.wait_ge(S("inv_read"), u - 1)
                for s in range(2):
                    for kt in range(NK):
                        ins = mm(ps[:, 4 + 2 * (u % 2) + s, 0:384], tk_s[:, s, kt, u * P:(u + 1) * P],
                                 (orr if s == 0 else oss)[:, kt, :], start=(kt == 0), stop=(kt == NK - 1))
                ins.then_inc(S("inv"), 1)
                if u >= 1:
                    back_transposes(u - 1)
            back_transposes(NU - 1)
            pe.wait_ge(S("yT3"), 2 * NU)
            for j in range(NT):
                for c in range(3):
                    if j >= NU:
                        lhs = yT3[:, 2 * (j - NU), c, :]
                    else:
                        lhs = yT3[:, 2 * (NU - 1 - j) + 1, c, :]
                    ins = mm(ps[:, 2 + j // 4, (j % 4) * P:(j % 4 + 1) * P], lhs, W("o3", c * P, (c + 1) * P),
                             start=(c == 0), stop=(c == 2))
            ins.then_inc(S("o3"), 1)
            transposes(xc, 4, S("d3"), 1, S("T3b"))
            pe.wait_ge(S("xT3b"), 2)
            for j in range(NT):
                ins = mm(ps[:, j // 4, (j % 4) * P:(j % 4 + 1) * P], xT[:, j * P:(j + 1) * P], W("t3"))
            ins.then_inc(S("t3"), 1)
            transposes(sq, 2, S("n4"), 1, S("T4"))
            pe.wait_ge(S("xT4"), 2)
            for j in range(NT):
                ins = mm(ps[:, 4 + j // 4, (j % 4) * P:(j % 4 + 1) * P], xT[:, j * P:(j + 1) * P], W("w4"))
            ins.then_inc(S("o4"), 1)

        xn_view = sq
        @block.scalar
        def _(act):
            chain = [0]

            def step(ins):
                chain[0] += 1
                ins.then_inc(act_chain, 1)
                act.wait_ge(act_chain, chain[0])

            def evac(bank, done_wait, value, out_sem, scale=None):
                act.wait_ge(done_wait, value)
                if scale is None:
                    nc.scalar.copy(xT[:, 0:512], ps[:, bank]).then_inc(out_sem, 1)
                else:
                    nc.scalar.activation(xT[:, 0:512], ps[:, bank], ACT.Copy, scale=scale).then_inc(out_sem, 1)

            act.wait_ge(ld_rp, 16)
            nc.scalar.activation(rh[:, 0], RP("lag"), ACT.Identity, scale=RP("pw"), bias=RP("pb")).then_inc(S("r_h"), 1)
            for i in range(LAYERS + 1):
                act.wait_ge(S("r_ss"), i + 1)
                if i >= 1:
                    act.wait_ge(S("r_act"), i)
                nc.scalar.activation(rh[:, 2], ps[:, 0, 0:P], ACT.Sqrt, scale=1.0 / R).then_inc(S("r_rms"), 1)
                if i < LAYERS:
                    act.wait_ge(S("r_lin"), i + 1)
                    nc.scalar.activation(rh[:, 0], ps[:, 1, 0:P], ACT.Identity, bias=RP("b%d" % i)).then_inc(S("r_h"), 1)
            act.wait_ge(S("var1"), 1)
            nc.scalar.activation(st[:, 3], st[:, 2], ACT.Sqrt).then_inc(S("std1"), 1)
            evac(2, S("T1"), 1, S("xT1"))
            act.wait_ge(S("qmin"), 1)
            nc.scalar.activation(qf1[:], tmp[:], ACT.Exp).then_inc(S("qexp"), 1)
            act.wait_ge(S("kmin"), 1)
            nc.scalar.activation(kf1[:], kf1[:], ACT.Exp).then_inc(S("kexp"), 1)
            act.wait_ge(S("kf1"), 1)
            nc.scalar.copy(va1[:, :, 0:P].rearrange("p j (b c) -> p j b c", b=B),
                           ps[:, 0:4].rearrange("p a (g b k c) -> p (a g) b k c", g=2, b=B, k=2)[:, :, :, 1, :]).then_inc(S("va1"), 1)
            evac(4, S("T1b"), 1, S("xT1b"))
            for s in range(2):
                act.wait_ge(S("gf"), s + 1)
                nc.scalar.copy(gt[:, s], ps[:, 4 + 2 * s:6 + 2 * s].rearrange("p a t -> p (a t)")).then_inc(S("gt_done"), 1)
            act.wait_ge(S("gt_done"), 1)
            step(nc.scalar.copy(gt2[:], gt[:, 0, 0:P]))
            act.wait_ge(S("gf"), 3)
            nc.scalar.copy(gt2[:, 0:1], ps[:, 2, 0:1]).then_inc(S("gt_done"), 1)
            act.wait_ge(S("var2"), 1)
            nc.scalar.activation(st[:, 3], st[:, 2], ACT.Sqrt).then_inc(S("std2"), 1)
            act.wait_ge(S("msq2"), 1)
            nc.scalar.activation(st[:, 6], st[:, 5], ACT.Sqrt).then_inc(S("rms2"), 1)
            evac(2, S("T2"), 1, S("xT2"), scale=W("ln1"))
            act.wait_ge(S("v2"), 1)
            act.wait_ge(S("va2_ones"), 1)
            nc.scalar.copy(va2[:, :, :, :, 0:HD],
                           ps[:, 4].rearrange("p (j b k d) -> p j b k d", j=NT, b=B, k=NKV)).then_inc(S("va2"), 1)
            for n in range(NK):
                act.wait_ge(S("afp"), n + 1)
                s, kt = n // 4, 2 * (n % 4)
                nc.scalar.copy(af[:, s, kt:kt + 2].rearrange("p k c -> p (k c)"), ps[:, n % 4, 0:384]).then_inc(S("af_done"), 1)
            act.wait_ge(S("afp"), NK + 1)
            nc.scalar.copy(afn[:], ps[:, 7, 0:D1]).then_inc(S("af_done"), 1)
            for b in range(B):
                for step_n, (j, heads) in enumerate(COL_STEPS):
                    n = b * len(COL_STEPS) + step_n
                    act.wait_ge(S("cols"), n + 1)
                    if b * NT + j >= 2 and heads[0] == 0:
                        act.wait_ge(S("pv"), b * NT + j - 1)
                    bank = 2 + 2 * (n % 2)
                    if len(heads) == 1:
                        dst = pt[:, j % 2, heads[0], j * P:N]
                        src = ps[:, bank:bank + 2].rearrange("p a t -> p (a t)")[:, j * P:N]
                    else:
                        dst = pt[:, j % 2, heads[0]:heads[1] + 1, j * P:N]
                        src = ps[:, bank:bank + 2, j * P - 512:512]
                    nc.scalar.activation(dst, src, ACT.Exp, scale=HD ** -0.5).then_inc(S("exp_done"), 1)
                act.wait_ge(S("pv"), (b + 1) * NT)
                nc.scalar.copy(yT[:, b, 0:512], ps[:, 6]).then_inc(S("yT%d" % b), 1)
            evac(4, S("T2b"), 1, S("xT2b"))
            act.wait_ge(S("var2b"), 1)
            nc.scalar.activation(st[:, 3], st[:, 2], ACT.Sqrt).then_inc(S("rms2b"), 1)
            for b in range(B):
                act.wait_ge(S("Te"), 2 * b + 1)
                nc.scalar.copy(xs[:, b, 0:512], ps[:, 2 + 2 * b]).then_inc(S("xs%d" % b), 1)
            act.wait_ge(S("lmax"), 1)
            nc.scalar.activation(rw[:, 1], rw[:, 0], ACT.Exp).then_inc(S("lexp"), 1)
            for n in range(16):
                for n3 in range(3):
                    m = 3 * n + n3
                    act.wait_ge(S("up"), m + 1)
                    if m >= 2:
                        act.wait_ge(S("gated"), m - 1)
                    nc.scalar.activation(sil[:, m % 2], ps[:, 2 * (m % 3)], ACT.Silu).then_inc(S("silu"), 1)
                if n >= 1:
                    act.wait_ge(S("wbp"), n)
                    if n >= 3:
                        act.wait_ge(S("zpair"), n - 2)
                    nc.scalar.copy(wb[:, (n - 1) % 2], ps[:, 7]).then_inc(S("wb"), 1)
            act.wait_ge(S("wbp"), 16)
            act.wait_ge(S("zpair"), 14)
            nc.scalar.copy(wb[:, 1], ps[:, 7]).then_inc(S("wb"), 1)
            act.wait_ge(S("var3"), 1)
            nc.scalar.activation(st[:, 3], st[:, 2], ACT.Sqrt).then_inc(S("std3"), 1)
            act.wait_ge(S("T3"), 1)
            nc.scalar.copy(xT[:, 0:512], ps[:, 2][:, ::-1]).then_inc(S("xT3"), 1)

            def y_columns(n):
                act.wait_ge(S("yTp"), n + 1)
                src = ps[:, n % 2, 0:384].rearrange("p (c t) -> p c t", c=3)
                nc.scalar.copy(yT3[:, n], src[:, :, ::-1] if n % 2 else src).then_inc(S("yT3"), 1)

            for n in range(2 * NT):
                act.wait_ge(S("uv_read"), n + 1)
                dst = (vs if n < NT else us)[:, n % NT]
                nc.scalar.activation(dst, dst, ACT.Silu).then_inc(S("uv_silu"), 1)
            for u in range(NU):
                act.wait_ge(S("inv"), u + 1)
                if u >= 1:
                    act.wait_ge(S("inv_read"), u)
                nc.scalar.copy(tmp[:, 0:384], ps[:, 4 + 2 * (u % 2), 0:384]).then_inc(S("even"), 1)
                for k in range(2):
                    if u >= 1:
                        y_columns(2 * (u - 1) + k)
            for n in range(2 * NU - 2, 2 * NU):
                y_columns(n)
            evac(4, S("T3b"), 1, S("xT3b"))
            act.wait_ge(S("var3b"), 1)
            nc.scalar.activation(st[:, 3], st[:, 2], ACT.Sqrt, scale=1.0 / D1).then_inc(S("rms3b"), 1)
            act.wait_ge(S("e3"), 1)
            nc.scalar.activation(xc[:], xc[:], ACT.Silu).then_inc(S("xr"), 1)
            act.wait_ge(S("var4"), 1)
            nc.scalar.activation(st[:, 3], st[:, 2], ACT.Sqrt).then_inc(S("std4"), 1)
            evac(2, S("T4"), 1, S("xT4"))

        @block.vector
        def _(dve):
            V = nc.vector
            chain = [0]

            def step(ins):
                chain[0] += 1
                ins.then_inc(dve_chain, 1)
                dve.wait_ge(dve_chain, chain[0])

            def evac(bank, done_wait, value, out_sem, scale=None):
                dve.wait_ge(done_wait, value)
                if scale is None:
                    V.tensor_copy(xT[:, 512:N], ps[:, bank]).then_inc(out_sem, 1)
                else:
                    V.tensor_scalar(xT[:, 512:N], ps[:, bank], scale, None, ALU.mult).then_inc(out_sem, 1)

            def per_token(v):
                return spread(v, 2, C)

            def flat3(t):
                return t[:].rearrange("p j b c -> p (j b) c")

            def flat2(t):
                return t[:].rearrange("p j b c -> p (j b c)")

            def centre(var_sem):
                step(V.tensor_reduce(st[:, 0], flat3(h), AXX, ALU.add))
                step(V.tensor_scalar(st[:, 0], st[:, 0], 1.0 / C, None, ALU.mult))
                step(V.tensor_tensor(flat3(xc), flat3(h), per_token(st[:, 0]), ALU.subtract))
                step(V.tensor_tensor(flat2(sq), flat2(xc), flat2(xc), ALU.mult))
                step(V.tensor_reduce(st[:, 1], flat3(sq), AXX, ALU.add))
                step(V.tensor_scalar(st[:, 1], st[:, 1], 1.0 / C, None, ALU.mult))
                V.tensor_scalar(st[:, 2], st[:, 1], 1e-5, None, ALU.add).then_inc(var_sem, 1)

            def weigh(n):
                dve.wait_ge(S("wb"), n + 1)
                dve.wait_ge(S("down"), n + 1)
                if n >= 2:
                    dve.wait_ge(S("zsum"), n - 1)
                V.tensor_tensor(zp_[:, n % 2], ps[:, 6], wb[:, n % 2], ALU.mult).then_inc(S("zpair"), 1)

            dve.wait_ge(ld_rp, 16)
            for i in range(LAYERS + 1):
                dve.wait_ge(S("r_h"), i + 1)
                if i >= 1:
                    dve.wait_ge(S("r_ss"), i)
                V.tensor_tensor(rh[:, 1], rh[:, 0], rh[:, 0], ALU.mult).then_inc(S("r_sq"), 1)
                dve.wait_ge(S("r_rms"), i + 1)
                step(V.tensor_scalar(rh[:, 2], rh[:, 2], 1e-8, None, ALU.add))
                step(V.reciprocal(rh[:, 2], rh[:, 2]))
                V.scalar_tensor_tensor(out=rh[:, 3], in0=rh[:, 0], scalar=0.0, in1=rh[:, 2], op0=ALU.max,
                                       op1=ALU.mult).then_inc(S("r_act"), 1)
            dve.wait_ge(S("r_T"), 1)
            dve.wait_ge(S("geo_ones"), 1)
            step(V.tensor_copy(rh[:, 1], ps[:, 1, 0:P]))
            plus = rh[:, 1, 0:64].rearrange("p (g r) -> p g r", r=R)
            minus = rh[:, 1, 64:128].rearrange("p (g r) -> p g r", r=R)
            step(V.tensor_tensor(geo[:, 0, :, 0:R], plus, minus, ALU.add))
            step(V.tensor_tensor(geo[:, 1, :, 0:R], plus, minus, ALU.subtract))
            dve.wait_ge(gathered, 16 * NT * B)
            dve.wait_ge(ld_pe, 16)
            for b in range(B):
                ins = V.tensor_tensor(h[:, :, b, :], xc[:, :, b, :], pe_s[:], ALU.add)
                step(ins)
            centre(S("var1"))
            dve.wait_ge(S("std1"), 1)
            step(V.reciprocal(st[:, 4], st[:, 3]))
            V.tensor_tensor(flat3(sq), flat3(xc), per_token(st[:, 4]), ALU.mult).then_inc(S("n1"), 1)
            evac(3, S("T1"), 2, S("xT1"))
            dve.wait_ge(S("xT1"), 2)
            V.tensor_copy(st[:, 0], st[:, 4]).then_inc(S("geo_done"), 1)
            dve.wait_ge(S("q1"), 2)
            qps = ps[:, 4:6].rearrange("p a t -> p (a t)")
            V.tensor_scalar(tmp[:], qps, 0.0, None, ALU.min).then_inc(S("qmin"), 1)
            dve.wait_ge(S("kv1"), NT)
            kps = ps[:, 0:4].rearrange("p a (g k c) -> p (a g) k c", g=4, k=2)[:, :, 0, :]
            V.tensor_scalar(kf1.rearrange("p j b c -> p (j b) c"), kps, 0.0, None, ALU.min).then_inc(S("kmin"), 1)
            dve.wait_ge(S("kexp"), 1)
            V.scalar_tensor_tensor(out=kf1.rearrange("p j b c -> p (j b) c"), in0=kps, scalar=0.0, in1=kf1.rearrange("p j b c -> p (j b) c"), op0=ALU.max,
                                   op1=ALU.add).then_inc(S("kf1"), 1)
            dve.wait_ge(S("qexp"), 1)
            V.scalar_tensor_tensor(out=qf1[:], in0=qps, scalar=0.0, in1=qf1[:], op0=ALU.max, op1=ALU.add).then_inc(S("qf1"), 1)
            dve.wait_ge(S("ctx1"), 1)
            dve.wait_ge(ld_w, 16)
            V.tensor_tensor(cbd[:, 0:P], ps[:, 6, 0:P], W("mask_c"), ALU.mult).then_inc(S("cbd"), 1)
            V.tensor_scalar(cbd[:, P:144], W("mask_k"), ps[:, 6, P:P + 1], None, ALU.mult).then_inc(S("cbd"), 1)
            dve.wait_ge(S("nd1"), 1)
            nd = ps[:, 0:4].rearrange("p a (g x) -> p (a g) x", g=2)
            den = rw[:, 0].rearrange("p (j g) -> p j g", g=16)
            step(V.tensor_scalar(den, nd[:, :, P:144], 1e-6, None, ALU.max))
            step(V.reciprocal(rw[:, 0], rw[:, 0]))
            V.tensor_tensor(sq[:].rearrange("p j b (g d) -> p j (b g) d", d=8),
                            nd[:, :, 0:P].rearrange("p j (g d) -> p j g d", d=8),
                            spread(den, 3, 8), ALU.mult).then_inc(S("attn1"), 1)
            step(V.tensor_tensor(h[:].rearrange("p j b c -> p j (b c)"), h[:].rearrange("p j b c -> p j (b c)"),
                                 spread(W("bproj"), 1, NT), ALU.add))
            evac(5, S("T1b"), 2, S("xT1b"))
            dve.wait_ge(S("o1"), 1)
            step(V.tensor_tensor(flat2(h), flat2(h), ps[:, 0:2].rearrange("p a t -> p (a t)"), ALU.add))
            centre(S("var2"))
            dve.wait_ge(S("std2"), 1)
            step(V.reciprocal(st[:, 4], st[:, 3]))
            step(V.tensor_tensor(st[:, 5], st[:, 4], st[:, 4], ALU.mult))
            step(V.tensor_tensor(st[:, 5], st[:, 5], st[:, 1], ALU.mult))
            V.tensor_scalar(st[:, 5], st[:, 5], 1e-6, None, ALU.add).then_inc(S("msq2"), 1)
            step(V.tensor_tensor(flat3(x1), flat3(xc), per_token(st[:, 4]), ALU.mult))
            dve.wait_ge(S("rms2"), 1)
            step(V.reciprocal(st[:, 7], st[:, 6]))
            V.tensor_tensor(flat3(sq), flat3(x1), per_token(st[:, 7]), ALU.mult).then_inc(S("n2"), 1)
            evac(3, S("T2"), 2, S("xT2"), scale=W("ln1"))
            dve.wait_ge(ld_rope, 16)
            dve.wait_ge(S("qk2"), 1)
            step(V.tensor_tensor(qr[:], ps[:, 4:6].rearrange("p a t -> p (a t)"), rope_s[:, 0], ALU.mult))
            dve.wait_ge(S("qk2"), 2)
            V.tensor_tensor(tmp[:], ps[:, 6:8].rearrange("p a t -> p (a t)"), rope_s[:, 1], ALU.mult).then_inc(S("qrot"), 1)
            dve.wait_ge(S("qrot"), 1)
            step(V.tensor_tensor(qr[:], qr[:], tmp[:], ALU.add))
            dve.wait_ge(S("qk2"), 4)
            step(V.tensor_tensor(kr[:], ps[0:64, 0:2].rearrange("p a t -> p (a t)"), rope_s[0:64, 0], ALU.mult))
            V.tensor_tensor(tmp[0:64], ps[0:64, 2:4].rearrange("p a t -> p (a t)"), rope_s[0:64, 1], ALU.mult).then_inc(S("krot"), 1)
            dve.wait_ge(S("krot"), 1)
            V.tensor_tensor(kr[:], kr[:], tmp[0:64], ALU.add).then_inc(S("qrot"), 1)
            dve.wait_ge(S("qrot"), 2)
            dve.wait_ge(S("gt_done"), 3)
            for x, pcs in ((qr, pieces_q), (kr, pieces_k[0:64])):
                t = tmp[:] if x is qr else tmp[0:64]
                step(V.tensor_copy(pcs[:, 0], x[:]))
                step(V.tensor_tensor(t, x[:], pcs[:, 0], ALU.subtract))
                step(V.tensor_copy(pcs[:, 1], t))
                V.tensor_tensor(pcs[:, 2], t, pcs[:, 1], ALU.subtract).then_inc(S("k_pieces"), 1)
            dve.wait_ge(ld_e, 32)
            V.tensor_copy(e_hi[:], e_raw).then_inc(S("e_split"), 1)
            dve.wait_ge(S("e_split"), 1)
            V.tensor_tensor(e_lo[:], e_raw, e_hi[:].bitcast(F32), ALU.subtract).then_inc(S("e_split"), 1)
            def maxima(b):
                mx = rw[:, b, 0:32]
                m2 = rw[:, 2 + b, 0:32]
                for n, (hh, i, c) in enumerate(ROW_CHUNKS):
                    n += b * len(ROW_CHUNKS)
                    dve.wait_ge(S("rows"), n + 1)
                    wd = min(512, (i + 1) * P - c * 512)
                    dst = (mx if c == 0 else m2)[:, hh * NT + i:hh * NT + i + 1]
                    V.tensor_reduce(dst, ps[:, row_bank(n), 0:wd], AXX, ALU.max).then_inc(S("max_read"), 1)
                at = (b + 1) * len(ROW_CHUNKS)
                dve.wait_ge(S("max_read"), at)
                a3 = mx.rearrange("p (h i) -> p h i", i=NT)[:, :, 4:NT]
                b3 = m2.rearrange("p (h i) -> p h i", i=NT)[:, :, 4:NT]
                step(V.tensor_tensor(a3, a3, b3, ALU.max))
                V.tensor_scalar(mx, mx, -1.0, None, ALU.mult).then_inc(S("max_all"), 1)
                dve.wait_ge(S("maxT"), b + 1)
                if b == 1:
                    dve.wait_ge(S("max_rows"), 48)
                bank = 6 if b == 0 else 0
                step(V.tensor_copy(mrow[:, 0], ps[0:32, bank, 0:P]))
                step(V.tensor_tensor(mtmp[:], ps[0:32, bank, 0:P], mrow[:, 0], ALU.subtract))
                step(V.tensor_copy(mrow[:, 1], mtmp[:]))
                V.tensor_tensor(mrow[:, 2], mtmp[:], mrow[:, 1], ALU.subtract).then_inc(S("max_pieces"), 1)

            maxima(0)
            maxima(1)
            for b in range(B):
                dve.wait_ge(S("pv"), (b + 1) * NT)
                V.tensor_copy(yT[:, b, 512:N], ps[:, 7]).then_inc(S("yT%d" % b), 1)
                dve.wait_ge(S("yTT"), b + 1)
                y = ps[:, 2 * b:2 * b + 2].rearrange("p a (j h d) -> p (a j) h d", j=4, h=NH)
                dn = rw[:, 4 + b, 0:32]
                step(V.tensor_copy(dn.rearrange("p (j h) -> p j h", h=NH), y[:, :, :, HD]))
                step(V.reciprocal(dn, dn))
                V.tensor_tensor(sq[:, :, b, :].rearrange("p j (h d) -> p j h d", d=HD), y[:, :, :, 0:HD],
                                spread(dn.rearrange("p (j h) -> p j h", h=NH), 3, HD),
                                ALU.mult).then_inc(S("yn"), 1)
            evac(5, S("T2b"), 2, S("xT2b"))
            dve.wait_ge(S("o2"), 1)
            step(V.tensor_tensor(flat2(x1), flat2(x1), ps[:, 0:2].rearrange("p a t -> p (a t)"), ALU.add))
            step(V.tensor_tensor(flat2(sq), flat2(x1), flat2(x1), ALU.mult))
            step(V.tensor_reduce(st[:, 1], flat3(sq), AXX, ALU.add))
            V.tensor_scalar(st[:, 2], st[:, 1], 1.0 / C, 1e-6, ALU.mult, ALU.add).then_inc(S("var2b"), 1)
            dve.wait_ge(S("rms2b"), 1)
            step(V.reciprocal(st[:, 4], st[:, 3]))
            step(V.tensor_tensor(flat3(xc), flat3(x1), per_token(st[:, 4]), ALU.mult))
            xcj = xc[:].rearrange("p j b c -> p j (b c)")
            step(V.tensor_tensor(xcj, xcj, spread(W("ln2"), 1, NT), ALU.mult))
            hi = fhl[:, :, :, 0, :].rearrange("p j b c -> p (j b) c")
            lo = fhl[:, :, :, 1, :].rearrange("p j b c -> p (j b) c")
            V.tensor_copy(hi.bitcast(F32R), flat3(xc)).then_inc(S("fhl"), 1)
            dve.wait_ge(S("fhl"), 1)
            V.tensor_tensor(lo, flat3(xc), hi, ALU.subtract).then_inc(S("fhl"), 1)
            step(V.tensor_tensor(flat2(h), flat2(h), flat2(x1), ALU.add))
            for b in range(B):
                dve.wait_ge(S("Te"), 2 * b + 2)
                V.tensor_copy(xs[:, b, 512:N], ps[:, 3 + 2 * b]).then_inc(S("xs%d" % b), 1)
            g3 = lambda k: rw[:, k].rearrange("p (g e) -> p g e", e=NE)
            each = lambda v: spread(v, 2, NE)
            dve.wait_ge(S("logits"), 1)
            lg = ps[:, 6, 0:P].rearrange("p (g e) -> p g e", e=NE)
            eidx = W("eidx").rearrange("p (g e) -> p g e", e=NE)
            step(V.tensor_reduce(st[:, 5], lg, AXX, ALU.max))
            V.tensor_tensor(g3(0), lg, each(st[:, 5]), ALU.subtract).then_inc(S("lmax"), 1)
            dve.wait_ge(S("lexp"), 1)
            step(V.tensor_reduce(st[:, 6], g3(1), AXX, ALU.add))
            step(V.reciprocal(st[:, 6], st[:, 6]))
            step(V.tensor_tensor(g3(2), g3(1), each(st[:, 6]), ALU.mult))
            step(V.tensor_copy(g3(3), g3(2)))
            for k in range(2):
                step(V.tensor_reduce(st[:, 7 + k], g3(3), AXX, ALU.max))
                step(V.tensor_tensor(g3(4), g3(3), each(st[:, 7 + k]), ALU.is_equal))
                step(V.scalar_tensor_tensor(out=g3(4), in0=g3(4), scalar=-TOPK_OFF, in1=eidx, op0=ALU.mult, op1=ALU.add))
                step(V.tensor_reduce(st[:, 9], g3(4), AXX, ALU.min))
                step(V.tensor_scalar(st[:, 9], st[:, 9], TOPK_OFF, None, ALU.add))
                step(V.tensor_tensor(g3(5 + k), eidx, each(st[:, 9]), ALU.is_equal))
                if k == 0:
                    step(V.scalar_tensor_tensor(out=g3(3), in0=g3(5), scalar=-2.0, in1=g3(3), op0=ALU.mult, op1=ALU.add))
            step(V.tensor_tensor(st[:, 7], st[:, 7], st[:, 8], ALU.add))
            step(V.tensor_scalar(st[:, 7], st[:, 7], 1e-9, None, ALU.add))
            step(V.reciprocal(st[:, 7], st[:, 7]))
            step(V.tensor_tensor(g3(5), g3(5), g3(6), ALU.add))
            step(V.tensor_tensor(g3(5), g3(5), g3(2), ALU.mult))
            V.tensor_tensor(g3(7), g3(5), each(st[:, 7]), ALU.mult).then_inc(S("wT_src"), 1)
            dve.wait_ge(S("wT"), 1)
            dve.wait_ge(S("wst_zero"), 1)
            wps = ps[0:16, 6:8].rearrange("p a t -> p (a t)")
            V.tensor_copy(wst[0:16], wps).then_inc(S("wst"), 1)
            dve.wait_ge(S("wst"), 1)
            step(V.tensor_tensor(tmp[0:16], wps, wst[0:16], ALU.subtract))
            V.tensor_copy(wst[32:48], tmp[0:16]).then_inc(S("wst"), 1)
            dve.wait_ge(S("wst"), 2)
            step(V.tensor_copy(tmp[32:48], wst[32:48]))
            step(V.tensor_copy(xT[0:16], tmp[32:48]))
            V.tensor_tensor(wst[64:80], tmp[0:16], xT[0:16], ALU.subtract).then_inc(S("wst"), 1)
            for n in range(16):
                for n3 in range(3):
                    m = 3 * n + n3
                    dve.wait_ge(S("silu"), m + 1)
                    if n >= 2 and n3 == 0:
                        dve.wait_ge(S("down"), n - 1)
                    V.tensor_tensor(gh[:, n % 2, n3], ps[:, 2 * (m % 3) + 1], sil[:, m % 2], ALU.mult).then_inc(S("gated"), 1)
                if n >= 1:
                    weigh(n - 1)
            weigh(15)
            dve.wait_ge(S("moe"), 1)
            step(V.tensor_tensor(flat2(h), flat2(h), ps[:, 0:2].rearrange("p a t -> p (a t)"), ALU.add))
            centre(S("var3"))
            dve.wait_ge(S("std3"), 1)
            step(V.reciprocal(st[:, 4], st[:, 3]))
            V.tensor_tensor(flat3(x1), flat3(xc), per_token(st[:, 4]), ALU.mult).then_inc(S("n3"), 1)
            evac(3, S("T3"), 2, S("xT3"))
            dve.wait_ge(S("xT3"), 2)
            V.tensor_copy(st[:, 8], st[:, 4]).then_inc(S("T3_read"), 1)
            for n in range(2 * NT):
                dve.wait_ge(S("uv"), n + 1)
                dst = (vs if n < NT else us)[:, n % NT]
                V.tensor_tensor(dst, ps[:, 4 + n % 4, 0:384], W("vb" if n < NT else "ub"), ALU.add).then_inc(S("uv_read"), 1)
                if n == NT + 3:
                    dve.wait_ge(S("uv_silu"), NT)
                    for s, op in enumerate((ALU.add, ALU.subtract)):
                        V.tensor_tensor(veo[:, s], vs[:, 0:NU], vs[:, NU:NT], op).then_inc(S("veo"), 1)
            step(V.tensor_tensor(flat2(h), flat2(h), flat2(x1), ALU.add))
            step(V.tensor_tensor(xc[:].rearrange("p j b c -> p j (b c)"), x1[:].rearrange("p j b c -> p j (b c)"),
                                 spread(W("ob"), 1, NT), ALU.subtract))
            two = lambda v: v.rearrange("p (b c) -> p b c", b=B)
            both = lambda v: spread(v, 1, B)
            dve.wait_ge(S("af_done"), NK + 1)
            for kt in range(NK):
                dve.wait_ge(S("spec"), kt + 1)
                pc, px = two(ps[:, 2 * (kt % 2), 0:384]), two(ps[:, 2 * (kt % 2) + 1, 0:384])
                ac, asn = both(af[:, 0, kt]), both(af[:, 1, kt])
                ac2 = both(afn[:]) if kt == 0 else ac
                t1, t2 = two(tmp[:, 0:384]), two(tmp[:, 384:768])
                step(V.tensor_tensor(two(orr[:, kt]), pc, ac, ALU.mult))
                step(V.tensor_tensor(t1, px, asn, ALU.mult))
                step(V.tensor_tensor(two(oss[:, kt]), pc, asn, ALU.mult))
                V.tensor_tensor(t2, px, ac2, ALU.mult).then_inc(S("spec_read"), 1)
                dve.wait_ge(S("spec_read"), kt + 1)
                step(V.tensor_tensor(two(orr[:, kt]), two(orr[:, kt]), t1, ALU.subtract))
                V.tensor_tensor(two(oss[:, kt]), two(oss[:, kt]), t2, ALU.add).then_inc(S("prod"), 1)
            dve.wait_ge(S("prod"), NK)
            dve.wait_ge(S("uv_silu"), 2 * NT)
            for u in range(NU):
                dve.wait_ge(S("even"), u + 1)
                odd = ps[:, 5 + 2 * (u % 2), 0:384]
                if u >= 1:
                    dve.wait_ge(S("yTp"), 2 * u)
                step(V.tensor_tensor(y3[:, 0], tmp[:, 0:384], odd, ALU.add))
                V.tensor_tensor(y3[:, 1], tmp[:, 0:384], odd, ALU.subtract).then_inc(S("inv_read"), 1)
                dve.wait_ge(S("inv_read"), u + 1)
                V.tensor_tensor(y3[:, 0], y3[:, 0], us[:, u], ALU.mult).then_inc(S("y3"), 1)
                V.tensor_tensor(y3[:, 1], y3[:, 1], us[:, NU + u], ALU.mult).then_inc(S("y3"), 1)
            dve.wait_ge(S("o3"), 1)
            V.tensor_tensor(flat2(xc), flat2(xc), ps[:, 2:4].rearrange("p a t -> p (a t)"), ALU.subtract).then_inc(S("d3"), 1)
            evac(5, S("T3b"), 2, S("xT3b"))
            dve.wait_ge(S("t3"), 1)
            dve.wait_ge(S("xT3b"), 2)
            step(V.tensor_tensor(xc[:].rearrange("p j b c -> p j (b c)"),
                                 ps[:, 0:2].rearrange("p a (j x) -> p (a j) x", j=4),
                                 spread(W("tb"), 1, NT), ALU.add))
            step(V.tensor_tensor(flat2(sq), flat2(xc), flat2(xc), ALU.mult))
            V.tensor_reduce(st[:, 2], flat3(sq), AXX, ALU.add).then_inc(S("var3b"), 1)
            dve.wait_ge(S("rms3b"), 1)
            step(V.tensor_scalar(st[:, 3], st[:, 3], 1e-8, None, ALU.add))
            step(V.reciprocal(st[:, 4], st[:, 3]))
            V.tensor_tensor(flat3(xc), flat3(xc), per_token(st[:, 4]), ALU.mult).then_inc(S("e3"), 1)
            dve.wait_ge(S("xr"), 1)
            step(V.tensor_tensor(flat2(h), flat2(h), flat2(xc), ALU.add))
            centre(S("var4"))
            dve.wait_ge(S("std4"), 1)
            step(V.reciprocal(st[:, 4], st[:, 3]))
            V.tensor_tensor(flat3(sq), flat3(xc), per_token(st[:, 4]), ALU.mult).then_inc(S("n4"), 1)
            evac(3, S("T4"), 2, S("xT4"))
            hj = h[:].rearrange("p j b c -> p j (b c)")
            step(V.tensor_tensor(hj, hj, spread(W("b4"), 1, NT), ALU.add))
            dve.wait_ge(S("o4"), 1)
            V.tensor_tensor(flat2(sq), flat2(h), ps[:, 4:6].rearrange("p a t -> p (a t)"), ALU.add).then_inc(S("final"), 1)



def positions():
    pos = np.arange(N, dtype=np.float32)[:, None]
    d = np.arange(C)
    inv = np.power(np.float32(10000.0), -((d - d % 2).astype(np.float32) / np.float32(C))).astype(np.float32)
    ang = (pos * inv).astype(np.float32).astype(np.float64)
    pe = np.where(d % 2 == 0, np.sin(ang), np.cos(ang)).astype(np.float32)
    return np.ascontiguousarray(pe.reshape(NT, P, C).transpose(1, 0, 2))


def rope_tables():
    inv = (1.0 / 10000.0 ** (np.arange(0, HD, 2, dtype=np.float32) / HD)).astype(np.float32)
    f = np.outer(np.arange(N, dtype=np.float32), inv).astype(np.float32)
    emb = np.concatenate([f, f], -1)
    sign = np.where(np.arange(HD) < HD // 2, -1.0, 1.0).astype(np.float32)
    t = np.stack([np.tile(np.cos(emb).T, (P // HD, 1)), np.tile((np.sin(emb) * sign).T, (P // HD, 1))], 1)
    return np.ascontiguousarray(t.astype(np.float32))


def fourier_tables():
    m, k = np.arange(N)[:, None], np.arange(N)[None, :]
    u = np.arange(N // 2)[:, None] + 0.5
    ph = 2 * np.pi * ((m * k) % (2 * N)) / (2 * N)
    tm = np.stack([np.cos(ph), np.sin(ph)])
    tm[:, 0] *= 0.5
    pu = 2 * np.pi * np.mod(u * k, 2 * N) / (2 * N)
    tu = np.stack([np.cos(pu), np.sin(pu)])
    tu[1, :, 0] = np.sin(np.pi * u[:, 0])
    wk = np.where(k == 0, 1.0, 2.0) / (2 * N)
    tk = (tu * wk).transpose(0, 2, 1)
    alt = np.repeat(np.where(np.arange(N) % 2 == 0, 1.0, -1.0)[:, None], 2, 1)
    alt[0] *= 0.5
    lay = lambda t, n: np.ascontiguousarray(t.reshape(2, n, P, -1).transpose(0, 2, 1, 3).astype(np.float32))
    return (lay(tm, NT), lay(tu, NU), lay(tk, NK).reshape(2, P, -1),
            alt.reshape(NT, P, 2).transpose(1, 0, 2).reshape(P, -1).astype(np.float32))


def kernel(**inputs):
    import concourse.bacc as _bacc
    from concourse.bass_utils import run_bass_kernel_spmd as _run
    import ml_dtypes

    a = {k: np.asarray(v) for k, v in inputs.items()}
    f32 = np.float32

    def twice(m):
        k, n = m.shape
        o = np.zeros((2 * k, 2 * n), f32)
        o[:k, :n] = m
        o[k:, n:] = m
        return o

    rot = np.concatenate([np.arange(HD // 2, HD), np.arange(HD // 2)])
    turned = lambda m: m.reshape(-1, HD, C)[:, rot].reshape(-1, C)
    wp = np.zeros((P, WTOT), f32)

    def put(name, m):
        lo, hi = WCOLS[name]
        wp[:m.shape[0], lo:hi] = m.reshape(m.shape[0], -1)

    rows = lambda v, n=1: np.broadcast_to(np.tile(v, n)[None], (P, v.size * n))
    put("q1", twice(a["L0_attn_Wq"].T))
    put("kv1", twice(a["L0_attn_Wkv"].T))
    put("proj1", twice(a["L0_attn_Wproj"].T))
    put("q2", twice(a["L0_ffn_wq"].T))
    put("q2r", twice(turned(a["L0_ffn_wq"]).T))
    put("k2", twice(a["L0_ffn_wk"].T))
    put("k2r", twice(turned(a["L0_ffn_wk"]).T))
    put("v2", twice(a["L0_ffn_wv"].T))
    put("wo2", twice(a["L0_ffn_wo"].T))
    put("v3", twice(a["L1_attn_v_w"].T))
    put("u3", twice(a["L1_attn_u_w"].T))
    o3 = twice(a["L1_attn_o_w"].T).reshape(3, P, P).transpose(1, 0, 2)
    put("o3", o3.reshape(P, -1))
    put("t3", twice(a["L1_attn_t_w"].T))
    put("w4", twice(a["L1_ffn_weight"].T))
    put("bproj", rows(a["L0_attn_bproj"], 2))
    put("ub", rows(a["L1_attn_u_b"], 2))
    put("vb", rows(a["L1_attn_v_b"], 2))
    put("ob", rows(a["L1_attn_o_b"], 2))
    put("tb", rows(a["L1_attn_t_b"], 2))
    put("b4", rows(a["L1_ffn_bias"], 2))
    put("ln2", rows(a["L0_ffn_ln2_w"], 2))
    put("ln1", np.tile(a["L0_ffn_ln1_w"], 2)[:, None])
    hd = np.arange(P) // 8
    put("mask_c", (hd[:, None] == hd[None, :]).astype(f32))
    put("mask_k", (hd[:, None] == np.arange(16)[None, :]).astype(f32))
    put("eidx", np.broadcast_to(np.tile(np.arange(NE) + NE, 16).astype(f32)[None], (P, P)))

    tm, tu, tk, alt = fourier_tables()
    rp = np.zeros((P, RTOT), f32)

    def rput(name, m):
        lo, hi = RCOLS[name]
        rp[:, lo:hi] = m

    groups = P // R
    lag = np.arange(N, dtype=f32).reshape(NT, P)
    rput("lag", np.repeat(np.concatenate([lag, -lag]), R, 0))
    g = np.arange(P) // R
    rput("ones", (g[:, None] == g[None, :]).astype(f32))
    for i in range(LAYERS):
        bd = np.zeros((P, P), f32)
        for q in range(groups):
            bd[q * R:(q + 1) * R, q * R:(q + 1) * R] = a["L1_attn_rpe_lw"][i].T
        rput("l%d" % i, bd)
        rput("b%d" % i, np.tile(a["L1_attn_rpe_lb"][i], groups)[:, None])
    rput("pw", np.tile(a["L1_attn_pos_w"][:, 0], groups)[:, None])
    rput("pb", np.tile(a["L1_attn_pos_b"], groups)[:, None])
    ow = np.zeros((4, 32, D1), f32)
    ow[:, :R] = a["L1_attn_out_w"].T
    ow[:, R] = a["L1_attn_out_b"]
    rput("outw", ow.reshape(P, D1))
    rput("alt", alt)

    ep = np.zeros((P, ETOT), f32)
    for name, key in (("w1", "L0_ffn_w1"), ("w3", "L0_ffn_w3")):
        src = a[key]
        t = np.zeros((12, P, C), f32)
        for pr in range(NPAIR):
            for k in range(2):
                t[3 * pr + k] = src[2 * pr + k, :P]
                t[3 * pr + 2, 64 * k:64 * k + REM] = src[2 * pr + k, P:]
        t = t.transpose(2, 0, 1).reshape(C, -1)
        ep[:, ECOLS[name][0]:ECOLS[name][1]] = np.concatenate([t, t])
    r = a["L0_ffn_router_w"].T
    ep[:, ECOLS["rt"][0]:ECOLS["rt"][1]] = np.concatenate([r, r])
    w2 = a["L0_ffn_w2"]
    ep[:, ECOLS["w2m"][0]:ECOLS["w2m"][1]] = w2[:, :, :P].transpose(2, 0, 1).reshape(P, -1)
    t = np.zeros((P, NPAIR, 2, C), f32)
    for pr in range(NPAIR):
        for k in range(2):
            t[64 * k:64 * k + REM, pr, k] = w2[2 * pr + k, :, P:].T
    ep[:, ECOLS["w2r"][0]:ECOLS["w2r"][1]] = t.reshape(P, -1)
    ep[:, ECOLS["ii"][0]:ECOLS["ii"][1]] = np.concatenate([np.eye(C, dtype=f32)] * 2)

    pq = np.arange(P)
    bfc = np.zeros((P, 3 * P + B * NPAIR * P), f32)
    bfc[:, 0:P] = np.where(pq[None, :] <= pq[:, None], 0.0, NEG)
    bfc[:, P:2 * P] = np.where(pq[None, :] >= pq[:, None], 0.0, NEG)
    bfc[:, 2 * P:3 * P] = np.eye(P)
    for b in range(B):
        for pr in range(NPAIR):
            for k in range(2):
                for pc in range(3):
                    c0 = 3 * P + (b * NPAIR + pr) * P + 64 * k
                    bfc[32 * pc + b * NE + 2 * pr + k, c0:c0 + 64] = 1.0
    bfc = bfc.astype(ml_dtypes.bfloat16)

    idx = np.ascontiguousarray(a["x"].reshape(B, NT, P).transpose(2, 1, 0).reshape(P, NT * B))
    arrays = {"idx": idx, "emb": np.ascontiguousarray(a["L0_tok_W"]), "pe": positions(), "wpack": wp, "rpack": rp,
              "epack": ep, "ident": np.eye(P, dtype=f32), "bfc": bfc, "rope": rope_tables(), "tm": tm, "tu": tu, "tk": tk}

    nc = _bacc.Bacc("TRN2", target_bir_lowering=False, num_devices=1)
    args = {n: nc.dram_tensor(n, v.shape, mybir.dt.from_np(v.dtype), kind="ExternalInput").ap() for n, v in arrays.items()}
    args["scr_q"] = nc.dram_tensor("scr_q", (3, P, N), BF16, kind="Internal").ap()
    args["scr_k"] = nc.dram_tensor("scr_k", (3, 64, N), BF16, kind="Internal").ap()
    args["out"] = nc.dram_tensor("out", (P, NT * B * C), F32, kind="ExternalOutput").ap()
    build(nc, **args)
    r = _run(nc, [arrays], core_ids=[0])
    o = r.results[0]["out"]
    return np.ascontiguousarray(np.asarray(o).reshape(P, NT, B, C).transpose(2, 1, 0, 3).reshape(B, N, C))
```

```python
from contextlib import ExitStack

import numpy as np
import concourse.bass as bass
from concourse import mybir

F32 = mybir.dt.float32
F32R = mybir.dt.float32r
BF16 = mybir.dt.bfloat16
I32 = mybir.dt.int32
ALU = mybir.AluOpType
ACT = mybir.ActivationFunctionType
AXX = mybir.AxisListType.X

P = 128
B, N, C = 2, 1024, 64
NT = N // P
H1 = 8
NH, NKV, HD = 4, 2, 16
NE, HID = 8, 170
NPAIR = NE // 2
REM = HID - P
D1 = 192
R = 8
LAYERS = 3
L = N // 2
NB = N // L
NW = 3
WINDOW = {(0, 0): 0, (0, 1): 1, (1, 0): 2, (1, 1): 0}
NU = L // 2 // P
NM = L // P
NK = L // P
EARLY_AF = 7
GR = R + 1
NEG = -1.0e30
TERMS_Q = [0, 0, 0, 1, 1, 2]
TERMS_K = [0, 1, 2, 0, 1, 0]
MROW = 16 * len(TERMS_Q)
KROWS = MROW + 3
TOPK_OFF = float(NE)
LAG = 4
GSLOTS = LAG + 1
ALL_PAIRS = 4 * NPAIR
DOWNS = [[] if n < LAG else [m for m in range(2 * (n - LAG) - 1, 2 * (n - LAG) + 1) if 0 <= m < n] if n < 2 * LAG
         else [n - 1] for n in range(ALL_PAIRS)]
DOWNS[-1].append(ALL_PAIRS - 1)
assert sum(DOWNS, []) == list(range(ALL_PAIRS))
ROW_CHUNKS = [(hh, i, c) for hh in range(NH) for i in range(NT) for c in range(i // 4 + 1)]
EARLY = 12
WIDE = len(ROW_CHUNKS) + EARLY


def row_bank(n):
    return n % 6 if n < WIDE else n % 2


def row_free(n):
    return n - 5 if n < WIDE + 2 else n - 1


def col_heads(j):
    return [(hh,) for hh in range(NH)] if j < 4 else [(0, 1), (2, 3)]


COL_STEPS = [(j, heads) for j in range(NT) for heads in col_heads(j)]


def col_steps(b, j):
    return b * len(COL_STEPS) + sum(len(col_heads(i)) for i in range(j + 1))

WCOLS = {}
_at = 0
for _n, _w in (("q1", P), ("kv1", 2 * P), ("proj1", P), ("q2", P), ("q2r", P), ("k2", 64), ("k2r", 64), ("v2", 64),
               ("wo2", P), ("v3", 2 * D1), ("u3", 2 * D1), ("o3", 3 * P), ("t3", P), ("w4", P),
               ("bproj", P), ("ub", 2 * D1), ("vb", 2 * D1), ("ob", P), ("tb", P), ("b4", P), ("ln2", P),
               ("ln1", 1), ("mask_c", P), ("mask_k", 16), ("eidx", P), ("enum", P)):
    WCOLS[_n] = (_at, _at + _w)
    _at += _w
WTOT = _at
RCOLS = {}
_at = 0
for _n, _w in (("lag", 2 * P), ("ones", P), ("l0", P), ("l1", P), ("l2", P), ("pw", 1), ("pb", 1), ("b0", 1), ("b1", 1),
               ("b2", 1), ("outw", NW * D1), ("alt", NM * 2)):
    RCOLS[_n] = (_at, _at + _w)
    _at += _w
RTOT = _at
ECOLS = {}
_at = 0
for _n, _w in (("w1", 12 * P), ("w3", 12 * P), ("rt", 8), ("w2m", NE * 64), ("w2r", NPAIR * P), ("ii", 64)):
    ECOLS[_n] = (_at, _at + _w)
    _at += _w
ETOT = _at
NSPLIT = ECOLS["rt"][1]


def spread(v, dim, n):
    v = v.unsqueeze(dim)
    shape = list(v.shape)
    shape[dim] = n
    return v.broadcast_to(shape)


def build(nc, idx, emb, pe, wpack, rpack, epack, ident, bfc, rope, tm, tu, tk, scr_q, scr_k, out):
    with ExitStack() as ctx:
        def sb(name, shape, dt=F32):
            return ctx.enter_context(nc.sbuf_tensor(name, shape, dt))

        def sem(name):
            return ctx.enter_context(nc.semaphore(name))

        ps = ctx.enter_context(nc.psum_tensor("ps", [P, 8, 512], F32))

        idx_s = sb("idx_s", [P, NT * B], I32)
        w = sb("w", [P, WTOT])
        rp = sb("rp", [P, RTOT])
        ew = sb("ew", [P, ETOT - NSPLIT])
        idt = sb("idt", [P, P])
        bfc_s = sb("bfc_s", [P, 3 * P + B * NPAIR * P], BF16)
        arena = sb("arena", [P, 2 * NT * N])
        tu_s = sb("tu_s", [P, 2, NU, L])
        tk_s = sb("tk_s", [P, 2, NK, L // 2])
        h = sb("h", [P, NT, B, C])
        xc = sb("xc", [P, NT, B, C])
        sq = sb("sq", [P, NT, B, C])
        x1 = sb("x1", [P, NT, B, C])
        xT = sb("xT", [P, N])
        st = sb("st", [P, 12, NT * B])
        rw = sb("rw", [P, 8, NT * B * NE])

        def W(name, lo=0, hi=None):
            a, b = WCOLS[name]
            return w[:, a + lo:(b if hi is None else a + hi)]

        def RP(name):
            a, b = RCOLS[name]
            return rp[:, a:b]

        def E(name, lo=0, hi=None):
            a, b = ECOLS[name]
            return ew[:, a - NSPLIT + lo:(b if hi is None else a + hi) - NSPLIT]

        def EP(piece, name, lo, hi):
            a = ECOLS[name][0]
            return piece[:, a + lo:a + hi]

        mask_ts, mask_st, ident_b = bfc_s[:, 0:P], bfc_s[:, P:2 * P], bfc_s[:, 2 * P:3 * P]

        def selw(b, pr):
            a = 3 * P + (b * NPAIR + pr) * P
            return bfc_s[:, a:a + P]

        def plan(region, *parts):
            at, views = 0, []
            for shape, dt in parts:
                cols = int(np.prod(shape)) // (2 if dt == BF16 else 1)
                v = region[:, at:at + cols]
                at += cols
                v = v if dt == F32 else v.bitcast(dt)
                names = ["a", "b", "c", "d"][:len(shape)]
                if len(shape) > 1:
                    v = v.rearrange("p (%s) -> p %s" % (" ".join(names), " ".join(names)),
                                    **dict(zip(names[1:], shape[1:])))
                views.append(v)
            assert at <= region.shape[1], (at, region.shape)
            return views

        qst, kst, yT, pt = plan(arena, ([B * NH, N], BF16), ([B * NKV, N], BF16), ([B, N], F32), ([2, NH, N], F32))
        _, _, _, pieces_q, pieces_k, e_raw = plan(arena, ([B * NH, N], BF16), ([B * NKV, N], BF16), ([B, N], F32),
                                                  ([3, N], BF16), ([3, N], BF16), ([NSPLIT], F32))
        _, _, rope_s, tm_s = plan(arena, ([B * NH, N], BF16), ([B * NKV, N], BF16), ([2, N], F32), ([2, NM, L], F32))
        fhl, sil, gh, wb, zp_ = plan(arena, ([NT, B, P], F32), ([2, 512], F32), ([GSLOTS, 3, 512], F32),
                                     ([2, 512], F32), ([2, 512], F32))
        fhl = fhl.rearrange("p j b (q c) -> p j b q c", q=2)
        zacc = (xc[:].rearrange("p j b c -> p (j b c)"), sq[:].rearrange("p j b c -> p (j b c)"))
        us, vs, osp, prd = plan(arena, ([NT, 384], F32), ([NT, 384], F32), ([NB * NK, 2, 384], F32), ([4, 2, 384], F32))
        _, yT3 = plan(arena, ([NT, 384], F32), ([NT, 3, P], F32))

        gt2 = sb("gt2", [P, P])
        af = sb("af", [P, NK, 2, NW, D1])
        afx = sb("afx", [P, 2, NW, D1])
        cbd = sb("cbd", [P, 144])
        tmp = sb("tmp", [P, N])
        va2 = sb("va2", [P, NT, B, NKV, 32])
        mrow = sb("mrow", [32, 3, P], BF16)
        mtmp = sb("mtmp", [32, P])
        wpc = sb("wpc", [P, NT, 3, 32], BF16)
        unused = sb("unused", [1, 16])
        wst = sb("wst", [P, N], BF16)
        with ExitStack() as experts:
            e_hi, e_lo, xs = (experts.enter_context(nc.sbuf_tensor(n, sh, F32R)) for n, sh in (
                ("e_hi", [P, NSPLIT]), ("e_lo", [P, NSPLIT]), ("xs", [P, B, N])))
        share = sb("share", [P, 2 * NSPLIT + B * N])
        pe_s, va1, kf1, qf1, qr, kr_, gt, rh, geo = plan(
            share, ([NT, C], F32), ([NT, 132], F32), ([NT, B, C], F32), ([N], F32), ([N], F32), ([N], F32),
            ([2, L], F32), ([4, 2 * P], F32), ([2, NM, 32], F32))
        kr = kr_[0:64]
        veo, y3, ssum = plan(share, ([2, NB, NU, 384], F32), ([2, 384], F32), ([2 * NB, 2, 384], F32))
        ld_idx, ld_pe, ld_rp, ld_id, ld_w, ld_bf, ld_rope, ld_m, ld_e, ld_u, ld_k = (
            sem(n) for n in ("ld_idx", "ld_pe", "ld_rp", "ld_id", "ld_w", "ld_bf", "ld_rope", "ld_m", "ld_e", "ld_u", "ld_k"))
        gathered = sem("gathered")
        dve_chain, act_chain, pool_chain = sem("dve_chain"), sem("act_chain"), sem("pool_chain")

        names = {}

        def S(name):
            if name not in names:
                names[name] = sem(name)
            return names[name]

        def mm(o, l, r, start=True, stop=True, **kw):
            return nc.tensor.matmul(o, l, r, start=start, stop=stop, **kw)

        block = ctx.enter_context(nc.Block())

        @block.sync
        def _(sp):
            sp.dma_start(idx_s[:], idx).then_inc(ld_idx, 16)
            sp.dma_start(rp[:], rpack).then_inc(ld_rp, 16)
            sp.dma_start(idt[:], ident).then_inc(ld_id, 16)
            sp.dma_start(pe_s[:], pe).then_inc(ld_pe, 16)
            sp.dma_start(w[:], wpack).then_inc(ld_w, 16)
            sp.dma_start(rope_s[:], rope).then_inc(ld_rope, 16)
            sp.dma_start(bfc_s[:], bfc).then_inc(ld_bf, 16)
            sp.wait_ge(gathered, 16 * NT * B)
            for s in range(2):
                sp.dma_start(tm_s[:, s], tm[s]).then_inc(ld_m, 16)
            sp.dma_start(ew[:], epack[:, NSPLIT:ETOT]).then_inc(ld_e, 16)
            sp.wait_ge(S("gf"), 3)
            sp.dma_start(e_raw, epack[:, 0:NSPLIT]).then_inc(ld_e, 16)
            sp.wait_ge(S("k_pieces"), 1)
            sp.dma_start(scr_q.rearrange("s p t -> p s t"), pieces_q).then_inc(S("scr_q_written"), 16)
            sp.wait_ge(S("k_pieces"), 2)
            sp.dma_start(scr_k.rearrange("s p t -> p s t"), pieces_k[0:64]).then_inc(S("scr_k_written"), 16)
            sp.wait_ge(S("scr_q_written"), 16)
            for n, pc in enumerate(TERMS_Q):
                sp.dma_start(qst[16 * n:16 * n + 16], scr_q[pc].rearrange("(g d) t -> d g t", d=HD)).then_inc(S("stacks"), 16)
            sp.wait_ge(S("scr_k_written"), 16)
            for n, pc in enumerate(TERMS_K):
                sp.dma_start(kst[16 * n:16 * n + 16], scr_k[pc].rearrange("(g d) t -> d g t", d=HD)).then_inc(S("stacks"), 16)
            for s in range(2):
                sp.dma_start(tu_s[:, s], tu[s]).then_inc(ld_u, 16)
            for s in range(2):
                sp.dma_start(tk_s[:, s], tk[s]).then_inc(ld_k, 16)
            for b in range(B):
                sp.wait_ge(S("max_pieces"), b + 1)
                for pc in range(3):
                    sp.dma_start(qst[MROW + pc:MROW + pc + 1, b * NH:(b + 1) * NH, :],
                                 mrow[:, pc, :]).then_inc(S("max_rows"), 16)
            sp.wait_ge(S("final"), 1)
            sp.dma_start(out, sq[:].rearrange("p j b c -> p (j b c)")).then_inc(S("stored"), 16)
            sp.wait_ge(S("stored"), 16)

        @block.gpsimd
        def _(pool):
            def step(ins):
                chain[0] += 1
                ins.then_inc(pool_chain, 1)
                pool.wait_ge(pool_chain, chain[0])

            chain = [0]
            pool.wait_ge(ld_idx, 16)
            for j in range(NT):
                for b in range(B):
                    n = j * B + b
                    nc.gpsimd.indirect_dma_start(
                        xc[:, j, b, :], None, emb,
                        bass.IndirectOffsetOnAxis(ap=idx_s[:, n:n + 1], axis=0)).then_inc(gathered, 16)
            nc.gpsimd.memset(geo[:], 0.0).then_inc(S("geo_zero"), 1)
            pool.wait_ge(S("geo_zero"), 1)
            nc.gpsimd.memset(geo[:, 0, :, 0:NW * GR].rearrange("p q (d n) -> p q d n", n=GR)[:, :, :, R], 2.0).then_inc(S("geo_ones"), 1)
            nc.gpsimd.memset(va1[:, :, P:P + 1], 1.0).then_inc(S("va1_ones"), 1)
            nc.gpsimd.memset(va2[:], 0.0).then_inc(S("va2_zero"), 1)
            pool.wait_ge(S("va2_zero"), 1)
            nc.gpsimd.memset(va2[:, :, :, :, HD:HD + 1], 1.0).then_inc(S("va2_ones"), 1)
            nc.gpsimd.memset(wst[:], 0.0).then_inc(S("wst_zero"), 1)
            pool.wait_ge(S("wst_zero"), 1)
            nc.gpsimd.memset(wpc[:], 0.0).then_inc(S("wpc_zero"), 1)
            pool.wait_ge(S("wpc_zero"), 1)
            nc.gpsimd.memset(kst[MROW:KROWS], 1.0).then_inc(S("k_ones"), 1)
            for t in range(4):
                b, hf = t // 2, t % 2
                for pr in range(NPAIR):
                    n = t * NPAIR + pr
                    pool.wait_ge(S("zpair"), n + 1)
                    z = zacc[b][:, hf * 512:(hf + 1) * 512]
                    if pr == 0:
                        nc.gpsimd.tensor_copy(z, zp_[:, n % 2, :]).then_inc(S("zsum"), 1)
                    else:
                        pool.wait_ge(S("zsum"), n)
                        nc.gpsimd.tensor_tensor(z, z, zp_[:, n % 2, :], ALU.add).then_inc(S("zsum"), 1)
            pool.wait_ge(S("uv_silu"), NT)
            nc.gpsimd.tensor_tensor(veo[:, 1, 1], vs[:, 4:6], vs[:, 6:8], ALU.subtract).then_inc(S("odd"), 1)
            for n in range(NB * NK):
                kt, i = n // NB, n % NB
                for o in range(NB):
                    q = NB * n + o
                    pool.wait_ge(S("prd"), q + 1)
                    if i == 0:
                        dst = osp[:, o * NK + kt]
                    else:
                        dst = ssum[:, (kt % 2) * NB + o]
                        if kt >= 2:
                            pool.wait_ge(S("spectra"), NB * (kt - 2) + o + 1)
                    p1, p2 = prd[:, 2 * (q % 2)], prd[:, 2 * (q % 2) + 1]
                    nc.gpsimd.tensor_tensor(dst[:, 0], p1[:, 0], p1[:, 1], ALU.subtract).then_inc(S("part"), 1)
                    nc.gpsimd.tensor_tensor(dst[:, 1], p2[:, 0], p2[:, 1], ALU.add).then_inc(S("part"), 1)

        @block.tensor
        def _(pe):
            def transposes(src, banks, ready, value, done):
                pe.wait_ge(ready, value)
                for j in range(NT):
                    ins = nc.tensor.transpose(ps[:, banks + j // 4, (j % 4) * P:(j % 4 + 1) * P],
                                              src[:, j].rearrange("p b c -> p (b c)"), idt[:])
                    if j % 4 == 3:
                        ins.then_inc(done, 1)

            pe.wait_ge(ld_rp, 16)
            pe.wait_ge(ld_id, 16)
            for i in range(LAYERS + 1):
                pe.wait_ge(S("r_sq"), i + 1)
                mm(ps[:, 0, 0:2 * P], RP("ones"), rh[:, 1]).then_inc(S("r_ss"), 1)
                if i < LAYERS:
                    pe.wait_ge(S("r_act"), i + 1)
                    mm(ps[:, 1, 0:2 * P], RP("l%d" % i), rh[:, 3]).then_inc(S("r_lin"), 1)
            transposes(sq, 2, S("n1"), 1, S("T1"))
            pe.wait_ge(ld_w, 16)
            pe.wait_ge(S("xT1"), 2)
            for c in range(2):
                mm(ps[:, 4 + c], W("q1"), xT[:, c * 512:(c + 1) * 512]).then_inc(S("q1"), 1)
            pe.wait_ge(S("r_act"), LAYERS + 1)
            nc.tensor.transpose(ps[:, 7, 0:P], rh[:, 3, 0:P], idt[:])
            nc.tensor.transpose(ps[:, 7, P:2 * P], rh[:, 3, P:2 * P], idt[:]).then_inc(S("r_T"), 1)
            KVB = (0, 1, 2, 3)
            for j in range(NT):
                mm(ps[:, KVB[j // 2], (j % 2) * 256:(j % 2 + 1) * 256], xT[:, j * P:(j + 1) * P], W("kv1")).then_inc(S("kv1"), 1)
            pe.wait_ge(S("kf1"), 1)
            pe.wait_ge(S("va1"), 1)
            pe.wait_ge(S("va1_ones"), 1)
            for j in range(NT):
                ins = mm(ps[:, 6, 0:P + 1], kf1[:, j].rearrange("p b c -> p (b c)"), va1[:, j, 0:P + 1],
                         start=(j == 0), stop=(j == NT - 1))
            ins.then_inc(S("ctx1"), 1)
            pe.wait_ge(S("cbd"), 2)
            pe.wait_ge(S("qf1"), 1)
            for j in range(NT):
                ins = mm(ps[:, j // 2, (j % 2) * 256:(j % 2) * 256 + 144], qf1[:, j * P:(j + 1) * P], cbd[:])
            ins.then_inc(S("nd1"), 1)
            transposes(sq, 4, S("attn1"), 1, S("T1b"))
            pe.wait_ge(S("xT1b"), 2)
            for j in range(NT):
                ins = mm(ps[:, j // 4, (j % 4) * P:(j % 4 + 1) * P], xT[:, j * P:(j + 1) * P], W("proj1"))
            ins.then_inc(S("o1"), 1)
            pe.wait_ge(ld_m, 32)
            pe.wait_ge(S("geo_done"), 2 * NW)
            pe.wait_ge(S("xT1b"), 2)
            for s in range(2):
                for q in range(NM):
                    ins = mm(ps[32 * q:32 * q + 32, 4 + s], geo[:, s, q, :], tm_s[:, s, q, :], tile_position=(0, 32 * q))
                ins.then_inc(S("gf"), 1)
            for q in range(NM):
                a = RCOLS["alt"][0] + 2 * q
                ins = mm(ps[32 * q:32 * q + 32, 6, 0:2], geo[:, 0, q, :], rp[:, a:a + 2], tile_position=(0, 32 * q))
            ins.then_inc(S("gf"), 1)
            pe.wait_ge(S("gt_done"), 4)

            def transfer(n, bank):
                lhs = gt2[:] if n == 2 * NK else gt[:, 1 - n % 2, n // 2 * P:(n // 2 + 1) * P]
                for x in range(2):
                    ins = mm(ps[:, bank + x, 0:288], lhs, RP("outw")[:, x * 288:(x + 1) * 288])
                ins.then_inc(S("afp"), 1)

            for n in range(EARLY_AF):
                if n >= 3:
                    pe.wait_ge(S("af_done"), n - 2)
                transfer(n, (2, 6, 4)[n % 3])
            pe.wait_ge(S("af_done"), EARLY_AF)
            transposes(sq, 2, S("n2"), 1, S("T2"))
            pe.wait_ge(S("xT2"), 2)
            for name, bank, rows in (("q2", 4, P), ("q2r", 6, P), ("k2", 0, 64), ("k2r", 2, 64)):
                for c in range(2):
                    ins = mm(ps[0:rows, bank + c], W(name), xT[:, c * 512:(c + 1) * 512])
                ins.then_inc(S("qk2"), 1)
            pe.wait_ge(S("qrot"), 1)
            for j in range(NT):
                ins = mm(ps[:, 4, j * 64:(j + 1) * 64], xT[:, j * P:(j + 1) * P], W("v2"))
            ins.then_inc(S("v2"), 1)
            pe.wait_ge(S("krot"), 1)
            for n in range(EARLY_AF, 2 * NK + 1):
                transfer(n, 2 * (n - EARLY_AF))
            pe.wait_ge(S("stacks"), 12 * 16)
            pe.wait_ge(S("k_ones"), 1)
            pe.wait_ge(S("af_done"), 2 * NK + 2)
            pe.wait_ge(ld_bf, 16)

            def score_rows(b, n):
                hh, i, c = ROW_CHUNKS[n]
                n += b * len(ROW_CHUNKS)
                if n >= 6:
                    pe.wait_ge(S("max_read"), row_free(n))
                bank = row_bank(n)
                wd = min(512, (i + 1) * P - c * 512)
                last = c == i // 4
                ins = mm(ps[:, bank, 0:wd], qst[0:MROW, b * NH + hh, i * P:(i + 1) * P],
                         kst[0:MROW, b * NKV + hh // 2, c * 512:c * 512 + wd], start=True, stop=not last)
                if last:
                    ins = mm(ps[:, bank, wd - P:wd], ident_b, mask_ts, start=False, stop=True)
                ins.then_inc(S("rows"), 1)

            def score_cols(b, step_n):
                j, heads = COL_STEPS[step_n]
                n = b * len(COL_STEPS) + step_n
                if n < 2:
                    pe.wait_ge(S("max_read"), WIDE - 2 + 2 * n)
                else:
                    pe.wait_ge(S("exp_done"), n - 1)
                bank = 2 + 2 * (n % 2)
                for x in range(2):
                    c, hh = (x, heads[0]) if len(heads) == 1 else (1, heads[x])
                    lo = max(j * P, c * 512)
                    diag = lo == j * P
                    ins = mm(ps[:, bank + x, lo - c * 512:512], kst[0:KROWS, b * NKV + hh // 2, j * P:(j + 1) * P],
                             qst[0:KROWS, b * NH + hh, lo:(c + 1) * 512], start=True, stop=not diag)
                    if diag:
                        ins = mm(ps[:, bank + x, lo - c * 512:lo - c * 512 + P], ident_b, mask_st, start=False, stop=True)
                ins.then_inc(S("cols"), 1)

            def weighted(b, j, c):
                if c < j // 4:
                    return
                pe.wait_ge(S("exp_done"), col_steps(b, j))
                if b == 1 and j == 0:
                    pe.wait_ge(S("yT0"), 2)
                lo = max(j * P, c * 512)
                for hh in range(NH):
                    ins = mm(ps[32 * hh:32 * hh + 32, 6 + c, lo - c * 512:512], va2[:, j, b, hh // 2, :],
                             pt[:, j % 2, hh, lo:(c + 1) * 512], start=(j == 0), stop=(j == 4 * c + 3),
                             tile_position=(0, 32 * hh))
                if c == 1:
                    ins.then_inc(S("pv"), 1)

            def y_transposes(b, bank):
                pe.wait_ge(S("yT%d" % b), 2)
                for j in range(NT):
                    ins = nc.tensor.transpose(ps[:, bank + j // 4, (j % 4) * P:(j % 4 + 1) * P], yT[:, b, j * P:(j + 1) * P], idt[:])
                ins.then_inc(S("yTT"), 1)

            for n in range(len(ROW_CHUNKS)):
                score_rows(0, n)
            for n in range(EARLY // 2):
                score_rows(1, n)
            pe.wait_ge(S("max_all"), 1)
            nc.tensor.transpose(ps[0:32, 6, 0:P], rw[:, 0, 0:32], idt[:]).then_inc(S("maxT"), 1)
            for n in range(EARLY // 2, EARLY):
                score_rows(1, n)
            todo = list(range(EARLY, len(ROW_CHUNKS)))
            pe.wait_ge(S("max_rows"), 48)
            pe.wait_ge(S("va2"), 1)
            for b in range(B):
                for n, (j, heads) in enumerate(COL_STEPS):
                    score_cols(b, n)
                    for _ in range(min(2, len(todo))):
                        score_rows(1, todo.pop(0))
                    if b == 0 and n == len(COL_STEPS) - 2:
                        pe.wait_ge(S("max_all"), 2)
                        nc.tensor.transpose(ps[0:32, 0, 0:P], rw[:, 1, 0:32], idt[:]).then_inc(S("maxT"), 1)
                    if j >= 1 and heads[-1] == 1:
                        weighted(b, j - 1, 0)
                    if j >= 1 and heads[-1] == 3:
                        weighted(b, j - 1, 1)
                    if b == 1 and j == 1 and heads[-1] == 3:
                        pe.wait_ge(S("max_pieces"), 2)
                        y_transposes(0, 0)
                weighted(b, NT - 1, 1)
                if b == 0:
                    pe.wait_ge(S("max_rows"), 96)
            y_transposes(1, 2)
            transposes(sq, 4, S("yn"), 2, S("T2b"))
            pe.wait_ge(S("xT2b"), 2)
            for j in range(NT):
                ins = mm(ps[:, j // 4, (j % 4) * P:(j % 4 + 1) * P], xT[:, j * P:(j + 1) * P], W("wo2"))
            ins.then_inc(S("o2"), 1)
            pe.wait_ge(S("fhl"), 2)
            for b in range(B):
                for j in range(NT):
                    ins = nc.tensor.transpose(ps[:, 2 + 2 * b + j // 4, (j % 4) * P:(j % 4 + 1) * P],
                                              fhl[:, j, b].rearrange("p q c -> p (q c)"), idt[:])
                    if j % 4 == 3:
                        ins.then_inc(S("Te"), 1)
            pe.wait_ge(S("e_split"), 2)
            for b in range(B):
                pe.wait_ge(S("xs%d" % b), 2)
                for j in range(NT):
                    o = ps[:, 6, (j * B + b) * 8:(j * B + b + 1) * 8]
                    mm(o, xs[:, b, j * P:(j + 1) * P], EP(e_hi, "rt", 0, 8), start=True, stop=False)
                    ins = mm(o, xs[:, b, j * P:(j + 1) * P], EP(e_lo, "rt", 0, 8), start=False, stop=True)
            ins.then_inc(S("logits"), 1)
            u_at = [0]
            z_at = [0]

            def up(t, pr, n3):
                b, hf = t // 2, t % 2
                n = u_at[0]
                u_at[0] += 1
                if n >= 3:
                    pe.wait_ge(S("gated"), n - 2)
                rhs = xs[:, b, hf * 512:(hf + 1) * 512]
                tile = 3 * pr + n3
                for m, name in enumerate(("w1", "w3")):
                    o = ps[:, 2 * (n % 3) + m]
                    mm(o, EP(e_hi, name, tile * P, (tile + 1) * P), rhs, start=True, stop=False)
                    ins = mm(o, EP(e_lo, name, tile * P, (tile + 1) * P), rhs, start=False, stop=True)
                ins.then_inc(S("up"), 1)

            def down(t, pr):
                n = t * NPAIR + pr
                b, hf = t // 2, t % 2
                if n == 0:
                    pe.wait_ge(S("wst"), 1)
                if n >= 1:
                    pe.wait_ge(S("zpair"), n)
                mm(ps[:, 7], selw(b, pr), wst[:, hf * 512:(hf + 1) * 512]).then_inc(S("wbp"), 1)
                pe.wait_ge(S("gated"), 3 * (n + 1))
                o = ps[:, 6]
                for k in range(2):
                    e = 2 * pr + k
                    mm(o[64 * k:64 * k + 64], E("w2m", e * 64, (e + 1) * 64), gh[:, n % GSLOTS, k, :], start=True, stop=False,
                       tile_position=(0, 64 * k), skip_group_check=True)
                mm(o, E("w2r", pr * P, (pr + 1) * P), gh[:, n % GSLOTS, 2, :], start=False, stop=True,
                   skip_group_check=True).then_inc(S("down"), 1)

            order = [(t, pr) for t in range(4) for pr in range(NPAIR)]
            for n, (t, pr) in enumerate(order):
                downs = list(DOWNS[n])
                for n3 in range(3):
                    up(t, pr, n3)
                if n == LAG - 1:
                    pe.wait_ge(S("wpc"), 3)
                    for j in range(NT):
                        ins = mm(ps[0:96, 6 + j // 4, (j % 4) * P:(j % 4 + 1) * P], wpc[:, j].rearrange("p q e -> p (q e)"), ident_b)
                    ins.then_inc(S("wT"), 1)
                for m in downs:
                    down(*order[m])
            pe.wait_ge(S("zsum"), 4 * NPAIR)
            pe.wait_ge(S("gated"), 48)
            for j in range(NT):
                for b in range(B):
                    ins = mm(ps[:, j // 4, (j % 4) * P + b * 64:(j % 4) * P + b * 64 + 64], zacc[b][:, j * P:(j + 1) * P], E("ii"))
            ins.then_inc(S("moe"), 1)
            transposes(x1, 2, S("n3"), 1, S("T3"))
            pe.wait_ge(S("xT3"), 4)

            def uv(n):
                tile = n % NT
                at = (tile // 4) * L + (1 - tile // 2 % 2) * (L // 2) + tile % 2 * P
                bank = 4 + n % 4 if n < NT else tile
                mm(ps[:, bank, 0:384], xT[:, at:at + P], W(("v3", "u3")[n // NT])).then_inc(S("uv"), 1)

            for n in range(2 * NT):
                if 4 <= n < NT:
                    pe.wait_ge(S("uv_read"), n - 3)
                if n == NT:
                    pe.wait_ge(S("T3_read"), 1)
                if n >= NT + 4:
                    pe.wait_ge(S("uv_read"), n - 7)
                uv(n)
            pe.wait_ge(ld_u, 32)
            for n in range(NB * NK):
                kt, i = n // NB, n % NB
                if n < 4:
                    pe.wait_ge(S("uv_read"), NT + 2 * n + 2)
                if n == 0:
                    pe.wait_ge(S("even"), 2)
                if n == 1:
                    pe.wait_ge(S("even"), 3)
                    pe.wait_ge(S("odd"), 1)
                if n >= 4:
                    pe.wait_ge(S("spec_read"), n - 3)
                for s in range(2):
                    for u in range(NU):
                        ins = mm(ps[:, 2 * (n % 4) + s, 0:384], tu_s[:, s, u, kt * P:(kt + 1) * P], veo[:, s, i, u, :],
                                 start=(u == 0), stop=(u == NU - 1))
                ins.then_inc(S("spec"), 1)
            pe.wait_ge(ld_k, 32)
            pe.wait_ge(S("spec_read"), NB * NK)

            def back_transposes(unit):
                for k in range(2):
                    n = 2 * unit + k
                    pe.wait_ge(S("y3"), n + 1)
                    if n >= 2:
                        pe.wait_ge(S("yT3"), n - 1)
                    for c in range(3):
                        ins = nc.tensor.transpose(ps[:, n % 2, c * P:(c + 1) * P],
                                                  y3[:, n % 2, c * P:(c + 1) * P], idt[:])
                    ins.then_inc(S("yTp"), 1)

            def output_projection(blk):
                pe.wait_ge(S("yT3"), 2 * NU * (blk + 1))
                for jj in range(4):
                    n = 2 * (2 * blk + jj - 2) if jj >= 2 else 2 * (2 * blk + 1 - jj) + 1
                    for c in range(3):
                        ins = mm(ps[:, 2 + blk, jj * P:(jj + 1) * P], yT3[:, n, c, :], W("o3", c * P, (c + 1) * P),
                                 start=(c == 0), stop=(c == 2))
                ins.then_inc(S("o3"), 1)

            for unit in range(NB * NU):
                blk, u = unit // NU, unit % NU
                pe.wait_ge(S("spectra"), NB * (NK - 1) + blk + 1)
                if unit >= 2:
                    pe.wait_ge(S("inv_read"), unit - 1)
                for s in range(2):
                    for kt in range(NK):
                        ins = mm(ps[:, 4 + 2 * (unit % 2) + s, 0:384], tk_s[:, s, kt, u * P:(u + 1) * P],
                                 osp[:, blk * NK + kt, s], start=(kt == 0), stop=(kt == NK - 1))
                ins.then_inc(S("inv"), 1)
                if unit >= 1:
                    back_transposes(unit - 1)
            output_projection(0)
            back_transposes(NB * NU - 1)
            output_projection(1)
            transposes(xc, 4, S("d3"), 1, S("T3b"))
            pe.wait_ge(S("xT3b"), 2)
            for j in range(NT):
                ins = mm(ps[:, j // 4, (j % 4) * P:(j % 4 + 1) * P], xT[:, j * P:(j + 1) * P], W("t3"))
            ins.then_inc(S("t3"), 1)
            transposes(sq, 2, S("n4"), 1, S("T4"))
            pe.wait_ge(S("xT4"), 2)
            for j in range(NT):
                ins = mm(ps[:, 4 + j // 4, (j % 4) * P:(j % 4 + 1) * P], xT[:, j * P:(j + 1) * P], W("w4"))
            ins.then_inc(S("o4"), 1)

        xn_view = sq
        @block.scalar
        def _(act):
            chain = [0]

            def step(ins):
                chain[0] += 1
                ins.then_inc(act_chain, 1)
                act.wait_ge(act_chain, chain[0])

            def evac(bank, done_wait, value, out_sem, scale=None):
                act.wait_ge(done_wait, value)
                if scale is None:
                    nc.scalar.copy(xT[:, 0:512], ps[:, bank]).then_inc(out_sem, 1)
                else:
                    nc.scalar.activation(xT[:, 0:512], ps[:, bank], ACT.Copy, scale=scale).then_inc(out_sem, 1)

            loads = [0]

            def next_function(func):
                nc.scalar.activation(unused[:, loads[0]:loads[0] + 1], idt[0:1, 0:1], func).then_inc(S("tables"), 1)
                loads[0] += 1

            act.wait_ge(ld_id, 16)
            next_function(ACT.Sqrt)
            act.wait_ge(ld_rp, 16)
            nc.scalar.activation(rh[:, 0], RP("lag"), ACT.Identity, scale=RP("pw"), bias=RP("pb")).then_inc(S("r_h"), 1)
            for i in range(LAYERS):
                act.wait_ge(S("r_ss"), i + 1)
                if i >= 1:
                    act.wait_ge(S("r_act"), i)
                nc.scalar.activation(rh[:, 2], ps[:, 0, 0:2 * P], ACT.Sqrt, scale=1.0 / R).then_inc(S("r_rms"), 1)
                act.wait_ge(S("r_lin"), i + 1)
                nc.scalar.activation(rh[:, 0], ps[:, 1, 0:2 * P], ACT.Identity, bias=RP("b%d" % i)).then_inc(S("r_h"), 1)
            act.wait_ge(S("var1"), 1)
            nc.scalar.activation(st[:, 3], st[:, 2], ACT.Sqrt).then_inc(S("std1"), 1)
            act.wait_ge(S("r_ss"), LAYERS + 1)
            nc.scalar.activation(rh[:, 2], ps[:, 0, 0:2 * P], ACT.Sqrt, scale=1.0 / R).then_inc(S("r_rms"), 1)
            next_function(ACT.Exp)
            evac(2, S("T1"), 1, S("xT1"))
            act.wait_ge(S("qmin"), 1)
            nc.scalar.activation(qf1[:], tmp[:], ACT.Exp).then_inc(S("qexp"), 1)
            act.wait_ge(S("kmin"), 1)
            nc.scalar.activation(kf1[:], kf1[:], ACT.Exp).then_inc(S("kexp"), 1)
            next_function(ACT.Sqrt)
            act.wait_ge(S("kf1"), 1)
            nc.scalar.copy(va1[:, :, 0:P].rearrange("p j (b c) -> p j b c", b=B),
                           ps[:, 0:4].rearrange("p a (g b k c) -> p (a g) b k c", g=2, b=B, k=2)[:, :, :, 1, :]).then_inc(S("va1"), 1)
            evac(4, S("T1b"), 1, S("xT1b"))
            for s in range(2):
                act.wait_ge(S("gf"), s + 1)
                nc.scalar.copy(gt[:, s], ps[:, 4 + s]).then_inc(S("gt_done"), 1)
            nc.scalar.copy(gt2[:, 1:P], ps[:, 4, 1:P]).then_inc(S("gt_done"), 1)
            act.wait_ge(S("gf"), 3)
            nc.scalar.copy(gt2[:, 0:1], ps[:, 6, 0:1]).then_inc(S("gt_done"), 1)

            def af_copy(n, bank):
                act.wait_ge(S("afp"), n + 1)
                dst = afx[:, 1] if n == 2 * NK else af[:, n // 2, n % 2]
                nc.scalar.copy(dst.rearrange("p d c -> p (d c)").rearrange("p (x c) -> p x c", x=2),
                               ps[:, bank:bank + 2, 0:288]).then_inc(S("af_done"), 1)

            for n in range(EARLY_AF):
                af_copy(n, (2, 6, 4)[n % 3])
                if n == 2:
                    act.wait_ge(S("var2"), 1)
                    nc.scalar.activation(st[:, 3], st[:, 2], ACT.Sqrt).then_inc(S("std2"), 1)
                if n == 4:
                    act.wait_ge(S("msq2"), 1)
                    nc.scalar.activation(st[:, 6], st[:, 5], ACT.Sqrt).then_inc(S("rms2"), 1)
            next_function(ACT.Exp)
            evac(2, S("T2"), 1, S("xT2"), scale=W("ln1"))
            act.wait_ge(S("gf"), 3)
            act.wait_ge(S("qrot"), 2)
            nc.scalar.copy(pieces_q[:, 0], qr[:]).then_inc(S("rounded"), 1)
            act.wait_ge(S("qrot"), 3)
            nc.scalar.copy(pieces_k[0:64, 0], kr[:]).then_inc(S("rounded"), 1)
            act.wait_ge(S("rest"), 1)
            nc.scalar.copy(pieces_q[:, 1], tmp[:]).then_inc(S("rounded"), 1)
            act.wait_ge(S("rest"), 2)
            nc.scalar.copy(pieces_k[0:64, 1], qf1[0:64]).then_inc(S("rounded"), 1)
            act.wait_ge(S("v2"), 1)
            act.wait_ge(S("va2_ones"), 1)
            nc.scalar.copy(va2[:, :, :, :, 0:HD],
                           ps[:, 4].rearrange("p (j b k d) -> p j b k d", j=NT, b=B, k=NKV)).then_inc(S("va2"), 1)
            for n in range(EARLY_AF, 2 * NK + 1):
                af_copy(n, 2 * (n - EARLY_AF))
            act.wait_ge(S("af_done"), 1)
            nc.scalar.copy(afx[:, 0], af[:, 0, 0]).then_inc(S("af_done"), 1)
            for b in range(B):
                for step_n, (j, heads) in enumerate(COL_STEPS):
                    n = b * len(COL_STEPS) + step_n
                    act.wait_ge(S("cols"), n + 1)
                    if b * NT + j >= 2 and heads[0] == 0:
                        act.wait_ge(S("pv"), b * NT + j - 1)
                    bank = 2 + 2 * (n % 2)
                    if len(heads) == 1:
                        dst = pt[:, j % 2, heads[0], j * P:N]
                        src = ps[:, bank:bank + 2].rearrange("p a t -> p (a t)")[:, j * P:N]
                    else:
                        dst = pt[:, j % 2, heads[0]:heads[1] + 1, j * P:N]
                        src = ps[:, bank:bank + 2, j * P - 512:512]
                    nc.scalar.activation(dst, src, ACT.Exp, scale=HD ** -0.5).then_inc(S("exp_done"), 1)
                act.wait_ge(S("pv"), (b + 1) * NT)
                nc.scalar.copy(yT[:, b, 0:512], ps[:, 6]).then_inc(S("yT%d" % b), 1)
            next_function(ACT.Sqrt)
            evac(4, S("T2b"), 1, S("xT2b"))
            act.wait_ge(S("var2b"), 1)
            nc.scalar.activation(st[:, 3], st[:, 2], ACT.Sqrt).then_inc(S("rms2b"), 1)
            next_function(ACT.Exp)
            for b in range(B):
                act.wait_ge(S("Te"), 2 * b + 1)
                nc.scalar.copy(xs[:, b, 0:512], ps[:, 2 + 2 * b]).then_inc(S("xs%d" % b), 1)
            act.wait_ge(S("lmax"), 1)
            nc.scalar.activation(rw[:, 1], rw[:, 0], ACT.Exp).then_inc(S("lexp"), 1)
            next_function(ACT.Silu)
            for n in range(ALL_PAIRS):
                for n3 in range(3):
                    m = 3 * n + n3
                    act.wait_ge(S("up"), m + 1)
                    if m >= 2:
                        act.wait_ge(S("gated"), m - 1)
                    nc.scalar.activation(sil[:, m % 2], ps[:, 2 * (m % 3)], ACT.Silu).then_inc(S("silu"), 1)
                if n == LAG - 1:
                    act.wait_ge(S("wT"), 1)
                    act.wait_ge(S("wst_zero"), 1)
                    nc.scalar.copy(wst[0:96], ps[0:96, 6:8].rearrange("p a t -> p (a t)")).then_inc(S("wst"), 1)
                for d in DOWNS[n]:
                    act.wait_ge(S("wbp"), d + 1)
                    if d >= 2:
                        act.wait_ge(S("zpair"), d - 1)
                    nc.scalar.copy(wb[:, d % 2], ps[:, 7]).then_inc(S("wb"), 1)
            next_function(ACT.Sqrt)
            act.wait_ge(S("var3"), 1)
            nc.scalar.activation(st[:, 3], st[:, 2], ACT.Sqrt).then_inc(S("std3"), 1)
            next_function(ACT.Silu)
            act.wait_ge(S("T3"), 1)
            nc.scalar.copy(xT[:, 0:L // 2], ps[:, 2, 0:L // 2][:, ::-1]).then_inc(S("xT3"), 1)
            nc.scalar.copy(xT[:, L // 2:L], ps[:, 2, L // 2:L]).then_inc(S("xT3"), 1)

            def y_columns(n):
                act.wait_ge(S("yTp"), n + 1)
                src = ps[:, n % 2, 0:384].rearrange("p (c t) -> p c t", c=3)
                nc.scalar.copy(yT3[:, n], src[:, :, ::-1] if n % 2 else src).then_inc(S("yT3"), 1)

            for n in range(2 * NT):
                act.wait_ge(S("uv_read"), n + 1)
                dst = (vs if n < NT else us)[:, n % NT]
                nc.scalar.activation(dst, dst, ACT.Silu).then_inc(S("uv_silu"), 1)
            next_function(ACT.Sqrt)
            for unit in range(NB * NU):
                act.wait_ge(S("inv"), unit + 1)
                if unit >= 1:
                    act.wait_ge(S("inv_read"), unit)
                nc.scalar.copy(tmp[:, 0:384], ps[:, 4 + 2 * (unit % 2), 0:384]).then_inc(S("inv_even"), 1)
                for k in range(2):
                    if unit >= 1:
                        y_columns(2 * (unit - 1) + k)
            for n in range(2 * NB * NU - 2, 2 * NB * NU):
                y_columns(n)
            evac(4, S("T3b"), 1, S("xT3b"))
            act.wait_ge(S("var3b"), 1)
            nc.scalar.activation(st[:, 3], st[:, 2], ACT.Sqrt, scale=1.0 / D1).then_inc(S("rms3b"), 1)
            next_function(ACT.Silu)
            act.wait_ge(S("e3"), 1)
            nc.scalar.activation(xc[:], xc[:], ACT.Silu).then_inc(S("xr"), 1)
            next_function(ACT.Sqrt)
            act.wait_ge(S("var4"), 1)
            nc.scalar.activation(st[:, 3], st[:, 2], ACT.Sqrt).then_inc(S("std4"), 1)
            evac(2, S("T4"), 1, S("xT4"))

        @block.vector
        def _(dve):
            V = nc.vector
            chain = [0]

            def step(ins):
                chain[0] += 1
                ins.then_inc(dve_chain, 1)
                dve.wait_ge(dve_chain, chain[0])

            def evac(bank, done_wait, value, out_sem, scale=None):
                dve.wait_ge(done_wait, value)
                if scale is None:
                    V.tensor_copy(xT[:, 512:N], ps[:, bank]).then_inc(out_sem, 1)
                else:
                    V.tensor_scalar(xT[:, 512:N], ps[:, bank], scale, None, ALU.mult).then_inc(out_sem, 1)

            def per_token(v):
                return spread(v, 2, C)

            def flat3(t):
                return t[:].rearrange("p j b c -> p (j b) c")

            def flat2(t):
                return t[:].rearrange("p j b c -> p (j b c)")

            def centre(var_sem):
                step(V.tensor_reduce(st[:, 0], flat3(h), AXX, ALU.add))
                step(V.tensor_scalar(st[:, 0], st[:, 0], 1.0 / C, None, ALU.mult))
                step(V.tensor_tensor(flat3(xc), flat3(h), per_token(st[:, 0]), ALU.subtract))
                step(V.tensor_tensor(flat2(sq), flat2(xc), flat2(xc), ALU.mult))
                step(V.tensor_reduce(st[:, 1], flat3(sq), AXX, ALU.add))
                step(V.tensor_scalar(st[:, 1], st[:, 1], 1.0 / C, None, ALU.mult))
                V.tensor_scalar(st[:, 2], st[:, 1], 1e-5, None, ALU.add).then_inc(var_sem, 1)

            def weigh(n):
                dve.wait_ge(S("wb"), n + 1)
                dve.wait_ge(S("down"), n + 1)
                if n >= 2:
                    dve.wait_ge(S("zsum"), n - 1)
                V.tensor_tensor(zp_[:, n % 2], ps[:, 6], wb[:, n % 2], ALU.mult).then_inc(S("zpair"), 1)

            dve.wait_ge(ld_rp, 16)

            def square(i):
                dve.wait_ge(S("r_h"), i + 1)
                if i >= 1:
                    dve.wait_ge(S("r_ss"), i)
                V.tensor_tensor(rh[:, 1], rh[:, 0], rh[:, 0], ALU.mult).then_inc(S("r_sq"), 1)

            def normalise(i):
                dve.wait_ge(S("r_rms"), i + 1)
                step(V.tensor_scalar(rh[:, 2], rh[:, 2], 1e-8, None, ALU.add))
                step(V.reciprocal(rh[:, 2], rh[:, 2]))
                V.scalar_tensor_tensor(out=rh[:, 3], in0=rh[:, 0], scalar=0.0, in1=rh[:, 2], op0=ALU.max,
                                       op1=ALU.mult).then_inc(S("r_act"), 1)

            for i in range(LAYERS):
                square(i)
                if i < LAYERS - 1:
                    normalise(i)
            dve.wait_ge(gathered, 16 * NT * B)
            dve.wait_ge(ld_pe, 16)
            V.tensor_tensor(h[:, :, 0, :], xc[:, :, 0, :], pe_s[:], ALU.add).then_inc(S("embedded"), 1)
            V.tensor_tensor(h[:, :, 1, :], xc[:, :, 1, :], pe_s[:], ALU.add).then_inc(S("embedded"), 1)
            normalise(LAYERS - 1)
            dve.wait_ge(S("embedded"), 2)
            centre(S("var1"))
            square(LAYERS)
            dve.wait_ge(S("std1"), 1)
            step(V.reciprocal(st[:, 4], st[:, 3]))
            V.tensor_tensor(flat3(sq), flat3(xc), per_token(st[:, 4]), ALU.mult).then_inc(S("n1"), 1)
            normalise(LAYERS)
            evac(3, S("T1"), 2, S("xT1"))
            dve.wait_ge(S("xT1"), 2)
            dve.wait_ge(S("q1"), 2)
            qps = ps[:, 4:6].rearrange("p a t -> p (a t)")
            V.tensor_scalar(tmp[:], qps, 0.0, None, ALU.min).then_inc(S("qmin"), 1)
            dve.wait_ge(S("r_T"), 1)
            dve.wait_ge(S("geo_ones"), 1)
            step(V.tensor_copy(rh[:, 1], ps[:, 7, 0:2 * P]))
            for d in range(NW):
                plus, minus = (rh[:, 1, (2 * d + sd) * 32:(2 * d + sd + 1) * 32].rearrange("p (q r) -> p q r", r=R)
                               for sd in range(2))
                V.tensor_tensor(geo[:, 0, :, d * GR:d * GR + R], plus, minus, ALU.add).then_inc(S("geo_done"), 1)
                V.tensor_tensor(geo[:, 1, :, d * GR:d * GR + R], plus, minus, ALU.subtract).then_inc(S("geo_done"), 1)
            dve.wait_ge(S("kv1"), NT)
            kps = ps[:, 0:4].rearrange("p a (g k c) -> p (a g) k c", g=4, k=2)[:, :, 0, :]
            V.tensor_scalar(kf1.rearrange("p j b c -> p (j b) c"), kps, 0.0, None, ALU.min).then_inc(S("kmin"), 1)
            dve.wait_ge(S("kexp"), 1)
            V.scalar_tensor_tensor(out=kf1.rearrange("p j b c -> p (j b) c"), in0=kps, scalar=0.0, in1=kf1.rearrange("p j b c -> p (j b) c"), op0=ALU.max,
                                   op1=ALU.add).then_inc(S("kf1"), 1)
            dve.wait_ge(S("qexp"), 1)
            V.scalar_tensor_tensor(out=qf1[:], in0=qps, scalar=0.0, in1=qf1[:], op0=ALU.max, op1=ALU.add).then_inc(S("qf1"), 1)
            dve.wait_ge(S("ctx1"), 1)
            dve.wait_ge(ld_w, 16)
            V.tensor_tensor(cbd[:, 0:P], ps[:, 6, 0:P], W("mask_c"), ALU.mult).then_inc(S("cbd"), 1)
            V.tensor_scalar(cbd[:, P:144], W("mask_k"), ps[:, 6, P:P + 1], None, ALU.mult).then_inc(S("cbd"), 1)
            dve.wait_ge(S("nd1"), 1)
            nd = ps[:, 0:4].rearrange("p a (g x) -> p (a g) x", g=2)
            den = rw[:, 0].rearrange("p (j g) -> p j g", g=16)
            step(V.tensor_scalar(den, nd[:, :, P:144], 1e-6, None, ALU.max))
            step(V.reciprocal(rw[:, 0], rw[:, 0]))
            V.tensor_tensor(sq[:].rearrange("p j b (g d) -> p j (b g) d", d=8),
                            nd[:, :, 0:P].rearrange("p j (g d) -> p j g d", d=8),
                            spread(den, 3, 8), ALU.mult).then_inc(S("attn1"), 1)
            step(V.tensor_tensor(h[:].rearrange("p j b c -> p j (b c)"), h[:].rearrange("p j b c -> p j (b c)"),
                                 spread(W("bproj"), 1, NT), ALU.add))
            evac(5, S("T1b"), 2, S("xT1b"))
            dve.wait_ge(S("o1"), 1)
            step(V.tensor_tensor(flat2(h), flat2(h), ps[:, 0:2].rearrange("p a t -> p (a t)"), ALU.add))
            centre(S("var2"))
            dve.wait_ge(S("std2"), 1)
            step(V.reciprocal(st[:, 4], st[:, 3]))
            step(V.tensor_tensor(st[:, 5], st[:, 4], st[:, 4], ALU.mult))
            step(V.tensor_tensor(st[:, 5], st[:, 5], st[:, 1], ALU.mult))
            V.tensor_scalar(st[:, 5], st[:, 5], 1e-6, None, ALU.add).then_inc(S("msq2"), 1)
            step(V.tensor_tensor(flat3(x1), flat3(xc), per_token(st[:, 4]), ALU.mult))
            dve.wait_ge(S("rms2"), 1)
            step(V.reciprocal(st[:, 7], st[:, 6]))
            V.tensor_tensor(flat3(sq), flat3(x1), per_token(st[:, 7]), ALU.mult).then_inc(S("n2"), 1)
            evac(3, S("T2"), 2, S("xT2"), scale=W("ln1"))
            dve.wait_ge(ld_rope, 16)
            dve.wait_ge(S("qk2"), 1)
            step(V.tensor_tensor(qr[:], ps[:, 4:6].rearrange("p a t -> p (a t)"), rope_s[:, 0], ALU.mult))
            dve.wait_ge(S("qk2"), 2)
            V.tensor_tensor(tmp[:], ps[:, 6:8].rearrange("p a t -> p (a t)"), rope_s[:, 1], ALU.mult).then_inc(S("qrot"), 1)
            dve.wait_ge(S("qrot"), 1)
            V.tensor_tensor(qr[:], qr[:], tmp[:], ALU.add).then_inc(S("qrot"), 1)
            dve.wait_ge(S("qrot"), 2)
            dve.wait_ge(S("qk2"), 4)
            step(V.tensor_tensor(kr[:], ps[0:64, 0:2].rearrange("p a t -> p (a t)"), rope_s[0:64, 0], ALU.mult))
            V.tensor_tensor(tmp[0:64], ps[0:64, 2:4].rearrange("p a t -> p (a t)"), rope_s[0:64, 1], ALU.mult).then_inc(S("krot"), 1)
            dve.wait_ge(S("krot"), 1)
            V.tensor_tensor(kr[:], kr[:], tmp[0:64], ALU.add).then_inc(S("qrot"), 1)
            dve.wait_ge(S("qrot"), 3)
            for n, (x, pcs, t) in enumerate(((qr[:], pieces_q, tmp[:]), (kr[:], pieces_k[0:64], qf1[0:64]))):
                dve.wait_ge(S("rounded"), n + 1)
                V.tensor_tensor(t, x, pcs[:, 0], ALU.subtract).then_inc(S("rest"), 1)
            for n, (pcs, t) in enumerate(((pieces_q, tmp[:]), (pieces_k[0:64], qf1[0:64]))):
                dve.wait_ge(S("rounded"), n + 3)
                V.tensor_tensor(pcs[:, 2], t, pcs[:, 1], ALU.subtract).then_inc(S("k_pieces"), 1)
            dve.wait_ge(S("k_pieces"), 2)
            dve.wait_ge(ld_e, 32)
            dve.wait_ge(S("af_done"), 2 * NK + 2)
            V.tensor_copy(e_hi[:], e_raw).then_inc(S("e_split"), 1)
            dve.wait_ge(S("e_split"), 1)
            V.tensor_tensor(e_lo[:], e_raw, e_hi[:].bitcast(F32), ALU.subtract).then_inc(S("e_split"), 1)
            def maxima(b):
                mx = rw[:, b, 0:32]
                m2 = rw[:, 2 + b, 0:32]
                for n, (hh, i, c) in enumerate(ROW_CHUNKS):
                    n += b * len(ROW_CHUNKS)
                    dve.wait_ge(S("rows"), n + 1)
                    wd = min(512, (i + 1) * P - c * 512)
                    dst = (mx if c == 0 else m2)[:, hh * NT + i:hh * NT + i + 1]
                    V.tensor_reduce(dst, ps[:, row_bank(n), 0:wd], AXX, ALU.max).then_inc(S("max_read"), 1)
                at = (b + 1) * len(ROW_CHUNKS)
                dve.wait_ge(S("max_read"), at)
                a3 = mx.rearrange("p (h i) -> p h i", i=NT)[:, :, 4:NT]
                b3 = m2.rearrange("p (h i) -> p h i", i=NT)[:, :, 4:NT]
                step(V.tensor_tensor(a3, a3, b3, ALU.max))
                V.tensor_scalar(mx, mx, -1.0, None, ALU.mult).then_inc(S("max_all"), 1)
                dve.wait_ge(S("maxT"), b + 1)
                if b == 1:
                    dve.wait_ge(S("max_rows"), 48)
                bank = 6 if b == 0 else 0
                step(V.tensor_copy(mrow[:, 0], ps[0:32, bank, 0:P]))
                step(V.tensor_tensor(mtmp[:], ps[0:32, bank, 0:P], mrow[:, 0], ALU.subtract))
                step(V.tensor_copy(mrow[:, 1], mtmp[:]))
                V.tensor_tensor(mrow[:, 2], mtmp[:], mrow[:, 1], ALU.subtract).then_inc(S("max_pieces"), 1)

            maxima(0)
            maxima(1)
            for b in range(B):
                dve.wait_ge(S("pv"), (b + 1) * NT)
                V.tensor_copy(yT[:, b, 512:N], ps[:, 7]).then_inc(S("yT%d" % b), 1)
                dve.wait_ge(S("yTT"), b + 1)
                y = ps[:, 2 * b:2 * b + 2].rearrange("p a (j h d) -> p (a j) h d", j=4, h=NH)
                dn = rw[:, 4 + b, 0:32]
                step(V.tensor_copy(dn.rearrange("p (j h) -> p j h", h=NH), y[:, :, :, HD]))
                step(V.reciprocal(dn, dn))
                V.tensor_tensor(sq[:, :, b, :].rearrange("p j (h d) -> p j h d", d=HD), y[:, :, :, 0:HD],
                                spread(dn.rearrange("p (j h) -> p j h", h=NH), 3, HD),
                                ALU.mult).then_inc(S("yn"), 1)
            evac(5, S("T2b"), 2, S("xT2b"))
            dve.wait_ge(S("o2"), 1)
            step(V.tensor_tensor(flat2(x1), flat2(x1), ps[:, 0:2].rearrange("p a t -> p (a t)"), ALU.add))
            step(V.tensor_tensor(flat2(sq), flat2(x1), flat2(x1), ALU.mult))
            step(V.tensor_reduce(st[:, 1], flat3(sq), AXX, ALU.add))
            V.tensor_scalar(st[:, 2], st[:, 1], 1.0 / C, 1e-6, ALU.mult, ALU.add).then_inc(S("var2b"), 1)
            dve.wait_ge(S("rms2b"), 1)
            step(V.reciprocal(st[:, 4], st[:, 3]))
            step(V.tensor_tensor(flat3(xc), flat3(x1), per_token(st[:, 4]), ALU.mult))
            xcj = xc[:].rearrange("p j b c -> p j (b c)")
            step(V.tensor_tensor(xcj, xcj, spread(W("ln2"), 1, NT), ALU.mult))
            hi = fhl[:, :, :, 0, :].rearrange("p j b c -> p (j b) c")
            lo = fhl[:, :, :, 1, :].rearrange("p j b c -> p (j b) c")
            V.tensor_copy(hi.bitcast(F32R), flat3(xc)).then_inc(S("fhl"), 1)
            dve.wait_ge(S("fhl"), 1)
            V.tensor_tensor(lo, flat3(xc), hi, ALU.subtract).then_inc(S("fhl"), 1)
            step(V.tensor_tensor(flat2(h), flat2(h), flat2(x1), ALU.add))
            for b in range(B):
                dve.wait_ge(S("Te"), 2 * b + 2)
                V.tensor_copy(xs[:, b, 512:N], ps[:, 3 + 2 * b]).then_inc(S("xs%d" % b), 1)
            g3 = lambda k: rw[:, k].rearrange("p (g e) -> p g e", e=NE)
            each = lambda v: spread(v, 2, NE)
            dve.wait_ge(S("logits"), 1)
            lg = ps[:, 6, 0:P].rearrange("p (g e) -> p g e", e=NE)
            eidx = W("eidx").rearrange("p (g e) -> p g e", e=NE)
            step(V.tensor_reduce(st[:, 5], lg, AXX, ALU.max))
            V.tensor_tensor(g3(0), lg, each(st[:, 5]), ALU.subtract).then_inc(S("lmax"), 1)
            gates = [0]

            def gate():
                m = gates[0]
                gates[0] += 1
                n, n3 = m // 3, m % 3
                dve.wait_ge(S("silu"), m + 1)
                if n >= GSLOTS and n3 == 0:
                    dve.wait_ge(S("down"), n - GSLOTS + 1)
                V.tensor_tensor(gh[:, n % GSLOTS, n3], ps[:, 2 * (m % 3) + 1], sil[:, m % 2], ALU.mult).then_inc(S("gated"), 1)

            eidx, enum = (W(k).rearrange("p (g e) -> p g e", e=NE) for k in ("eidx", "enum"))
            dve.wait_ge(S("lexp"), 1)
            step(V.tensor_reduce(st[:, 6], g3(1), AXX, ALU.add))
            step(V.reciprocal(st[:, 6], st[:, 6]))
            step(V.tensor_tensor(g3(2), g3(1), each(st[:, 6]), ALU.mult))
            for k in range(2):
                probs = g3(2 + k)
                step(V.tensor_reduce(st[:, 7 + k], probs, AXX, ALU.max))
                step(V.tensor_tensor(g3(4), probs, each(st[:, 7 + k]), ALU.is_equal))
                gate()
                step(V.scalar_tensor_tensor(out=g3(4), in0=g3(4), scalar=-TOPK_OFF, in1=eidx, op0=ALU.mult, op1=ALU.add))
                step(V.tensor_reduce(st[:, 9], g3(4), AXX, ALU.min))
                gate()
                step(V.tensor_tensor(g3(5 + k), enum, each(st[:, 9]), ALU.is_equal))
                if k == 0:
                    step(V.scalar_tensor_tensor(out=g3(3), in0=g3(5), scalar=-2.0, in1=g3(2), op0=ALU.mult, op1=ALU.add))
                    gate()
            step(V.tensor_tensor(st[:, 7], st[:, 7], st[:, 8], ALU.add))
            step(V.tensor_scalar(st[:, 7], st[:, 7], 1e-9, None, ALU.add))
            gate()
            step(V.reciprocal(st[:, 7], st[:, 7]))
            step(V.tensor_tensor(g3(5), g3(5), g3(6), ALU.add))
            gate()
            step(V.tensor_tensor(g3(5), g3(5), g3(2), ALU.mult))
            step(V.tensor_tensor(g3(7), g3(5), each(st[:, 7]), ALU.mult))
            gate()
            dve.wait_ge(S("wpc_zero"), 1)
            pieces_w = [wpc[:, :, q, 0:B * NE] for q in range(3)]
            w16, r16 = (rw[:, k].rearrange("p (j e) -> p j e", e=B * NE) for k in (7, 0))
            V.tensor_copy(pieces_w[0], w16).then_inc(S("wpc"), 1)
            dve.wait_ge(S("wpc"), 1)
            step(V.tensor_tensor(r16, w16, pieces_w[0], ALU.subtract))
            gate()
            V.tensor_copy(pieces_w[1], r16).then_inc(S("wpc"), 1)
            dve.wait_ge(S("wpc"), 2)
            V.tensor_tensor(pieces_w[2], r16, pieces_w[1], ALU.subtract).then_inc(S("wpc"), 1)
            for n in range(ALL_PAIRS):
                while gates[0] < 3 * (n + 1):
                    gate()
                for d in DOWNS[n]:
                    weigh(d)
            dve.wait_ge(S("moe"), 1)
            step(V.tensor_tensor(flat2(h), flat2(h), ps[:, 0:2].rearrange("p a t -> p (a t)"), ALU.add))
            centre(S("var3"))
            dve.wait_ge(S("std3"), 1)
            step(V.reciprocal(st[:, 4], st[:, 3]))
            V.tensor_tensor(flat3(x1), flat3(xc), per_token(st[:, 4]), ALU.mult).then_inc(S("n3"), 1)
            dve.wait_ge(S("T3"), 2)
            V.tensor_copy(xT[:, L:L + L // 2], ps[:, 3, 0:L // 2][:, ::-1]).then_inc(S("xT3"), 1)
            V.tensor_copy(xT[:, L + L // 2:N], ps[:, 3, L // 2:L]).then_inc(S("xT3"), 1)
            dve.wait_ge(S("xT3"), 4)
            V.tensor_copy(st[:, 8], st[:, 4]).then_inc(S("T3_read"), 1)

            def uv_bias(n):
                dve.wait_ge(S("uv"), n + 1)
                bank = 4 + n % 4 if n < NT else n % NT
                dst = (vs if n < NT else us)[:, n % NT]
                V.tensor_tensor(dst, ps[:, bank, 0:384], W("vb" if n < NT else "ub"), ALU.add).then_inc(S("uv_read"), 1)

            for n in range(NT + 4):
                uv_bias(n)
            dve.wait_ge(S("uv_silu"), NT)
            V.tensor_tensor(veo[:, 0, 0], vs[:, 0:2], vs[:, 2:4], ALU.add).then_inc(S("even"), 1)
            V.tensor_tensor(veo[:, 1, 0], vs[:, 0:2], vs[:, 2:4], ALU.subtract).then_inc(S("even"), 1)
            V.tensor_tensor(veo[:, 0, 1], vs[:, 4:6], vs[:, 6:8], ALU.add).then_inc(S("even"), 1)
            for n in range(NT + 4, 2 * NT):
                uv_bias(n)

            def spectra(kt, o):
                q = NB * (NB * kt + 1) + o
                dve.wait_ge(S("part"), 2 * (q + 1))
                V.tensor_tensor(osp[:, o * NK + kt], osp[:, o * NK + kt], ssum[:, (kt % 2) * NB + o],
                                ALU.add).then_inc(S("spectra"), 1)

            dve.wait_ge(S("af_done"), 2 * NK + 2)
            for n in range(NB * NK):
                kt, i = n // NB, n % NB
                dve.wait_ge(S("spec"), n + 1)
                pcs = ps[:, 2 * (n % 4):2 * (n % 4) + 2, 0:384].rearrange("p s (b c) -> p s b c", b=B)
                for o in range(NB):
                    q, d = NB * n + o, WINDOW[i, o]
                    if q >= 2:
                        dve.wait_ge(S("part"), 2 * (q - 1))
                    own, cross = (prd[:, 2 * (q % 2) + x].rearrange("p s (b c) -> p s b c", b=B) for x in range(2))
                    sc = (afx[:] if kt == 0 else af[:, kt])[:, :, d]
                    step(V.tensor_tensor(own, pcs, spread(af[:, kt, ::-1, d], 2, B), ALU.mult))
                    ins = V.tensor_tensor(cross, pcs, spread(sc, 2, B), ALU.mult)
                    ins.then_inc(S("prd"), 1)
                dve.wait_ge(S("prd"), NB * (n + 1))
                V.tensor_copy(st[:, 9, 0:1], st[:, 4, 0:1]).then_inc(S("spec_read"), 1)
                if i == 0 and kt >= 1:
                    for o in range(NB):
                        spectra(kt - 1, o)
            for o in range(NB):
                spectra(NK - 1, o)
            step(V.tensor_tensor(flat2(h), flat2(h), flat2(x1), ALU.add))
            step(V.tensor_tensor(xc[:].rearrange("p j b c -> p j (b c)"), x1[:].rearrange("p j b c -> p j (b c)"),
                                 spread(W("ob"), 1, NT), ALU.subtract))
            dve.wait_ge(S("uv_silu"), 2 * NT)
            for unit in range(NB * NU):
                dve.wait_ge(S("inv_even"), unit + 1)
                odd = ps[:, 5 + 2 * (unit % 2), 0:384]
                if unit >= 1:
                    dve.wait_ge(S("yTp"), 2 * unit)
                step(V.tensor_tensor(y3[:, 0], tmp[:, 0:384], odd, ALU.add))
                V.tensor_tensor(y3[:, 1], tmp[:, 0:384], odd, ALU.subtract).then_inc(S("inv_read"), 1)
                dve.wait_ge(S("inv_read"), unit + 1)
                at = 4 * (unit // NU) + unit % NU
                V.tensor_tensor(y3[:, 0], y3[:, 0], us[:, at], ALU.mult).then_inc(S("y3"), 1)
                V.tensor_tensor(y3[:, 1], y3[:, 1], us[:, at + NU], ALU.mult).then_inc(S("y3"), 1)
            dve.wait_ge(S("o3"), 2)
            V.tensor_tensor(flat2(xc), flat2(xc), ps[:, 2:4].rearrange("p a t -> p (a t)"), ALU.subtract).then_inc(S("d3"), 1)
            evac(5, S("T3b"), 2, S("xT3b"))
            dve.wait_ge(S("t3"), 1)
            dve.wait_ge(S("xT3b"), 2)
            step(V.tensor_tensor(xc[:].rearrange("p j b c -> p j (b c)"),
                                 ps[:, 0:2].rearrange("p a (j x) -> p (a j) x", j=4),
                                 spread(W("tb"), 1, NT), ALU.add))
            step(V.tensor_tensor(flat2(sq), flat2(xc), flat2(xc), ALU.mult))
            V.tensor_reduce(st[:, 2], flat3(sq), AXX, ALU.add).then_inc(S("var3b"), 1)
            dve.wait_ge(S("rms3b"), 1)
            step(V.tensor_scalar(st[:, 3], st[:, 3], 1e-8, None, ALU.add))
            step(V.reciprocal(st[:, 4], st[:, 3]))
            V.tensor_tensor(flat3(xc), flat3(xc), per_token(st[:, 4]), ALU.mult).then_inc(S("e3"), 1)
            dve.wait_ge(S("xr"), 1)
            step(V.tensor_tensor(flat2(h), flat2(h), flat2(xc), ALU.add))
            centre(S("var4"))
            dve.wait_ge(S("std4"), 1)
            step(V.reciprocal(st[:, 4], st[:, 3]))
            V.tensor_tensor(flat3(sq), flat3(xc), per_token(st[:, 4]), ALU.mult).then_inc(S("n4"), 1)
            evac(3, S("T4"), 2, S("xT4"))
            hj = h[:].rearrange("p j b c -> p j (b c)")
            step(V.tensor_tensor(hj, hj, spread(W("b4"), 1, NT), ALU.add))
            dve.wait_ge(S("o4"), 1)
            V.tensor_tensor(flat2(sq), flat2(h), ps[:, 4:6].rearrange("p a t -> p (a t)"), ALU.add).then_inc(S("final"), 1)



def positions():
    pos = np.arange(N, dtype=np.float32)[:, None]
    d = np.arange(C)
    inv = np.power(np.float32(10000.0), -((d - d % 2).astype(np.float32) / np.float32(C))).astype(np.float32)
    ang = (pos * inv).astype(np.float32).astype(np.float64)
    pe = np.where(d % 2 == 0, np.sin(ang), np.cos(ang)).astype(np.float32)
    return np.ascontiguousarray(pe.reshape(NT, P, C).transpose(1, 0, 2))


def rope_tables():
    inv = (1.0 / 10000.0 ** (np.arange(0, HD, 2, dtype=np.float32) / HD)).astype(np.float32)
    f = np.outer(np.arange(N, dtype=np.float32), inv).astype(np.float32)
    emb = np.concatenate([f, f], -1)
    sign = np.where(np.arange(HD) < HD // 2, -1.0, 1.0).astype(np.float32)
    t = np.stack([np.tile(np.cos(emb).T, (P // HD, 1)), np.tile((np.sin(emb) * sign).T, (P // HD, 1))], 1)
    return np.ascontiguousarray(t.astype(np.float32))


def fourier_tables():
    m, k = np.arange(L)[:, None], np.arange(L)[None, :]
    u = np.arange(L // 2)[:, None] + 0.5
    ph = 2 * np.pi * ((m * k) % (2 * L)) / (2 * L)
    tm = np.stack([np.cos(ph), np.sin(ph)])
    tm[:, 0] *= 0.5
    pu = 2 * np.pi * np.mod(u * k, 2 * L) / (2 * L)
    tu = np.stack([np.cos(pu), np.sin(pu)])
    tu[1, :, 0] = np.sin(np.pi * u[:, 0])
    wk = np.where(k == 0, 1.0, 2.0) / (2 * L)
    tk = (tu * wk).transpose(0, 2, 1)
    alt = np.repeat(np.where(np.arange(L) % 2 == 0, 1.0, -1.0)[:, None], 2, 1)
    alt[0] *= 0.5
    lay = lambda t, n: np.ascontiguousarray(t.reshape(2, n, P, -1).transpose(0, 2, 1, 3).astype(np.float32))
    return (lay(tm, NM), lay(tu, NU), lay(tk, NK),
            alt.reshape(NM, P, 2).transpose(1, 0, 2).reshape(P, -1).astype(np.float32))


def kernel(**inputs):
    import concourse.bacc as _bacc
    from concourse.bass_utils import run_bass_kernel_spmd as _run
    import ml_dtypes

    a = {k: np.asarray(v) for k, v in inputs.items()}
    f32 = np.float32

    def twice(m):
        k, n = m.shape
        o = np.zeros((2 * k, 2 * n), f32)
        o[:k, :n] = m
        o[k:, n:] = m
        return o

    rot = np.concatenate([np.arange(HD // 2, HD), np.arange(HD // 2)])
    turned = lambda m: m.reshape(-1, HD, C)[:, rot].reshape(-1, C)
    wp = np.zeros((P, WTOT), f32)

    def put(name, m):
        lo, hi = WCOLS[name]
        wp[:m.shape[0], lo:hi] = m.reshape(m.shape[0], -1)

    rows = lambda v, n=1: np.broadcast_to(np.tile(v, n)[None], (P, v.size * n))
    put("q1", twice(a["L0_attn_Wq"].T))
    put("kv1", twice(a["L0_attn_Wkv"].T))
    put("proj1", twice(a["L0_attn_Wproj"].T))
    put("q2", twice(a["L0_ffn_wq"].T))
    put("q2r", twice(turned(a["L0_ffn_wq"]).T))
    put("k2", twice(a["L0_ffn_wk"].T))
    put("k2r", twice(turned(a["L0_ffn_wk"]).T))
    put("v2", twice(a["L0_ffn_wv"].T))
    put("wo2", twice(a["L0_ffn_wo"].T))
    put("v3", twice(a["L1_attn_v_w"].T))
    put("u3", twice(a["L1_attn_u_w"].T))
    o3 = twice(a["L1_attn_o_w"].T).reshape(3, P, P).transpose(1, 0, 2)
    put("o3", o3.reshape(P, -1))
    put("t3", twice(a["L1_attn_t_w"].T))
    put("w4", twice(a["L1_ffn_weight"].T))
    put("bproj", rows(a["L0_attn_bproj"], 2))
    put("ub", rows(a["L1_attn_u_b"], 2))
    put("vb", rows(a["L1_attn_v_b"], 2))
    put("ob", rows(a["L1_attn_o_b"], 2))
    put("tb", rows(a["L1_attn_t_b"], 2))
    put("b4", rows(a["L1_ffn_bias"], 2))
    put("ln2", rows(a["L0_ffn_ln2_w"], 2))
    put("ln1", np.tile(a["L0_ffn_ln1_w"], 2)[:, None])
    hd = np.arange(P) // 8
    put("mask_c", (hd[:, None] == hd[None, :]).astype(f32))
    put("mask_k", (hd[:, None] == np.arange(16)[None, :]).astype(f32))
    put("eidx", np.broadcast_to(np.tile(np.arange(NE) + NE, 16).astype(f32)[None], (P, P)))
    put("enum", np.broadcast_to(np.tile(np.arange(NE), 16).astype(f32)[None], (P, P)))

    tm, tu, tk, alt = fourier_tables()
    rp = np.zeros((P, RTOT), f32)

    def rput(name, m):
        lo, hi = RCOLS[name]
        rp[:, lo:hi] = m

    groups = P // R
    side = np.arange(L, dtype=f32).reshape(NM, P)
    lag = np.zeros((2 * groups, P), f32)
    lag[:NW * 2 * NM] = np.concatenate([mid + sign * side for mid in (0, L, -L) for sign in (1, -1)])
    rput("lag", np.repeat(lag, R, 0).reshape(2, P, P).transpose(1, 0, 2).reshape(P, 2 * P))
    g = np.arange(P) // R
    rput("ones", (g[:, None] == g[None, :]).astype(f32))
    for i in range(LAYERS):
        bd = np.zeros((P, P), f32)
        for q in range(groups):
            bd[q * R:(q + 1) * R, q * R:(q + 1) * R] = a["L1_attn_rpe_lw"][i].T
        rput("l%d" % i, bd)
        rput("b%d" % i, np.tile(a["L1_attn_rpe_lb"][i], groups)[:, None])
    rput("pw", np.tile(a["L1_attn_pos_w"][:, 0], groups)[:, None])
    rput("pb", np.tile(a["L1_attn_pos_b"], groups)[:, None])
    ow = np.zeros((NM, 32, NW, D1), f32)
    for d in range(NW):
        ow[:, d * GR:d * GR + R, d] = a["L1_attn_out_w"].T
        ow[:, d * GR + R, d] = a["L1_attn_out_b"]
    rput("outw", ow.reshape(P, NW * D1))
    rput("alt", alt)

    ep = np.zeros((P, ETOT), f32)
    for name, key in (("w1", "L0_ffn_w1"), ("w3", "L0_ffn_w3")):
        src = a[key]
        t = np.zeros((12, P, C), f32)
        for pr in range(NPAIR):
            for k in range(2):
                t[3 * pr + k] = src[2 * pr + k, :P]
                t[3 * pr + 2, 64 * k:64 * k + REM] = src[2 * pr + k, P:]
        t = t.transpose(2, 0, 1).reshape(C, -1)
        ep[:, ECOLS[name][0]:ECOLS[name][1]] = np.concatenate([t, t])
    r = a["L0_ffn_router_w"].T
    ep[:, ECOLS["rt"][0]:ECOLS["rt"][1]] = np.concatenate([r, r])
    w2 = a["L0_ffn_w2"]
    ep[:, ECOLS["w2m"][0]:ECOLS["w2m"][1]] = w2[:, :, :P].transpose(2, 0, 1).reshape(P, -1)
    t = np.zeros((P, NPAIR, 2, C), f32)
    for pr in range(NPAIR):
        for k in range(2):
            t[64 * k:64 * k + REM, pr, k] = w2[2 * pr + k, :, P:].T
    ep[:, ECOLS["w2r"][0]:ECOLS["w2r"][1]] = t.reshape(P, -1)
    ep[:, ECOLS["ii"][0]:ECOLS["ii"][1]] = np.concatenate([np.eye(C, dtype=f32)] * 2)

    pq = np.arange(P)
    bfc = np.zeros((P, 3 * P + B * NPAIR * P), f32)
    bfc[:, 0:P] = np.where(pq[None, :] <= pq[:, None], 0.0, NEG)
    bfc[:, P:2 * P] = np.where(pq[None, :] >= pq[:, None], 0.0, NEG)
    bfc[:, 2 * P:3 * P] = np.eye(P)
    for b in range(B):
        for pr in range(NPAIR):
            for k in range(2):
                for pc in range(3):
                    c0 = 3 * P + (b * NPAIR + pr) * P + 64 * k
                    bfc[32 * pc + b * NE + 2 * pr + k, c0:c0 + 64] = 1.0
    bfc = bfc.astype(ml_dtypes.bfloat16)

    idx = np.ascontiguousarray(a["x"].reshape(B, NT, P).transpose(2, 1, 0).reshape(P, NT * B))
    arrays = {"idx": idx, "emb": np.ascontiguousarray(a["L0_tok_W"]), "pe": positions(), "wpack": wp, "rpack": rp,
              "epack": ep, "ident": np.eye(P, dtype=f32), "bfc": bfc, "rope": rope_tables(), "tm": tm, "tu": tu, "tk": tk}

    nc = _bacc.Bacc("TRN2", target_bir_lowering=False, num_devices=1)
    args = {n: nc.dram_tensor(n, v.shape, mybir.dt.from_np(v.dtype), kind="ExternalInput").ap() for n, v in arrays.items()}
    args["scr_q"] = nc.dram_tensor("scr_q", (3, P, N), BF16, kind="Internal").ap()
    args["scr_k"] = nc.dram_tensor("scr_k", (3, 64, N), BF16, kind="Internal").ap()
    args["out"] = nc.dram_tensor("out", (P, NT * B * C), F32, kind="ExternalOutput").ap()
    build(nc, **args)
    r = _run(nc, [arrays], core_ids=[0])
    o = r.results[0]["out"]
    return np.ascontiguousarray(np.asarray(o).reshape(P, NT, B, C).transpose(2, 1, 0, 3).reshape(B, N, C))
```

```python
from contextlib import ExitStack

import numpy as np
import concourse.bass as bass
from concourse import mybir

F32 = mybir.dt.float32
F32R = mybir.dt.float32r
BF16 = mybir.dt.bfloat16
I32 = mybir.dt.int32
ALU = mybir.AluOpType
ACT = mybir.ActivationFunctionType
AXX = mybir.AxisListType.X

P = 128
B, N, C = 2, 1024, 64
NT = N // P
H1 = 8
NH, NKV, HD = 4, 2, 16
NE, HID = 8, 170
NPAIR = NE // 2
REM = HID - P
D1 = 192
R = 8
LAYERS = 3
L = N // 2
NB = N // L
NW = 3
WINDOW = {(0, 0): 0, (0, 1): 1, (1, 0): 2, (1, 1): 0}
NU = L // 2 // P
NM = L // P
NK = L // P
CONSTANTS = {n: i + 1 for i, n in enumerate(("geo_zero", "geo_ones", "va1_ones", "va2_zero", "va2_ones", "wst_zero",
                                             "wpc_zero", "k_ones"))}
NORMS = {"var1": 1, "var2": 2, "msq2": 3, "var2b": 4, "var3": 5, "var3b": 6, "var4": 7,
         "std1": 1, "std2": 2, "rms2": 3, "rms2b": 4, "std3": 5, "rms3b": 6, "std4": 7}
EARLY_AF = 7
GR = R + 1
NEG = -1.0e30
TERMS_Q = [0, 0, 0, 1, 1, 2]
TERMS_K = [0, 1, 2, 0, 1, 0]
MROW = 16 * len(TERMS_Q)
KROWS = MROW + 3
TOPK_OFF = float(NE)
LAG = 4
GSLOTS = LAG + 1
ALL_PAIRS = 4 * NPAIR
DOWNS = [[] if n < LAG else [m for m in range(2 * (n - LAG) - 1, 2 * (n - LAG) + 1) if 0 <= m < n] if n < 2 * LAG
         else [n - 1] for n in range(ALL_PAIRS)]
DOWNS[-1].append(ALL_PAIRS - 1)
assert sum(DOWNS, []) == list(range(ALL_PAIRS))
ROW_CHUNKS = [(hh, i, c) for hh in range(NH) for i in range(NT) for c in range(i // 4 + 1)]
EARLY = 12
WIDE = len(ROW_CHUNKS) + EARLY


def row_bank(n):
    return n % 6 if n < WIDE else n % 2


def row_free(n):
    return n - 5 if n < WIDE + 2 else n - 1


def col_heads(j):
    return [(hh,) for hh in range(NH)] if j < 4 else [(0, 1), (2, 3)]


COL_STEPS = [(j, heads) for j in range(NT) for heads in col_heads(j)]


def col_steps(b, j):
    return b * len(COL_STEPS) + sum(len(col_heads(i)) for i in range(j + 1))

WCOLS = {}
_at = 0
for _n, _w in (("q1", P), ("kv1", 2 * P), ("proj1", P), ("q2", P), ("q2r", P), ("k2", 64), ("k2r", 64), ("v2", 64),
               ("wo2", P), ("v3", 2 * D1), ("u3", 2 * D1), ("o3", 3 * P), ("t3", P), ("w4", P),
               ("bproj", P), ("ub", 2 * D1), ("vb", 2 * D1), ("ob", P), ("tb", P), ("b4", P), ("ln2", P),
               ("ln1", 1), ("mask_c", P), ("mask_k", 16), ("eidx", P), ("enum", P)):
    WCOLS[_n] = (_at, _at + _w)
    _at += _w
WTOT = _at
RCOLS = {}
_at = 0
for _n, _w in (("lag", 2 * P), ("ones", P), ("l0", P), ("l1", P), ("l2", P), ("pw", 1), ("pb", 1), ("b0", 1), ("b1", 1),
               ("b2", 1), ("outw", NW * D1), ("alt", NM * 2)):
    RCOLS[_n] = (_at, _at + _w)
    _at += _w
RTOT = _at
ECOLS = {}
_at = 0
for _n, _w in (("w1", 12 * P), ("w3", 12 * P), ("rt", 8), ("w2m", NE * 64), ("w2r", NPAIR * P), ("ii", 64)):
    ECOLS[_n] = (_at, _at + _w)
    _at += _w
ETOT = _at
NSPLIT = ECOLS["rt"][1]


def spread(v, dim, n):
    v = v.unsqueeze(dim)
    shape = list(v.shape)
    shape[dim] = n
    return v.broadcast_to(shape)


def build(nc, idx, emb, pe, wpack, rpack, epack, ident, bfc, rope, tm, tu, tk, scr_q, scr_k, out):
    with ExitStack() as ctx:
        def sb(name, shape, dt=F32):
            return ctx.enter_context(nc.sbuf_tensor(name, shape, dt))

        def sem(name):
            return ctx.enter_context(nc.semaphore(name))

        ps = ctx.enter_context(nc.psum_tensor("ps", [P, 8, 512], F32))

        idx_s = sb("idx_s", [P, NT * B], I32)
        w = sb("w", [P, WTOT])
        rp = sb("rp", [P, RTOT])
        ew = sb("ew", [P, ETOT - NSPLIT])
        idt = sb("idt", [P, P])
        bfc_s = sb("bfc_s", [P, 3 * P + B * NPAIR * P], BF16)
        arena = sb("arena", [P, 2 * NT * N])
        tu_s = sb("tu_s", [P, 2, NU, L])
        tk_s = sb("tk_s", [P, 2, NK, L // 2])
        h = sb("h", [P, NT, B, C])
        xc = sb("xc", [P, NT, B, C])
        sq = sb("sq", [P, NT, B, C])
        x1 = sb("x1", [P, NT, B, C])
        xT = sb("xT", [P, N])
        st = sb("st", [P, 12, NT * B])
        rw = sb("rw", [P, 8, NT * B * NE])

        def W(name, lo=0, hi=None):
            a, b = WCOLS[name]
            return w[:, a + lo:(b if hi is None else a + hi)]

        def RP(name):
            a, b = RCOLS[name]
            return rp[:, a:b]

        def E(name, lo=0, hi=None):
            a, b = ECOLS[name]
            return ew[:, a - NSPLIT + lo:(b if hi is None else a + hi) - NSPLIT]

        def EP(piece, name, lo, hi):
            a = ECOLS[name][0]
            return piece[:, a + lo:a + hi]

        mask_ts, mask_st, ident_b = bfc_s[:, 0:P], bfc_s[:, P:2 * P], bfc_s[:, 2 * P:3 * P]

        def selw(b, pr):
            a = 3 * P + (b * NPAIR + pr) * P
            return bfc_s[:, a:a + P]

        def plan(region, *parts):
            at, views = 0, []
            for shape, dt in parts:
                cols = int(np.prod(shape)) // (2 if dt == BF16 else 1)
                v = region[:, at:at + cols]
                at += cols
                v = v if dt == F32 else v.bitcast(dt)
                names = ["a", "b", "c", "d"][:len(shape)]
                if len(shape) > 1:
                    v = v.rearrange("p (%s) -> p %s" % (" ".join(names), " ".join(names)),
                                    **dict(zip(names[1:], shape[1:])))
                views.append(v)
            assert at <= region.shape[1], (at, region.shape)
            return views

        qst, kst, yT, pt = plan(arena, ([B * NH, N], BF16), ([B * NKV, N], BF16), ([B, N], F32), ([2, NH, N], F32))
        _, _, _, pieces_q, pieces_k, e_raw = plan(arena, ([B * NH, N], BF16), ([B * NKV, N], BF16), ([B, N], F32),
                                                  ([3, N], BF16), ([3, N], BF16), ([NSPLIT], F32))
        _, _, rope_s, tm_s = plan(arena, ([B * NH, N], BF16), ([B * NKV, N], BF16), ([2, N], F32), ([2, NM, L], F32))
        fhl, sil, gh, wb, zp_ = plan(arena, ([NT, B, P], F32), ([2, 512], F32), ([GSLOTS, 3, 512], F32),
                                     ([2, 512], F32), ([2, 512], F32))
        fhl = fhl.rearrange("p j b (q c) -> p j b q c", q=2)
        zacc = (xc[:].rearrange("p j b c -> p (j b c)"), sq[:].rearrange("p j b c -> p (j b c)"))
        us, vs, osp, prd = plan(arena, ([NT, 384], F32), ([NT, 384], F32), ([NB * NK, 2, 384], F32), ([4, 2, 384], F32))
        _, yT3 = plan(arena, ([NT, 384], F32), ([NT, 3, P], F32))

        gt2 = sb("gt2", [P, P])
        af = sb("af", [P, NK, 2, NW, D1])
        afx = sb("afx", [P, 2, NW, D1])
        cbd = sb("cbd", [P, 144])
        tmp = sb("tmp", [P, N])
        va2 = sb("va2", [P, NT, B, NKV, 32])
        mrow = sb("mrow", [32, 3, P], BF16)
        mtmp = sb("mtmp", [32, P])
        wpc = sb("wpc", [P, NT, 3, 32], BF16)
        unused = sb("unused", [1, 16])
        wst = sb("wst", [P, N], BF16)
        with ExitStack() as experts:
            e_hi, e_lo, xs = (experts.enter_context(nc.sbuf_tensor(n, sh, F32R)) for n, sh in (
                ("e_hi", [P, NSPLIT]), ("e_lo", [P, NSPLIT]), ("xs", [P, B, N])))
        share = sb("share", [P, 2 * NSPLIT + B * N])
        pe_s, va1, kf1, qf1, qr, kr_, gt, rh, geo = plan(
            share, ([NT, C], F32), ([NT, 132], F32), ([NT, B, C], F32), ([N], F32), ([N], F32), ([N], F32),
            ([2, L], F32), ([4, 2 * P], F32), ([2, NM, 32], F32))
        kr = kr_[0:64]
        veo, y3, ssum = plan(share, ([2, NB, NU, 384], F32), ([2, 384], F32), ([2 * NB, 2, 384], F32))
        ld_idx, ld_pe, ld_rp, ld_id, ld_w, ld_bf, ld_rope, ld_m, ld_e, ld_u, ld_k = (
            sem(n) for n in ("ld_idx", "ld_pe", "ld_rp", "ld_id", "ld_w", "ld_bf", "ld_rope", "ld_m", "ld_e", "ld_u", "ld_k"))
        gathered = sem("gathered")
        dve_chain, act_chain, pool_chain = sem("dve_chain"), sem("act_chain"), sem("pool_chain")

        names = {}

        def S(name):
            if name not in names:
                names[name] = sem(name)
            return names[name]

        def mm(o, l, r, start=True, stop=True, **kw):
            return nc.tensor.matmul(o, l, r, start=start, stop=stop, **kw)

        block = ctx.enter_context(nc.Block())

        @block.sync
        def _(sp):
            sp.dma_start(idx_s[:], idx).then_inc(ld_idx, 16)
            sp.dma_start(rp[:], rpack).then_inc(ld_rp, 16)
            sp.dma_start(idt[:], ident).then_inc(ld_id, 16)
            sp.dma_start(pe_s[:], pe).then_inc(ld_pe, 16)
            sp.dma_start(w[:], wpack).then_inc(ld_w, 16)
            sp.dma_start(rope_s[:], rope).then_inc(ld_rope, 16)
            sp.dma_start(bfc_s[:], bfc).then_inc(ld_bf, 16)
            sp.wait_ge(gathered, 16 * NT * B)
            for s in range(2):
                sp.dma_start(tm_s[:, s], tm[s]).then_inc(ld_m, 16)
            sp.dma_start(ew[:], epack[:, NSPLIT:ETOT]).then_inc(ld_e, 16)
            sp.wait_ge(S("gf"), 3)
            sp.dma_start(e_raw, epack[:, 0:NSPLIT]).then_inc(ld_e, 16)
            sp.wait_ge(S("k_pieces"), 1)
            sp.dma_start(scr_q.rearrange("s p t -> p s t"), pieces_q).then_inc(S("scr_q_written"), 16)
            sp.wait_ge(S("k_pieces"), 2)
            sp.dma_start(scr_k.rearrange("s p t -> p s t"), pieces_k[0:64]).then_inc(S("scr_k_written"), 16)
            sp.wait_ge(S("scr_q_written"), 16)
            for n, pc in enumerate(TERMS_Q):
                sp.dma_start(qst[16 * n:16 * n + 16], scr_q[pc].rearrange("(g d) t -> d g t", d=HD)).then_inc(S("stacks"), 16)
            sp.wait_ge(S("scr_k_written"), 16)
            for n, pc in enumerate(TERMS_K):
                sp.dma_start(kst[16 * n:16 * n + 16], scr_k[pc].rearrange("(g d) t -> d g t", d=HD)).then_inc(S("stacks"), 16)
            for s in range(2):
                sp.dma_start(tu_s[:, s], tu[s]).then_inc(ld_u, 16)
            for s in range(2):
                sp.dma_start(tk_s[:, s], tk[s]).then_inc(ld_k, 16)
            for b in range(B):
                sp.wait_ge(S("max_pieces"), b + 1)
                for pc in range(3):
                    sp.dma_start(qst[MROW + pc:MROW + pc + 1, b * NH:(b + 1) * NH, :],
                                 mrow[:, pc, :]).then_inc(S("max_rows"), 16)
            for a in range(2):
                sp.wait_ge(S("final"), a + 1)
                sp.dma_start(out[:, a * 512:(a + 1) * 512],
                             sq[:, 4 * a:4 * a + 4].rearrange("p j b c -> p (j b c)")).then_inc(S("stored"), 16)
            sp.wait_ge(S("stored"), 32)

        @block.gpsimd
        def _(pool):
            def step(ins):
                chain[0] += 1
                ins.then_inc(pool_chain, 1)
                pool.wait_ge(pool_chain, chain[0])

            chain = [0]
            pool.wait_ge(ld_idx, 16)
            for j in range(NT):
                for b in range(B):
                    n = j * B + b
                    nc.gpsimd.indirect_dma_start(
                        xc[:, j, b, :], None, emb,
                        bass.IndirectOffsetOnAxis(ap=idx_s[:, n:n + 1], axis=0)).then_inc(gathered, 16)
            nc.gpsimd.memset(geo[:], 0.0).then_inc(S("constants"), 1)
            pool.wait_ge(S("constants"), CONSTANTS["geo_zero"])
            nc.gpsimd.memset(geo[:, 0, :, 0:NW * GR].rearrange("p q (d n) -> p q d n", n=GR)[:, :, :, R], 2.0).then_inc(S("constants"), 1)
            nc.gpsimd.memset(va1[:, :, P:P + 1], 1.0).then_inc(S("constants"), 1)
            nc.gpsimd.memset(va2[:], 0.0).then_inc(S("constants"), 1)
            pool.wait_ge(S("constants"), CONSTANTS["va2_zero"])
            nc.gpsimd.memset(va2[:, :, :, :, HD:HD + 1], 1.0).then_inc(S("constants"), 1)
            nc.gpsimd.memset(wst[:], 0.0).then_inc(S("constants"), 1)
            pool.wait_ge(S("constants"), CONSTANTS["wst_zero"])
            nc.gpsimd.memset(wpc[:], 0.0).then_inc(S("constants"), 1)
            pool.wait_ge(S("constants"), CONSTANTS["wpc_zero"])
            nc.gpsimd.memset(kst[MROW:KROWS], 1.0).then_inc(S("constants"), 1)
            for t in range(4):
                b, hf = t // 2, t % 2
                for pr in range(NPAIR):
                    n = t * NPAIR + pr
                    pool.wait_ge(S("zpair"), n + 1)
                    z = zacc[b][:, hf * 512:(hf + 1) * 512]
                    if pr == 0:
                        nc.gpsimd.tensor_copy(z, zp_[:, n % 2, :]).then_inc(S("zsum"), 1)
                    else:
                        pool.wait_ge(S("zsum"), n)
                        nc.gpsimd.tensor_tensor(z, z, zp_[:, n % 2, :], ALU.add).then_inc(S("zsum"), 1)
            pool.wait_ge(S("uv_silu"), NT)
            nc.gpsimd.tensor_tensor(veo[:, 1, 1], vs[:, 4:6], vs[:, 6:8], ALU.subtract).then_inc(S("odd"), 1)
            for n in range(NB * NK):
                kt, i = n // NB, n % NB
                for o in range(NB):
                    q = NB * n + o
                    pool.wait_ge(S("prd"), q + 1)
                    if i == 0:
                        dst = osp[:, o * NK + kt]
                    else:
                        dst = ssum[:, (kt % 2) * NB + o]
                        if kt >= 2:
                            pool.wait_ge(S("spectra"), NB * (kt - 2) + o + 1)
                    p1, p2 = prd[:, 2 * (q % 2)], prd[:, 2 * (q % 2) + 1]
                    nc.gpsimd.tensor_tensor(dst[:, 0], p1[:, 0], p1[:, 1], ALU.subtract).then_inc(S("part"), 1)
                    nc.gpsimd.tensor_tensor(dst[:, 1], p2[:, 0], p2[:, 1], ALU.add).then_inc(S("part"), 1)

        @block.tensor
        def _(pe):
            def transposes(src, banks, ready, done, values=(1, 2)):
                for j in range(NT):
                    if j % 4 == 0:
                        pe.wait_ge(ready, values[j // 4])
                    ins = nc.tensor.transpose(ps[:, banks + j // 4, (j % 4) * P:(j % 4 + 1) * P],
                                              src[:, j].rearrange("p b c -> p (b c)"), idt[:])
                    if j % 4 == 3:
                        ins.then_inc(done, 1)

            def projection(x, weights, banks, done):
                for j in range(NT):
                    if j % 4 == 0:
                        pe.wait_ge(S(x + ("_lo", "_hi")[j // 4]), 1)
                    ins = mm(ps[:, banks + j // 4, (j % 4) * P:(j % 4 + 1) * P], xT[:, j * P:(j + 1) * P], W(weights))
                    if j % 4 == 3:
                        ins.then_inc(done, 1)

            pe.wait_ge(ld_rp, 16)
            pe.wait_ge(ld_id, 16)
            for i in range(LAYERS + 1):
                pe.wait_ge(S("r_sq"), i + 1)
                mm(ps[:, 0, 0:2 * P], RP("ones"), rh[:, 1]).then_inc(S("r_ss"), 1)
                if i < LAYERS:
                    pe.wait_ge(S("r_act"), i + 1)
                    mm(ps[:, 1, 0:2 * P], RP("l%d" % i), rh[:, 3]).then_inc(S("r_lin"), 1)
            transposes(sq, 2, S("n1"), S("T1"))
            pe.wait_ge(ld_w, 16)
            for c in range(2):
                pe.wait_ge(S(("xT1_lo", "xT1_hi")[c]), 1)
                mm(ps[:, 4 + c], W("q1"), xT[:, c * 512:(c + 1) * 512]).then_inc(S("q1"), 1)
            pe.wait_ge(S("r_act"), LAYERS + 1)
            nc.tensor.transpose(ps[:, 7, 0:P], rh[:, 3, 0:P], idt[:])
            nc.tensor.transpose(ps[:, 7, P:2 * P], rh[:, 3, P:2 * P], idt[:]).then_inc(S("r_T"), 1)
            KVB = (0, 1, 2, 3)
            for j in range(NT):
                mm(ps[:, KVB[j // 2], (j % 2) * 256:(j % 2 + 1) * 256], xT[:, j * P:(j + 1) * P], W("kv1")).then_inc(S("kv1"), 1)
            pe.wait_ge(S("kf1"), 1)
            pe.wait_ge(S("va1"), 1)
            pe.wait_ge(S("constants"), CONSTANTS["va1_ones"])
            for j in range(NT):
                ins = mm(ps[:, 6, 0:P + 1], kf1[:, j].rearrange("p b c -> p (b c)"), va1[:, j, 0:P + 1],
                         start=(j == 0), stop=(j == NT - 1))
            ins.then_inc(S("ctx1"), 1)
            pe.wait_ge(S("cbd"), 2)
            pe.wait_ge(S("qf1"), 1)
            for j in range(NT):
                ins = mm(ps[:, j // 2, (j % 2) * 256:(j % 2) * 256 + 144], qf1[:, j * P:(j + 1) * P], cbd[:])
                if j % 4 == 3:
                    ins.then_inc(S("nd1"), 1)
            transposes(sq, 4, S("attn1"), S("T1b"))
            projection("xT1b", "proj1", 0, S("o1"))
            pe.wait_ge(ld_m, 32)
            pe.wait_ge(S("geo_done"), 2 * NW)
            for s in range(2):
                for q in range(NM):
                    ins = mm(ps[32 * q:32 * q + 32, 4 + s], geo[:, s, q, :], tm_s[:, s, q, :], tile_position=(0, 32 * q))
                ins.then_inc(S("gf"), 1)
            for q in range(NM):
                a = RCOLS["alt"][0] + 2 * q
                ins = mm(ps[32 * q:32 * q + 32, 6, 0:2], geo[:, 0, q, :], rp[:, a:a + 2], tile_position=(0, 32 * q))
            ins.then_inc(S("gf"), 1)
            pe.wait_ge(S("gt_done"), 4)

            def transfer(n, bank):
                lhs = gt2[:] if n == 2 * NK else gt[:, 1 - n % 2, n // 2 * P:(n // 2 + 1) * P]
                for x in range(2):
                    ins = mm(ps[:, bank + x, 0:288], lhs, RP("outw")[:, x * 288:(x + 1) * 288])
                ins.then_inc(S("afp"), 1)

            for n in range(EARLY_AF):
                if n >= 3:
                    pe.wait_ge(S("af_done"), n - 2)
                transfer(n, (2, 6, 4)[n % 3])
            pe.wait_ge(S("af_done"), EARLY_AF)
            transposes(sq, 2, S("n2"), S("T2"))
            for name, bank, rows in (("q2", 4, P), ("q2r", 6, P), ("k2", 0, 64), ("k2r", 2, 64)):
                for c in range(2):
                    if name == "q2":
                        pe.wait_ge(S(("xT2_lo", "xT2_hi")[c]), 1)
                    ins = mm(ps[0:rows, bank + c], W(name), xT[:, c * 512:(c + 1) * 512])
                ins.then_inc(S("qk2"), 1)
            pe.wait_ge(S("qrot"), 1)
            for j in range(NT):
                ins = mm(ps[:, 4, j * 64:(j + 1) * 64], xT[:, j * P:(j + 1) * P], W("v2"))
            ins.then_inc(S("v2"), 1)
            pe.wait_ge(S("krot"), 1)
            for n in range(EARLY_AF, 2 * NK + 1):
                transfer(n, 2 * (n - EARLY_AF))
            pe.wait_ge(S("stacks"), 12 * 16)
            pe.wait_ge(S("constants"), CONSTANTS["k_ones"])
            pe.wait_ge(S("af_done"), 2 * NK + 2)
            pe.wait_ge(ld_bf, 16)

            def score_rows(b, n):
                hh, i, c = ROW_CHUNKS[n]
                n += b * len(ROW_CHUNKS)
                if n >= 6:
                    pe.wait_ge(S("max_read"), row_free(n))
                bank = row_bank(n)
                wd = min(512, (i + 1) * P - c * 512)
                last = c == i // 4
                ins = mm(ps[:, bank, 0:wd], qst[0:MROW, b * NH + hh, i * P:(i + 1) * P],
                         kst[0:MROW, b * NKV + hh // 2, c * 512:c * 512 + wd], start=True, stop=not last)
                if last:
                    ins = mm(ps[:, bank, wd - P:wd], ident_b, mask_ts, start=False, stop=True)
                ins.then_inc(S("rows"), 1)

            def score_cols(b, step_n):
                j, heads = COL_STEPS[step_n]
                n = b * len(COL_STEPS) + step_n
                if n < 2:
                    pe.wait_ge(S("max_read"), WIDE - 2 + 2 * n)
                else:
                    pe.wait_ge(S("exp_done"), n - 1)
                bank = 2 + 2 * (n % 2)
                for x in range(2):
                    c, hh = (x, heads[0]) if len(heads) == 1 else (1, heads[x])
                    lo = max(j * P, c * 512)
                    diag = lo == j * P
                    ins = mm(ps[:, bank + x, lo - c * 512:512], kst[0:KROWS, b * NKV + hh // 2, j * P:(j + 1) * P],
                             qst[0:KROWS, b * NH + hh, lo:(c + 1) * 512], start=True, stop=not diag)
                    if diag:
                        ins = mm(ps[:, bank + x, lo - c * 512:lo - c * 512 + P], ident_b, mask_st, start=False, stop=True)
                ins.then_inc(S("cols"), 1)

            def weighted(b, j, c):
                if c < j // 4:
                    return
                pe.wait_ge(S("exp_done"), col_steps(b, j))
                if b == 1 and j == 0:
                    pe.wait_ge(S(("yT_lo", "yT_hi")[c]), 1)
                lo = max(j * P, c * 512)
                for hh in range(NH):
                    ins = mm(ps[32 * hh:32 * hh + 32, 6 + c, lo - c * 512:512], va2[:, j, b, hh // 2, :],
                             pt[:, j % 2, hh, lo:(c + 1) * 512], start=(j == 0), stop=(j == 4 * c + 3),
                             tile_position=(0, 32 * hh))
                if c == 1:
                    ins.then_inc(S("pv"), 1)

            def y_transposes(b, half):
                pe.wait_ge(S(("yT_lo", "yT_hi")[half]), b + 1)
                for j in range(4 * half, 4 * half + 4):
                    ins = nc.tensor.transpose(ps[:, half, (j % 4) * P:(j % 4 + 1) * P], yT[:, b, j * P:(j + 1) * P], idt[:])
                ins.then_inc(S("yTT"), 1)

            for n in range(len(ROW_CHUNKS)):
                score_rows(0, n)
            for n in range(EARLY // 2):
                score_rows(1, n)
            pe.wait_ge(S("max_all"), 1)
            nc.tensor.transpose(ps[0:32, 6, 0:P], rw[:, 0, 0:32], idt[:]).then_inc(S("maxT"), 1)
            for n in range(EARLY // 2, EARLY):
                score_rows(1, n)
            todo = list(range(EARLY, len(ROW_CHUNKS)))
            pe.wait_ge(S("max_rows"), 48)
            pe.wait_ge(S("va2"), 1)
            for b in range(B):
                for n, (j, heads) in enumerate(COL_STEPS):
                    score_cols(b, n)
                    for _ in range(min(2, len(todo))):
                        score_rows(1, todo.pop(0))
                    if b == 0 and n == len(COL_STEPS) - 2:
                        pe.wait_ge(S("max_all"), 2)
                        nc.tensor.transpose(ps[0:32, 0, 0:P], rw[:, 1, 0:32], idt[:]).then_inc(S("maxT"), 1)
                    if j >= 1 and heads[-1] == 1:
                        weighted(b, j - 1, 0)
                    if j >= 1 and heads[-1] == 3:
                        weighted(b, j - 1, 1)
                    if b == 1 and j == 1 and heads[-1] == 3:
                        pe.wait_ge(S("max_pieces"), 2)
                        y_transposes(0, 0)
                        y_transposes(0, 1)
                    if b == 1 and j == 6 and heads[-1] == 3:
                        pe.wait_ge(S("yn"), 1)
                        y_transposes(1, 0)
                weighted(b, NT - 1, 1)
                if b == 0:
                    pe.wait_ge(S("max_rows"), 96)
            y_transposes(1, 1)
            transposes(sq, 4, S("yn"), S("T2b"), values=(2, 3))
            projection("xT2b", "wo2", 2, S("o2"))
            for half in range(2):
                pe.wait_ge(S("fhl"), 2 * half + 2)
                for b in range(B):
                    bank = (0, 4)[b] + half
                    for j in range(4 * half, 4 * half + 4):
                        ins = nc.tensor.transpose(ps[:, bank, (j % 4) * P:(j % 4 + 1) * P],
                                                  fhl[:, j, b].rearrange("p q c -> p (q c)"), idt[:])
                    ins.then_inc(S("Te"), 1)
            pe.wait_ge(S("e_split"), 2)
            for b in range(B):
                pe.wait_ge(S("xs%d" % b), 2)
                for j in range(NT):
                    o = ps[:, 6, (j * B + b) * 8:(j * B + b + 1) * 8]
                    mm(o, xs[:, b, j * P:(j + 1) * P], EP(e_hi, "rt", 0, 8), start=True, stop=False)
                    ins = mm(o, xs[:, b, j * P:(j + 1) * P], EP(e_lo, "rt", 0, 8), start=False, stop=True)
            ins.then_inc(S("logits"), 1)
            u_at = [0]
            z_at = [0]

            def up(t, pr, n3):
                b, hf = t // 2, t % 2
                n = u_at[0]
                u_at[0] += 1
                if n >= 3:
                    pe.wait_ge(S("gated"), n - 2)
                rhs = xs[:, b, hf * 512:(hf + 1) * 512]
                tile = 3 * pr + n3
                for m, name in enumerate(("w1", "w3")):
                    o = ps[:, 2 * (n % 3) + m]
                    mm(o, EP(e_hi, name, tile * P, (tile + 1) * P), rhs, start=True, stop=False)
                    ins = mm(o, EP(e_lo, name, tile * P, (tile + 1) * P), rhs, start=False, stop=True)
                ins.then_inc(S("up"), 1)

            def down(t, pr):
                n = t * NPAIR + pr
                b, hf = t // 2, t % 2
                if n == 0:
                    pe.wait_ge(S("wst"), 1)
                if n >= 1:
                    pe.wait_ge(S("zpair"), n)
                mm(ps[:, 7], selw(b, pr), wst[:, hf * 512:(hf + 1) * 512]).then_inc(S("wbp"), 1)
                pe.wait_ge(S("gated"), 3 * (n + 1))
                o = ps[:, 6]
                for k in range(2):
                    e = 2 * pr + k
                    mm(o[64 * k:64 * k + 64], E("w2m", e * 64, (e + 1) * 64), gh[:, n % GSLOTS, k, :], start=True, stop=False,
                       tile_position=(0, 64 * k), skip_group_check=True)
                mm(o, E("w2r", pr * P, (pr + 1) * P), gh[:, n % GSLOTS, 2, :], start=False, stop=True,
                   skip_group_check=True).then_inc(S("down"), 1)

            order = [(t, pr) for t in range(4) for pr in range(NPAIR)]
            for n, (t, pr) in enumerate(order):
                downs = list(DOWNS[n])
                for n3 in range(3):
                    up(t, pr, n3)
                if n == LAG - 1:
                    pe.wait_ge(S("wpc"), 3)
                    for j in range(NT):
                        ins = mm(ps[0:96, 6 + j // 4, (j % 4) * P:(j % 4 + 1) * P], wpc[:, j].rearrange("p q e -> p (q e)"), ident_b)
                    ins.then_inc(S("wT"), 1)
                for m in downs:
                    down(*order[m])
            pe.wait_ge(S("zsum"), 4 * NPAIR)
            pe.wait_ge(S("gated"), 48)
            for j in range(NT):
                for b in range(B):
                    ins = mm(ps[:, j // 4, (j % 4) * P + b * 64:(j % 4) * P + b * 64 + 64], zacc[b][:, j * P:(j + 1) * P], E("ii"))
                if j % 4 == 3:
                    ins.then_inc(S("moe"), 1)
            transposes(x1, 2, S("n3"), S("T3"))

            def uv(n):
                tile = n % NT
                at = (tile // 4) * L + (1 - tile // 2 % 2) * (L // 2) + tile % 2 * P
                bank = 4 + n % 4 if n < NT else tile
                mm(ps[:, bank, 0:384], xT[:, at:at + P], W(("v3", "u3")[n // NT])).then_inc(S("uv"), 1)

            for n in range(2 * NT):
                if 4 <= n < NT:
                    pe.wait_ge(S("uv_read"), n - 3)
                if n % 4 == 0 and n < NT:
                    pe.wait_ge(S(("xT3_lo", "xT3_hi")[n // 4]), 2)
                if n >= NT + 4:
                    pe.wait_ge(S("uv_read"), n - 7)
                uv(n)
            pe.wait_ge(ld_u, 32)
            for n in range(NB * NK):
                kt, i = n // NB, n % NB
                if n < 4:
                    pe.wait_ge(S("uv_read"), NT + 2 * n + 2)
                if n == 0:
                    pe.wait_ge(S("even"), 2)
                if n == 1:
                    pe.wait_ge(S("even"), 3)
                    pe.wait_ge(S("odd"), 1)
                if n >= 4:
                    pe.wait_ge(S("spec_read"), n - 3)
                for s in range(2):
                    for u in range(NU):
                        ins = mm(ps[:, 2 * (n % 4) + s, 0:384], tu_s[:, s, u, kt * P:(kt + 1) * P], veo[:, s, i, u, :],
                                 start=(u == 0), stop=(u == NU - 1))
                ins.then_inc(S("spec"), 1)
            pe.wait_ge(ld_k, 32)
            pe.wait_ge(S("spec_read"), NB * NK)

            def back_transposes(unit):
                for k in range(2):
                    n = 2 * unit + k
                    pe.wait_ge(S("y3"), n + 1)
                    if n >= 2:
                        pe.wait_ge(S("yT3"), n - 1)
                    for c in range(3):
                        ins = nc.tensor.transpose(ps[:, n % 2, c * P:(c + 1) * P],
                                                  y3[:, n % 2, c * P:(c + 1) * P], idt[:])
                    ins.then_inc(S("yTp"), 1)

            def output_projection(blk):
                pe.wait_ge(S("yT3"), 2 * NU * (blk + 1))
                for jj in range(4):
                    n = 2 * (2 * blk + jj - 2) if jj >= 2 else 2 * (2 * blk + 1 - jj) + 1
                    for c in range(3):
                        ins = mm(ps[:, 2 + blk, jj * P:(jj + 1) * P], yT3[:, n, c, :], W("o3", c * P, (c + 1) * P),
                                 start=(c == 0), stop=(c == 2))
                ins.then_inc(S("o3"), 1)

            for unit in range(NB * NU):
                blk, u = unit // NU, unit % NU
                pe.wait_ge(S("spectra"), NB * (NK - 1) + blk + 1)
                if unit >= 2:
                    pe.wait_ge(S("inv_read"), unit - 1)
                for s in range(2):
                    for kt in range(NK):
                        ins = mm(ps[:, 4 + 2 * (unit % 2) + s, 0:384], tk_s[:, s, kt, u * P:(u + 1) * P],
                                 osp[:, blk * NK + kt, s], start=(kt == 0), stop=(kt == NK - 1))
                ins.then_inc(S("inv"), 1)
                if unit >= 1:
                    back_transposes(unit - 1)
            output_projection(0)
            back_transposes(NB * NU - 1)
            output_projection(1)
            transposes(xc, 4, S("d3"), S("T3b"))
            projection("xT3b", "t3", 0, S("t3"))
            transposes(sq, 2, S("n4"), S("T4"))
            projection("xT4", "w4", 4, S("o4"))

        @block.scalar
        def _(act):
            chain = [0]

            def step(ins):
                chain[0] += 1
                ins.then_inc(act_chain, 1)
                act.wait_ge(act_chain, chain[0])

            def evac(bank, done_wait, value, out_sem, scale=None):
                act.wait_ge(done_wait, value)
                if scale is None:
                    nc.scalar.copy(xT[:, 0:512], ps[:, bank]).then_inc(out_sem, 1)
                else:
                    nc.scalar.activation(xT[:, 0:512], ps[:, bank], ACT.Copy, scale=scale).then_inc(out_sem, 1)

            def squares(i, src):
                for a in range(2):
                    act.wait_ge(S("centred"), 2 * i + a + 1)
                    nc.scalar.activation(sq[:, 4 * a:4 * a + 4], src[:, 4 * a:4 * a + 4], ACT.Square).then_inc(S("squared"), 1)

            loads = [0]

            def next_function(func):
                nc.scalar.activation(unused[:, loads[0]:loads[0] + 1], idt[0:1, 0:1], func)
                loads[0] += 1

            act.wait_ge(ld_id, 16)
            next_function(ACT.Sqrt)
            act.wait_ge(ld_rp, 16)
            nc.scalar.activation(rh[:, 0], RP("lag"), ACT.Identity, scale=RP("pw"), bias=RP("pb")).then_inc(S("r_h"), 1)
            for i in range(LAYERS):
                act.wait_ge(S("r_ss"), i + 1)
                if i >= 1:
                    act.wait_ge(S("r_act"), i)
                nc.scalar.activation(rh[:, 2], ps[:, 0, 0:2 * P], ACT.Sqrt, scale=1.0 / R).then_inc(S("r_rms"), 1)
                act.wait_ge(S("r_lin"), i + 1)
                nc.scalar.activation(rh[:, 0], ps[:, 1, 0:2 * P], ACT.Identity, bias=RP("b%d" % i)).then_inc(S("r_h"), 1)
            squares(0, xc)
            act.wait_ge(S("mean_squares"), NORMS["var1"])
            nc.scalar.activation(st[:, 3], st[:, 2], ACT.Sqrt).then_inc(S("roots"), 1)
            act.wait_ge(S("r_ss"), LAYERS + 1)
            nc.scalar.activation(rh[:, 2], ps[:, 0, 0:2 * P], ACT.Sqrt, scale=1.0 / R).then_inc(S("r_rms"), 1)
            next_function(ACT.Exp)
            evac(2, S("T1"), 1, S("xT1_lo"))
            act.wait_ge(S("qmin"), 1)
            nc.scalar.activation(qf1[:], tmp[:], ACT.Exp).then_inc(S("qexp"), 1)
            act.wait_ge(S("kmin"), 1)
            nc.scalar.activation(kf1[:], kf1[:], ACT.Exp).then_inc(S("kexp"), 1)
            next_function(ACT.Sqrt)
            act.wait_ge(S("kf1"), 1)
            nc.scalar.copy(va1[:, :, 0:P].rearrange("p j (b c) -> p j b c", b=B),
                           ps[:, 0:4].rearrange("p a (g b k c) -> p (a g) b k c", g=2, b=B, k=2)[:, :, :, 1, :]).then_inc(S("va1"), 1)
            evac(4, S("T1b"), 1, S("xT1b_lo"))
            for s in range(2):
                act.wait_ge(S("gf"), s + 1)
                nc.scalar.copy(gt[:, s], ps[:, 4 + s]).then_inc(S("gt_done"), 1)
            nc.scalar.copy(gt2[:, 1:P], ps[:, 4, 1:P]).then_inc(S("gt_done"), 1)
            act.wait_ge(S("gf"), 3)
            nc.scalar.copy(gt2[:, 0:1], ps[:, 6, 0:1]).then_inc(S("gt_done"), 1)

            def af_copy(n, bank):
                act.wait_ge(S("afp"), n + 1)
                dst = afx[:, 1] if n == 2 * NK else af[:, n // 2, n % 2]
                nc.scalar.copy(dst.rearrange("p d c -> p (d c)").rearrange("p (x c) -> p x c", x=2),
                               ps[:, bank:bank + 2, 0:288]).then_inc(S("af_done"), 1)

            for n in range(EARLY_AF):
                af_copy(n, (2, 6, 4)[n % 3])
                if n == 2:
                    squares(1, xc)
                    act.wait_ge(S("mean_squares"), NORMS["var2"])
                    nc.scalar.activation(st[:, 3], st[:, 2], ACT.Sqrt).then_inc(S("roots"), 1)
                if n == 4:
                    act.wait_ge(S("mean_squares"), NORMS["msq2"])
                    nc.scalar.activation(st[:, 6], st[:, 5], ACT.Sqrt).then_inc(S("roots"), 1)
            next_function(ACT.Exp)
            evac(2, S("T2"), 1, S("xT2_lo"), scale=W("ln1"))
            act.wait_ge(S("gf"), 3)
            act.wait_ge(S("qrot"), 2)
            nc.scalar.copy(pieces_q[:, 0], qr[:]).then_inc(S("rounded"), 1)
            act.wait_ge(S("qrot"), 3)
            nc.scalar.copy(pieces_k[0:64, 0], kr[:]).then_inc(S("rounded"), 1)
            act.wait_ge(S("rest"), 1)
            nc.scalar.copy(pieces_q[:, 1], tmp[:]).then_inc(S("rounded"), 1)
            act.wait_ge(S("rest"), 2)
            nc.scalar.copy(pieces_k[0:64, 1], qf1[0:64]).then_inc(S("rounded"), 1)
            act.wait_ge(S("v2"), 1)
            act.wait_ge(S("constants"), CONSTANTS["va2_ones"])
            nc.scalar.copy(va2[:, :, :, :, 0:HD],
                           ps[:, 4].rearrange("p (j b k d) -> p j b k d", j=NT, b=B, k=NKV)).then_inc(S("va2"), 1)
            for n in range(EARLY_AF, 2 * NK + 1):
                af_copy(n, 2 * (n - EARLY_AF))
            act.wait_ge(S("af_done"), 1)
            nc.scalar.copy(afx[:, 0], af[:, 0, 0]).then_inc(S("af_done"), 1)
            for b in range(B):
                for step_n, (j, heads) in enumerate(COL_STEPS):
                    n = b * len(COL_STEPS) + step_n
                    act.wait_ge(S("cols"), n + 1)
                    if b * NT + j >= 2 and heads[0] == 0:
                        act.wait_ge(S("pv"), b * NT + j - 1)
                    bank = 2 + 2 * (n % 2)
                    if len(heads) == 1:
                        dst = pt[:, j % 2, heads[0], j * P:N]
                        src = ps[:, bank:bank + 2].rearrange("p a t -> p (a t)")[:, j * P:N]
                    else:
                        dst = pt[:, j % 2, heads[0]:heads[1] + 1, j * P:N]
                        src = ps[:, bank:bank + 2, j * P - 512:512]
                    nc.scalar.activation(dst, src, ACT.Exp, scale=HD ** -0.5).then_inc(S("exp_done"), 1)
                    if (j, heads[-1]) == (5, NH - 1):
                        act.wait_ge(S("pv"), b * NT + 4)
                        nc.scalar.copy(yT[:, b, 0:512], ps[:, 6]).then_inc(S("yT_lo"), 1)
            next_function(ACT.Sqrt)
            evac(4, S("T2b"), 1, S("xT2b_lo"))
            squares(2, x1)
            act.wait_ge(S("mean_squares"), NORMS["var2b"])
            nc.scalar.activation(st[:, 3], st[:, 2], ACT.Sqrt).then_inc(S("roots"), 1)
            next_function(ACT.Exp)
            for b in range(B):
                act.wait_ge(S("Te"), b + 1)
                nc.scalar.copy(xs[:, b, 0:512], ps[:, (0, 4)[b]]).then_inc(S("xs%d" % b), 1)
            act.wait_ge(S("lmax"), 1)
            nc.scalar.activation(rw[:, 1], rw[:, 0], ACT.Exp).then_inc(S("lexp"), 1)
            next_function(ACT.Silu)
            for n in range(ALL_PAIRS):
                for n3 in range(3):
                    m = 3 * n + n3
                    act.wait_ge(S("up"), m + 1)
                    if m >= 2:
                        act.wait_ge(S("gated"), m - 1)
                    nc.scalar.activation(sil[:, m % 2], ps[:, 2 * (m % 3)], ACT.Silu).then_inc(S("silu"), 1)
                if n == LAG - 1:
                    act.wait_ge(S("wT"), 1)
                    act.wait_ge(S("constants"), CONSTANTS["wst_zero"])
                    nc.scalar.copy(wst[0:96], ps[0:96, 6:8].rearrange("p a t -> p (a t)")).then_inc(S("wst"), 1)
                for d in DOWNS[n]:
                    act.wait_ge(S("wbp"), d + 1)
                    if d >= 2:
                        act.wait_ge(S("zpair"), d - 1)
                    nc.scalar.copy(wb[:, d % 2], ps[:, 7]).then_inc(S("wb"), 1)
            next_function(ACT.Sqrt)
            squares(3, xc)
            act.wait_ge(S("mean_squares"), NORMS["var3"])
            nc.scalar.activation(st[:, 3], st[:, 2], ACT.Sqrt).then_inc(S("roots"), 1)
            next_function(ACT.Silu)
            act.wait_ge(S("T3"), 1)
            nc.scalar.copy(xT[:, 0:L // 2], ps[:, 2, 0:L // 2][:, ::-1]).then_inc(S("xT3_lo"), 1)
            nc.scalar.copy(xT[:, L // 2:L], ps[:, 2, L // 2:L]).then_inc(S("xT3_lo"), 1)

            def y_columns(n):
                act.wait_ge(S("yTp"), n + 1)
                src = ps[:, n % 2, 0:384].rearrange("p (c t) -> p c t", c=3)
                nc.scalar.copy(yT3[:, n], src[:, :, ::-1] if n % 2 else src).then_inc(S("yT3"), 1)

            for n in range(2 * NT):
                act.wait_ge(S("uv_read"), n + 1)
                dst = (vs if n < NT else us)[:, n % NT]
                nc.scalar.activation(dst, dst, ACT.Silu).then_inc(S("uv_silu"), 1)
            next_function(ACT.Sqrt)
            for unit in range(NB * NU):
                act.wait_ge(S("inv"), unit + 1)
                if unit >= 1:
                    act.wait_ge(S("inv_read"), unit)
                nc.scalar.copy(tmp[:, 0:384], ps[:, 4 + 2 * (unit % 2), 0:384]).then_inc(S("inv_even"), 1)
                for k in range(2):
                    if unit >= 1:
                        y_columns(2 * (unit - 1) + k)
            for n in range(2 * NB * NU - 2, 2 * NB * NU):
                y_columns(n)
            evac(4, S("T3b"), 1, S("xT3b_lo"))
            squares(4, xc)
            act.wait_ge(S("mean_squares"), NORMS["var3b"])
            nc.scalar.activation(st[:, 3], st[:, 2], ACT.Sqrt, scale=1.0 / D1).then_inc(S("roots"), 1)
            next_function(ACT.Silu)
            for a in range(2):
                act.wait_ge(S("e3"), a + 1)
                v = xc[:, 4 * a:4 * a + 4]
                nc.scalar.activation(v, v, ACT.Silu).then_inc(S("xr"), 1)
            next_function(ACT.Sqrt)
            squares(5, xc)
            act.wait_ge(S("mean_squares"), NORMS["var4"])
            nc.scalar.activation(st[:, 3], st[:, 2], ACT.Sqrt).then_inc(S("roots"), 1)
            evac(2, S("T4"), 1, S("xT4_lo"))

        @block.vector
        def _(dve):
            V = nc.vector
            chain = [0]

            def step(ins):
                chain[0] += 1
                ins.then_inc(dve_chain, 1)
                dve.wait_ge(dve_chain, chain[0])

            def evac(bank, done_wait, value, out_sem, scale=None):
                dve.wait_ge(done_wait, value)
                if scale is None:
                    V.tensor_copy(xT[:, 512:N], ps[:, bank]).then_inc(out_sem, 1)
                else:
                    V.tensor_scalar(xT[:, 512:N], ps[:, bank], scale, None, ALU.mult).then_inc(out_sem, 1)

            def per_token(v):
                return spread(v, 2, C)

            def flat3(t):
                return t[:].rearrange("p j b c -> p (j b) c")

            def flat2(t):
                return t[:].rearrange("p j b c -> p (j b c)")

            def half3(t, a):
                return t[:, 4 * a:4 * a + 4].rearrange("p j b c -> p (j b) c")

            def half2(t, a):
                return t[:, 4 * a:4 * a + 4].rearrange("p j b c -> p (j b c)")

            def halfj(t, a):
                return t[:, 4 * a:4 * a + 4].rearrange("p j b c -> p j (b c)")

            def hst(k, a):
                return st[:, k, 8 * a:8 * a + 8]

            def square_sums(i):
                for a in range(2):
                    dve.wait_ge(S("squared"), 2 * i + a + 1)
                    step(V.tensor_reduce(hst(1, a), half3(sq, a), AXX, ALU.add))

            def centre(i, var_sem, complete=None):
                for a in range(2):
                    if complete:
                        complete(a)
                    step(V.tensor_reduce(hst(0, a), half3(h, a), AXX, ALU.add))
                    V.scalar_tensor_tensor(out=half3(xc, a), in0=spread(hst(0, a), 2, C), scalar=-1.0 / C, in1=half3(h, a),
                                           op0=ALU.mult, op1=ALU.add).then_inc(S("centred"), 1)
                square_sums(i)
                V.tensor_scalar(st[:, 2], st[:, 1], 1.0 / C, 1e-5, ALU.mult, ALU.add).then_inc(var_sem, 1)

            def scale_rows(dst, src, k, done):
                for a in range(2):
                    V.tensor_tensor(half3(dst, a), half3(src, a), spread(hst(k, a), 2, C), ALU.mult).then_inc(done, 1)

            def add_bank(t, banks, ready):
                def complete(a):
                    dve.wait_ge(ready, a + 1)
                    step(V.tensor_tensor(half2(t, a), half2(t, a), ps[:, banks + a], ALU.add))
                return complete

            def weigh(n):
                dve.wait_ge(S("wb"), n + 1)
                dve.wait_ge(S("down"), n + 1)
                if n >= 2:
                    dve.wait_ge(S("zsum"), n - 1)
                V.tensor_tensor(zp_[:, n % 2], ps[:, 6], wb[:, n % 2], ALU.mult).then_inc(S("zpair"), 1)

            dve.wait_ge(ld_rp, 16)

            def square(i):
                dve.wait_ge(S("r_h"), i + 1)
                if i >= 1:
                    dve.wait_ge(S("r_ss"), i)
                V.tensor_tensor(rh[:, 1], rh[:, 0], rh[:, 0], ALU.mult).then_inc(S("r_sq"), 1)

            def normalise(i):
                dve.wait_ge(S("r_rms"), i + 1)
                step(V.tensor_scalar(rh[:, 2], rh[:, 2], 1e-8, None, ALU.add))
                step(V.reciprocal(rh[:, 2], rh[:, 2]))
                V.scalar_tensor_tensor(out=rh[:, 3], in0=rh[:, 0], scalar=0.0, in1=rh[:, 2], op0=ALU.max,
                                       op1=ALU.mult).then_inc(S("r_act"), 1)

            for i in range(LAYERS):
                square(i)
                if i < LAYERS - 1:
                    normalise(i)
            dve.wait_ge(gathered, 16 * NT * B)
            dve.wait_ge(ld_pe, 16)
            V.tensor_tensor(h[:, :, 0, :], xc[:, :, 0, :], pe_s[:], ALU.add).then_inc(S("embedded"), 1)
            V.tensor_tensor(h[:, :, 1, :], xc[:, :, 1, :], pe_s[:], ALU.add).then_inc(S("embedded"), 1)
            normalise(LAYERS - 1)
            dve.wait_ge(S("embedded"), 2)
            centre(0, S("mean_squares"))
            square(LAYERS)
            dve.wait_ge(S("roots"), NORMS["std1"])
            step(V.reciprocal(st[:, 4], st[:, 3]))
            scale_rows(sq, xc, 4, S("n1"))
            normalise(LAYERS)
            evac(3, S("T1"), 2, S("xT1_hi"))
            dve.wait_ge(S("xT1_lo"), 1)
            dve.wait_ge(S("xT1_hi"), 1)
            dve.wait_ge(S("q1"), 2)
            qps = ps[:, 4:6].rearrange("p a t -> p (a t)")
            V.tensor_scalar(tmp[:], qps, 0.0, None, ALU.min).then_inc(S("qmin"), 1)
            dve.wait_ge(S("r_T"), 1)
            dve.wait_ge(S("constants"), CONSTANTS["geo_ones"])
            step(V.tensor_copy(rh[:, 1], ps[:, 7, 0:2 * P]))
            for d in range(NW):
                plus, minus = (rh[:, 1, (2 * d + sd) * 32:(2 * d + sd + 1) * 32].rearrange("p (q r) -> p q r", r=R)
                               for sd in range(2))
                V.tensor_tensor(geo[:, 0, :, d * GR:d * GR + R], plus, minus, ALU.add).then_inc(S("geo_done"), 1)
                V.tensor_tensor(geo[:, 1, :, d * GR:d * GR + R], plus, minus, ALU.subtract).then_inc(S("geo_done"), 1)
            dve.wait_ge(S("kv1"), NT)
            kps = ps[:, 0:4].rearrange("p a (g k c) -> p (a g) k c", g=4, k=2)[:, :, 0, :]
            V.tensor_scalar(kf1.rearrange("p j b c -> p (j b) c"), kps, 0.0, None, ALU.min).then_inc(S("kmin"), 1)
            dve.wait_ge(S("kexp"), 1)
            V.scalar_tensor_tensor(out=kf1.rearrange("p j b c -> p (j b) c"), in0=kps, scalar=0.0, in1=kf1.rearrange("p j b c -> p (j b) c"), op0=ALU.max,
                                   op1=ALU.add).then_inc(S("kf1"), 1)
            dve.wait_ge(S("qexp"), 1)
            V.scalar_tensor_tensor(out=qf1[:], in0=qps, scalar=0.0, in1=qf1[:], op0=ALU.max, op1=ALU.add).then_inc(S("qf1"), 1)
            dve.wait_ge(S("ctx1"), 1)
            dve.wait_ge(ld_w, 16)
            V.tensor_tensor(cbd[:, 0:P], ps[:, 6, 0:P], W("mask_c"), ALU.mult).then_inc(S("cbd"), 1)
            V.tensor_scalar(cbd[:, P:144], W("mask_k"), ps[:, 6, P:P + 1], None, ALU.mult).then_inc(S("cbd"), 1)
            nd = ps[:, 0:4].rearrange("p a (g x) -> p (a g) x", g=2)
            den = rw[:, 0].rearrange("p (j g) -> p j g", g=16)
            for a in range(2):
                js = slice(4 * a, 4 * a + 4)
                dve.wait_ge(S("nd1"), a + 1)
                step(V.tensor_scalar(den[:, js], nd[:, js, P:144], 1e-6, None, ALU.max))
                step(V.reciprocal(den[:, js], den[:, js]))
                V.tensor_tensor(sq[:, js].rearrange("p j b (g d) -> p j (b g) d", d=8),
                                nd[:, js, 0:P].rearrange("p j (g d) -> p j g d", d=8),
                                spread(den[:, js], 3, 8), ALU.mult).then_inc(S("attn1"), 1)
            step(V.tensor_tensor(h[:].rearrange("p j b c -> p j (b c)"), h[:].rearrange("p j b c -> p j (b c)"),
                                 spread(W("bproj"), 1, NT), ALU.add))
            evac(5, S("T1b"), 2, S("xT1b_hi"))
            centre(1, S("mean_squares"), add_bank(h, 0, S("o1")))
            dve.wait_ge(S("roots"), NORMS["std2"])
            step(V.reciprocal(st[:, 4], st[:, 3]))
            step(V.tensor_tensor(st[:, 5], st[:, 4], st[:, 4], ALU.mult))
            step(V.tensor_tensor(st[:, 5], st[:, 5], st[:, 1], ALU.mult))
            V.tensor_scalar(st[:, 5], st[:, 5], 1.0 / C, 1e-6, ALU.mult, ALU.add).then_inc(S("mean_squares"), 1)
            step(V.tensor_tensor(flat3(x1), flat3(xc), per_token(st[:, 4]), ALU.mult))
            dve.wait_ge(S("roots"), NORMS["rms2"])
            step(V.reciprocal(st[:, 7], st[:, 6]))
            scale_rows(sq, x1, 7, S("n2"))
            evac(3, S("T2"), 2, S("xT2_hi"), scale=W("ln1"))
            dve.wait_ge(ld_rope, 16)
            dve.wait_ge(S("qk2"), 1)
            step(V.tensor_tensor(qr[:], ps[:, 4:6].rearrange("p a t -> p (a t)"), rope_s[:, 0], ALU.mult))
            dve.wait_ge(S("qk2"), 2)
            V.tensor_tensor(tmp[:], ps[:, 6:8].rearrange("p a t -> p (a t)"), rope_s[:, 1], ALU.mult).then_inc(S("qrot"), 1)
            dve.wait_ge(S("qrot"), 1)
            V.tensor_tensor(qr[:], qr[:], tmp[:], ALU.add).then_inc(S("qrot"), 1)
            dve.wait_ge(S("qrot"), 2)
            dve.wait_ge(S("qk2"), 4)
            step(V.tensor_tensor(kr[:], ps[0:64, 0:2].rearrange("p a t -> p (a t)"), rope_s[0:64, 0], ALU.mult))
            V.tensor_tensor(tmp[0:64], ps[0:64, 2:4].rearrange("p a t -> p (a t)"), rope_s[0:64, 1], ALU.mult).then_inc(S("krot"), 1)
            dve.wait_ge(S("krot"), 1)
            V.tensor_tensor(kr[:], kr[:], tmp[0:64], ALU.add).then_inc(S("qrot"), 1)
            dve.wait_ge(S("qrot"), 3)
            for n, (x, pcs, t) in enumerate(((qr[:], pieces_q, tmp[:]), (kr[:], pieces_k[0:64], qf1[0:64]))):
                dve.wait_ge(S("rounded"), n + 1)
                V.tensor_tensor(t, x, pcs[:, 0], ALU.subtract).then_inc(S("rest"), 1)
            for n, (pcs, t) in enumerate(((pieces_q, tmp[:]), (pieces_k[0:64], qf1[0:64]))):
                dve.wait_ge(S("rounded"), n + 3)
                V.tensor_tensor(pcs[:, 2], t, pcs[:, 1], ALU.subtract).then_inc(S("k_pieces"), 1)
            dve.wait_ge(S("k_pieces"), 2)
            dve.wait_ge(ld_e, 32)
            dve.wait_ge(S("af_done"), 2 * NK + 2)
            V.tensor_copy(e_hi[:], e_raw).then_inc(S("e_split"), 1)
            dve.wait_ge(S("e_split"), 1)
            V.tensor_tensor(e_lo[:], e_raw, e_hi[:].bitcast(F32), ALU.subtract).then_inc(S("e_split"), 1)
            def maxima(b):
                mx = rw[:, b, 0:32]
                m2 = rw[:, 2 + b, 0:32]
                for n, (hh, i, c) in enumerate(ROW_CHUNKS):
                    n += b * len(ROW_CHUNKS)
                    dve.wait_ge(S("rows"), n + 1)
                    wd = min(512, (i + 1) * P - c * 512)
                    dst = (mx if c == 0 else m2)[:, hh * NT + i:hh * NT + i + 1]
                    V.tensor_reduce(dst, ps[:, row_bank(n), 0:wd], AXX, ALU.max).then_inc(S("max_read"), 1)
                at = (b + 1) * len(ROW_CHUNKS)
                dve.wait_ge(S("max_read"), at)
                a3 = mx.rearrange("p (h i) -> p h i", i=NT)[:, :, 4:NT]
                b3 = m2.rearrange("p (h i) -> p h i", i=NT)[:, :, 4:NT]
                step(V.tensor_tensor(a3, a3, b3, ALU.max))
                V.tensor_scalar(mx, mx, -1.0, None, ALU.mult).then_inc(S("max_all"), 1)
                dve.wait_ge(S("maxT"), b + 1)
                if b == 1:
                    dve.wait_ge(S("max_rows"), 48)
                bank = 6 if b == 0 else 0
                step(V.tensor_copy(mrow[:, 0], ps[0:32, bank, 0:P]))
                step(V.tensor_tensor(mtmp[:], ps[0:32, bank, 0:P], mrow[:, 0], ALU.subtract))
                step(V.tensor_copy(mrow[:, 1], mtmp[:]))
                V.tensor_tensor(mrow[:, 2], mtmp[:], mrow[:, 1], ALU.subtract).then_inc(S("max_pieces"), 1)

            maxima(0)
            maxima(1)
            def divide(b, js):
                y = ps[:, 0:2].rearrange("p a (j h d) -> p (a j) h d", j=4, h=NH)[:, js]
                dn = rw[:, 4 + b, 0:32].rearrange("p (j h) -> p j h", h=NH)[:, js]
                step(V.tensor_copy(dn, y[:, :, :, HD]))
                step(V.reciprocal(dn, dn))
                V.tensor_tensor(sq[:, js, b, :].rearrange("p j (h d) -> p j h d", d=HD), y[:, :, :, 0:HD],
                                spread(dn, 3, HD), ALU.mult).then_inc(S("yn"), 1)

            dve.wait_ge(S("pv"), NT)
            V.tensor_copy(yT[:, 0, 512:N], ps[:, 7]).then_inc(S("yT_hi"), 1)
            dve.wait_ge(S("yTT"), 2)
            divide(0, slice(0, NT))
            dve.wait_ge(S("yTT"), 3)
            divide(1, slice(0, 4))
            dve.wait_ge(S("pv"), 2 * NT)
            V.tensor_copy(yT[:, 1, 512:N], ps[:, 7]).then_inc(S("yT_hi"), 1)
            dve.wait_ge(S("yTT"), 4)
            divide(1, slice(4, NT))
            evac(5, S("T2b"), 2, S("xT2b_hi"))
            for a in range(2):
                dve.wait_ge(S("o2"), a + 1)
                V.tensor_tensor(half2(x1, a), half2(x1, a), ps[:, 2 + a], ALU.add).then_inc(S("centred"), 1)
            square_sums(2)
            V.tensor_scalar(st[:, 2], st[:, 1], 1.0 / C, 1e-6, ALU.mult, ALU.add).then_inc(S("mean_squares"), 1)
            dve.wait_ge(S("roots"), NORMS["rms2b"])
            step(V.reciprocal(st[:, 4], st[:, 3]))
            for a in range(2):
                step(V.tensor_tensor(half3(xc, a), half3(x1, a), spread(hst(4, a), 2, C), ALU.mult))
                step(V.tensor_tensor(halfj(xc, a), halfj(xc, a), spread(W("ln2"), 1, 4), ALU.mult))
                hi, lo = (fhl[:, 4 * a:4 * a + 4, :, q, :].rearrange("p j b c -> p (j b) c") for q in range(2))
                V.tensor_copy(hi.bitcast(F32R), half3(xc, a)).then_inc(S("fhl"), 1)
                dve.wait_ge(S("fhl"), 2 * a + 1)
                V.tensor_tensor(lo, half3(xc, a), hi, ALU.subtract).then_inc(S("fhl"), 1)
            for b in range(B):
                dve.wait_ge(S("Te"), 3 + b)
                V.tensor_copy(xs[:, b, 512:N], ps[:, (1, 5)[b]]).then_inc(S("xs%d" % b), 1)
            step(V.tensor_tensor(flat2(h), flat2(h), flat2(x1), ALU.add))
            g3 = lambda k: rw[:, k].rearrange("p (g e) -> p g e", e=NE)
            each = lambda v: spread(v, 2, NE)
            dve.wait_ge(S("logits"), 1)
            lg = ps[:, 6, 0:P].rearrange("p (g e) -> p g e", e=NE)
            eidx = W("eidx").rearrange("p (g e) -> p g e", e=NE)
            step(V.tensor_reduce(st[:, 5], lg, AXX, ALU.max))
            V.tensor_tensor(g3(0), lg, each(st[:, 5]), ALU.subtract).then_inc(S("lmax"), 1)
            gates = [0]

            def gate():
                m = gates[0]
                gates[0] += 1
                n, n3 = m // 3, m % 3
                dve.wait_ge(S("silu"), m + 1)
                if n >= GSLOTS and n3 == 0:
                    dve.wait_ge(S("down"), n - GSLOTS + 1)
                V.tensor_tensor(gh[:, n % GSLOTS, n3], ps[:, 2 * (m % 3) + 1], sil[:, m % 2], ALU.mult).then_inc(S("gated"), 1)

            eidx, enum = (W(k).rearrange("p (g e) -> p g e", e=NE) for k in ("eidx", "enum"))
            dve.wait_ge(S("lexp"), 1)
            step(V.tensor_reduce(st[:, 6], g3(1), AXX, ALU.add))
            step(V.reciprocal(st[:, 6], st[:, 6]))
            step(V.tensor_tensor(g3(2), g3(1), each(st[:, 6]), ALU.mult))
            for k in range(2):
                probs = g3(2 + k)
                step(V.tensor_reduce(st[:, 7 + k], probs, AXX, ALU.max))
                step(V.tensor_tensor(g3(4), probs, each(st[:, 7 + k]), ALU.is_equal))
                gate()
                step(V.scalar_tensor_tensor(out=g3(4), in0=g3(4), scalar=-TOPK_OFF, in1=eidx, op0=ALU.mult, op1=ALU.add))
                step(V.tensor_reduce(st[:, 9], g3(4), AXX, ALU.min))
                gate()
                step(V.tensor_tensor(g3(5 + k), enum, each(st[:, 9]), ALU.is_equal))
                if k == 0:
                    step(V.scalar_tensor_tensor(out=g3(3), in0=g3(5), scalar=-2.0, in1=g3(2), op0=ALU.mult, op1=ALU.add))
                    gate()
            step(V.tensor_tensor(st[:, 7], st[:, 7], st[:, 8], ALU.add))
            step(V.tensor_scalar(st[:, 7], st[:, 7], 1e-9, None, ALU.add))
            gate()
            step(V.reciprocal(st[:, 7], st[:, 7]))
            step(V.tensor_tensor(g3(5), g3(5), g3(6), ALU.add))
            gate()
            step(V.tensor_tensor(g3(5), g3(5), g3(2), ALU.mult))
            step(V.tensor_tensor(g3(7), g3(5), each(st[:, 7]), ALU.mult))
            gate()
            dve.wait_ge(S("constants"), CONSTANTS["wpc_zero"])
            pieces_w = [wpc[:, :, q, 0:B * NE] for q in range(3)]
            w16, r16 = (rw[:, k].rearrange("p (j e) -> p j e", e=B * NE) for k in (7, 0))
            V.tensor_copy(pieces_w[0], w16).then_inc(S("wpc"), 1)
            dve.wait_ge(S("wpc"), 1)
            step(V.tensor_tensor(r16, w16, pieces_w[0], ALU.subtract))
            gate()
            V.tensor_copy(pieces_w[1], r16).then_inc(S("wpc"), 1)
            dve.wait_ge(S("wpc"), 2)
            V.tensor_tensor(pieces_w[2], r16, pieces_w[1], ALU.subtract).then_inc(S("wpc"), 1)
            for n in range(ALL_PAIRS):
                while gates[0] < 3 * (n + 1):
                    gate()
                for d in DOWNS[n]:
                    weigh(d)
            centre(3, S("mean_squares"), add_bank(h, 0, S("moe")))
            dve.wait_ge(S("roots"), NORMS["std3"])
            step(V.reciprocal(st[:, 4], st[:, 3]))
            scale_rows(x1, xc, 4, S("n3"))
            dve.wait_ge(S("T3"), 2)
            V.tensor_copy(xT[:, L:L + L // 2], ps[:, 3, 0:L // 2][:, ::-1]).then_inc(S("xT3_hi"), 1)
            V.tensor_copy(xT[:, L + L // 2:N], ps[:, 3, L // 2:L]).then_inc(S("xT3_hi"), 1)

            def uv_bias(n):
                dve.wait_ge(S("uv"), n + 1)
                bank = 4 + n % 4 if n < NT else n % NT
                dst = (vs if n < NT else us)[:, n % NT]
                V.tensor_tensor(dst, ps[:, bank, 0:384], W("vb" if n < NT else "ub"), ALU.add).then_inc(S("uv_read"), 1)

            for n in range(NT + 4):
                uv_bias(n)
            dve.wait_ge(S("uv_silu"), NT)
            V.tensor_tensor(veo[:, 0, 0], vs[:, 0:2], vs[:, 2:4], ALU.add).then_inc(S("even"), 1)
            V.tensor_tensor(veo[:, 1, 0], vs[:, 0:2], vs[:, 2:4], ALU.subtract).then_inc(S("even"), 1)
            V.tensor_tensor(veo[:, 0, 1], vs[:, 4:6], vs[:, 6:8], ALU.add).then_inc(S("even"), 1)
            for n in range(NT + 4, 2 * NT):
                uv_bias(n)

            def spectra(kt, o):
                q = NB * (NB * kt + 1) + o
                dve.wait_ge(S("part"), 2 * (q + 1))
                V.tensor_tensor(osp[:, o * NK + kt], osp[:, o * NK + kt], ssum[:, (kt % 2) * NB + o],
                                ALU.add).then_inc(S("spectra"), 1)

            dve.wait_ge(S("af_done"), 2 * NK + 2)
            for n in range(NB * NK):
                kt, i = n // NB, n % NB
                dve.wait_ge(S("spec"), n + 1)
                pcs = ps[:, 2 * (n % 4):2 * (n % 4) + 2, 0:384].rearrange("p s (b c) -> p s b c", b=B)
                for o in range(NB):
                    q, d = NB * n + o, WINDOW[i, o]
                    if q >= 2:
                        dve.wait_ge(S("part"), 2 * (q - 1))
                    own, cross = (prd[:, 2 * (q % 2) + x].rearrange("p s (b c) -> p s b c", b=B) for x in range(2))
                    sc = (afx[:] if kt == 0 else af[:, kt])[:, :, d]
                    step(V.tensor_tensor(own, pcs, spread(af[:, kt, ::-1, d], 2, B), ALU.mult))
                    ins = V.tensor_tensor(cross, pcs, spread(sc, 2, B), ALU.mult)
                    ins.then_inc(S("prd"), 1)
                dve.wait_ge(S("prd"), NB * (n + 1))
                V.tensor_copy(st[:, 9, 0:1], st[:, 4, 0:1]).then_inc(S("spec_read"), 1)
                if i == 0 and kt >= 1:
                    for o in range(NB):
                        spectra(kt - 1, o)
            for o in range(NB):
                spectra(NK - 1, o)
            step(V.tensor_tensor(flat2(h), flat2(h), flat2(x1), ALU.add))
            step(V.tensor_tensor(xc[:].rearrange("p j b c -> p j (b c)"), x1[:].rearrange("p j b c -> p j (b c)"),
                                 spread(W("ob"), 1, NT), ALU.subtract))
            dve.wait_ge(S("uv_silu"), 2 * NT)
            for unit in range(NB * NU):
                dve.wait_ge(S("inv_even"), unit + 1)
                odd = ps[:, 5 + 2 * (unit % 2), 0:384]
                if unit >= 1:
                    dve.wait_ge(S("yTp"), 2 * unit)
                step(V.tensor_tensor(y3[:, 0], tmp[:, 0:384], odd, ALU.add))
                V.tensor_tensor(y3[:, 1], tmp[:, 0:384], odd, ALU.subtract).then_inc(S("inv_read"), 1)
                dve.wait_ge(S("inv_read"), unit + 1)
                at = 4 * (unit // NU) + unit % NU
                V.tensor_tensor(y3[:, 0], y3[:, 0], us[:, at], ALU.mult).then_inc(S("y3"), 1)
                V.tensor_tensor(y3[:, 1], y3[:, 1], us[:, at + NU], ALU.mult).then_inc(S("y3"), 1)
            for a in range(2):
                dve.wait_ge(S("o3"), a + 1)
                V.tensor_tensor(half2(xc, a), half2(xc, a), ps[:, 2 + a], ALU.subtract).then_inc(S("d3"), 1)
            evac(5, S("T3b"), 2, S("xT3b_hi"))
            for a in range(2):
                dve.wait_ge(S("t3"), a + 1)
                V.tensor_tensor(halfj(xc, a), ps[:, a].rearrange("p (j x) -> p j x", j=4), spread(W("tb"), 1, 4),
                                ALU.add).then_inc(S("centred"), 1)
            square_sums(4)
            V.tensor_copy(st[:, 2], st[:, 1]).then_inc(S("mean_squares"), 1)
            dve.wait_ge(S("roots"), NORMS["rms3b"])
            step(V.tensor_scalar(st[:, 3], st[:, 3], 1e-8, None, ALU.add))
            step(V.reciprocal(st[:, 4], st[:, 3]))
            scale_rows(xc, xc, 4, S("e3"))

            def add_branch(a):
                dve.wait_ge(S("xr"), a + 1)
                step(V.tensor_tensor(half2(h, a), half2(h, a), half2(xc, a), ALU.add))

            centre(5, S("mean_squares"), add_branch)
            dve.wait_ge(S("roots"), NORMS["std4"])
            step(V.reciprocal(st[:, 4], st[:, 3]))
            scale_rows(sq, xc, 4, S("n4"))
            evac(3, S("T4"), 2, S("xT4_hi"))
            hj = h[:].rearrange("p j b c -> p j (b c)")
            step(V.tensor_tensor(hj, hj, spread(W("b4"), 1, NT), ALU.add))
            for a in range(2):
                dve.wait_ge(S("o4"), a + 1)
                V.tensor_tensor(half2(sq, a), half2(h, a), ps[:, 4 + a], ALU.add).then_inc(S("final"), 1)



def positions():
    pos = np.arange(N, dtype=np.float32)[:, None]
    d = np.arange(C)
    inv = np.power(np.float32(10000.0), -((d - d % 2).astype(np.float32) / np.float32(C))).astype(np.float32)
    ang = (pos * inv).astype(np.float32).astype(np.float64)
    pe = np.where(d % 2 == 0, np.sin(ang), np.cos(ang)).astype(np.float32)
    return np.ascontiguousarray(pe.reshape(NT, P, C).transpose(1, 0, 2))


def rope_tables():
    inv = (1.0 / 10000.0 ** (np.arange(0, HD, 2, dtype=np.float32) / HD)).astype(np.float32)
    f = np.outer(np.arange(N, dtype=np.float32), inv).astype(np.float32)
    emb = np.concatenate([f, f], -1)
    sign = np.where(np.arange(HD) < HD // 2, -1.0, 1.0).astype(np.float32)
    t = np.stack([np.tile(np.cos(emb).T, (P // HD, 1)), np.tile((np.sin(emb) * sign).T, (P // HD, 1))], 1)
    return np.ascontiguousarray(t.astype(np.float32))


def fourier_tables():
    m, k = np.arange(L)[:, None], np.arange(L)[None, :]
    u = np.arange(L // 2)[:, None] + 0.5
    ph = 2 * np.pi * ((m * k) % (2 * L)) / (2 * L)
    tm = np.stack([np.cos(ph), np.sin(ph)])
    tm[:, 0] *= 0.5
    pu = 2 * np.pi * np.mod(u * k, 2 * L) / (2 * L)
    tu = np.stack([np.cos(pu), np.sin(pu)])
    tu[1, :, 0] = np.sin(np.pi * u[:, 0])
    wk = np.where(k == 0, 1.0, 2.0) / (2 * L)
    tk = (tu * wk).transpose(0, 2, 1)
    alt = np.repeat(np.where(np.arange(L) % 2 == 0, 1.0, -1.0)[:, None], 2, 1)
    alt[0] *= 0.5
    lay = lambda t, n: np.ascontiguousarray(t.reshape(2, n, P, -1).transpose(0, 2, 1, 3).astype(np.float32))
    return (lay(tm, NM), lay(tu, NU), lay(tk, NK),
            alt.reshape(NM, P, 2).transpose(1, 0, 2).reshape(P, -1).astype(np.float32))


def kernel(**inputs):
    import concourse.bacc as _bacc
    from concourse.bass_utils import run_bass_kernel_spmd as _run
    import ml_dtypes

    a = {k: np.asarray(v) for k, v in inputs.items()}
    f32 = np.float32

    def twice(m):
        k, n = m.shape
        o = np.zeros((2 * k, 2 * n), f32)
        o[:k, :n] = m
        o[k:, n:] = m
        return o

    rot = np.concatenate([np.arange(HD // 2, HD), np.arange(HD // 2)])
    turned = lambda m: m.reshape(-1, HD, C)[:, rot].reshape(-1, C)
    wp = np.zeros((P, WTOT), f32)

    def put(name, m):
        lo, hi = WCOLS[name]
        wp[:m.shape[0], lo:hi] = m.reshape(m.shape[0], -1)

    rows = lambda v, n=1: np.broadcast_to(np.tile(v, n)[None], (P, v.size * n))
    put("q1", twice(a["L0_attn_Wq"].T))
    put("kv1", twice(a["L0_attn_Wkv"].T))
    put("proj1", twice(a["L0_attn_Wproj"].T))
    put("q2", twice(a["L0_ffn_wq"].T))
    put("q2r", twice(turned(a["L0_ffn_wq"]).T))
    put("k2", twice(a["L0_ffn_wk"].T))
    put("k2r", twice(turned(a["L0_ffn_wk"]).T))
    put("v2", twice(a["L0_ffn_wv"].T))
    put("wo2", twice(a["L0_ffn_wo"].T))
    put("v3", twice(a["L1_attn_v_w"].T))
    put("u3", twice(a["L1_attn_u_w"].T))
    o3 = twice(a["L1_attn_o_w"].T).reshape(3, P, P).transpose(1, 0, 2)
    put("o3", o3.reshape(P, -1))
    put("t3", twice(a["L1_attn_t_w"].T))
    put("w4", twice(a["L1_ffn_weight"].T))
    put("bproj", rows(a["L0_attn_bproj"], 2))
    put("ub", rows(a["L1_attn_u_b"], 2))
    put("vb", rows(a["L1_attn_v_b"], 2))
    put("ob", rows(a["L1_attn_o_b"], 2))
    put("tb", rows(a["L1_attn_t_b"], 2))
    put("b4", rows(a["L1_ffn_bias"], 2))
    put("ln2", rows(a["L0_ffn_ln2_w"], 2))
    put("ln1", np.tile(a["L0_ffn_ln1_w"], 2)[:, None])
    hd = np.arange(P) // 8
    put("mask_c", (hd[:, None] == hd[None, :]).astype(f32))
    put("mask_k", (hd[:, None] == np.arange(16)[None, :]).astype(f32))
    put("eidx", np.broadcast_to(np.tile(np.arange(NE) + NE, 16).astype(f32)[None], (P, P)))
    put("enum", np.broadcast_to(np.tile(np.arange(NE), 16).astype(f32)[None], (P, P)))

    tm, tu, tk, alt = fourier_tables()
    rp = np.zeros((P, RTOT), f32)

    def rput(name, m):
        lo, hi = RCOLS[name]
        rp[:, lo:hi] = m

    groups = P // R
    side = np.arange(L, dtype=f32).reshape(NM, P)
    lag = np.zeros((2 * groups, P), f32)
    lag[:NW * 2 * NM] = np.concatenate([mid + sign * side for mid in (0, L, -L) for sign in (1, -1)])
    rput("lag", np.repeat(lag, R, 0).reshape(2, P, P).transpose(1, 0, 2).reshape(P, 2 * P))
    g = np.arange(P) // R
    rput("ones", (g[:, None] == g[None, :]).astype(f32))
    for i in range(LAYERS):
        bd = np.zeros((P, P), f32)
        for q in range(groups):
            bd[q * R:(q + 1) * R, q * R:(q + 1) * R] = a["L1_attn_rpe_lw"][i].T
        rput("l%d" % i, bd)
        rput("b%d" % i, np.tile(a["L1_attn_rpe_lb"][i], groups)[:, None])
    rput("pw", np.tile(a["L1_attn_pos_w"][:, 0], groups)[:, None])
    rput("pb", np.tile(a["L1_attn_pos_b"], groups)[:, None])
    ow = np.zeros((NM, 32, NW, D1), f32)
    for d in range(NW):
        ow[:, d * GR:d * GR + R, d] = a["L1_attn_out_w"].T
        ow[:, d * GR + R, d] = a["L1_attn_out_b"]
    rput("outw", ow.reshape(P, NW * D1))
    rput("alt", alt)

    ep = np.zeros((P, ETOT), f32)
    for name, key in (("w1", "L0_ffn_w1"), ("w3", "L0_ffn_w3")):
        src = a[key]
        t = np.zeros((12, P, C), f32)
        for pr in range(NPAIR):
            for k in range(2):
                t[3 * pr + k] = src[2 * pr + k, :P]
                t[3 * pr + 2, 64 * k:64 * k + REM] = src[2 * pr + k, P:]
        t = t.transpose(2, 0, 1).reshape(C, -1)
        ep[:, ECOLS[name][0]:ECOLS[name][1]] = np.concatenate([t, t])
    r = a["L0_ffn_router_w"].T
    ep[:, ECOLS["rt"][0]:ECOLS["rt"][1]] = np.concatenate([r, r])
    w2 = a["L0_ffn_w2"]
    ep[:, ECOLS["w2m"][0]:ECOLS["w2m"][1]] = w2[:, :, :P].transpose(2, 0, 1).reshape(P, -1)
    t = np.zeros((P, NPAIR, 2, C), f32)
    for pr in range(NPAIR):
        for k in range(2):
            t[64 * k:64 * k + REM, pr, k] = w2[2 * pr + k, :, P:].T
    ep[:, ECOLS["w2r"][0]:ECOLS["w2r"][1]] = t.reshape(P, -1)
    ep[:, ECOLS["ii"][0]:ECOLS["ii"][1]] = np.concatenate([np.eye(C, dtype=f32)] * 2)

    pq = np.arange(P)
    bfc = np.zeros((P, 3 * P + B * NPAIR * P), f32)
    bfc[:, 0:P] = np.where(pq[None, :] <= pq[:, None], 0.0, NEG)
    bfc[:, P:2 * P] = np.where(pq[None, :] >= pq[:, None], 0.0, NEG)
    bfc[:, 2 * P:3 * P] = np.eye(P)
    for b in range(B):
        for pr in range(NPAIR):
            for k in range(2):
                for pc in range(3):
                    c0 = 3 * P + (b * NPAIR + pr) * P + 64 * k
                    bfc[32 * pc + b * NE + 2 * pr + k, c0:c0 + 64] = 1.0
    bfc = bfc.astype(ml_dtypes.bfloat16)

    idx = np.ascontiguousarray(a["x"].reshape(B, NT, P).transpose(2, 1, 0).reshape(P, NT * B))
    arrays = {"idx": idx, "emb": np.ascontiguousarray(a["L0_tok_W"]), "pe": positions(), "wpack": wp, "rpack": rp,
              "epack": ep, "ident": np.eye(P, dtype=f32), "bfc": bfc, "rope": rope_tables(), "tm": tm, "tu": tu, "tk": tk}

    nc = _bacc.Bacc("TRN2", target_bir_lowering=False, num_devices=1)
    args = {n: nc.dram_tensor(n, v.shape, mybir.dt.from_np(v.dtype), kind="ExternalInput").ap() for n, v in arrays.items()}
    args["scr_q"] = nc.dram_tensor("scr_q", (3, P, N), BF16, kind="Internal").ap()
    args["scr_k"] = nc.dram_tensor("scr_k", (3, 64, N), BF16, kind="Internal").ap()
    args["out"] = nc.dram_tensor("out", (P, NT * B * C), F32, kind="ExternalOutput").ap()
    build(nc, **args)
    r = _run(nc, [arrays], core_ids=[0])
    o = r.results[0]["out"]
    return np.ascontiguousarray(np.asarray(o).reshape(P, NT, B, C).transpose(2, 1, 0, 3).reshape(B, N, C))
```
